# Optimizing a Trainium2 kernel written in Bass

```python
import numpy as np
import jax
import jax.numpy as jnp

def _softmax(x, axis=-1):
    return jax.nn.softmax(x, axis=axis)

def _gelu(x):
    return jax.nn.gelu(x, approximate=True)

def _silu(x):
    return jax.nn.silu(x)

def _sigmoid(x):
    return jax.nn.sigmoid(x)

def _layernorm(x, axis=-1, eps=1e-05):
    m = jnp.mean(x, axis=axis, keepdims=True)
    v = jnp.var(x, axis=axis, keepdims=True)
    return (x - m) / jnp.sqrt(v + eps)

def _scatter_add(tgt, idx, src, axis=0):
    return tgt.at[idx].add(src)

def _segment_sum(src, seg, n):
    return jax.ops.segment_sum(src, seg, n)
kernel_name = 'mk_cond_seq_d4_seqx_r4_368ac2'

def setup_inputs(seed: int=0):
    np.random.seed(seed)
    _w = jnp.asarray

    def _rec_inputs():
        import jax
        import jax.numpy as jnp
        _rk = jax.random.key(seed)
        x = -0.0002928 + 1 * jax.random.normal(jax.random.fold_in(_rk, 1), (64, 64, 256), jnp.float32)
        _lenS = 64 - jax.random.randint(jax.random.fold_in(_rk, 7), (64,), 0, max(1, 64 // 4) + 1, jnp.int32)
        _lenS2 = 64 - jax.random.randint(jax.random.fold_in(_rk, 8), (64,), 0, max(1, 64 // 4) + 1, jnp.int32)
        cond_1024 = 0.0061147 + 1.02565 * jax.random.normal(jax.random.fold_in(_rk, 11), (64, 256), jnp.float32)
        return (x, cond_1024)
    x, cond_1024 = _rec_inputs()

    def _L0_cond_setup():
        import jax, jax.numpy as jnp
        import numpy as np
        EPS = 1e-05

        def _sln(h, w, ln_g, ln_b, Wg, bg, Wb, bb):
            mu = jnp.mean(h, axis=-1, keepdims=True)
            var = jnp.mean((h - mu) ** 2, axis=-1, keepdims=True)
            ln = (h - mu) / jnp.sqrt(var + EPS) * ln_g + ln_b
            gamma = (w @ Wg.T + bg)[:, None, :]
            beta = (w @ Wb.T + bb)[:, None, :]
            return gamma * ln + beta
        key = jax.random.key(seed)
        ks = jax.random.split(key, 20)
        B, N, D = (4, 256, 256)
        F = 4 * D
        s = lambda fan: 1.0 / np.sqrt(fan)
        inp = {'hidden': jax.random.normal(ks[0], (B, N, D), jnp.float32), 'w': jax.random.normal(ks[1], (B, D), jnp.float32), 'ln_g': jnp.ones((D,), jnp.float32), 'ln_b': jnp.zeros((D,), jnp.float32), 'Wg': jax.random.normal(ks[2], (D, D), jnp.float32) * s(D), 'bg': jnp.zeros((D,), jnp.float32), 'Wb': jax.random.normal(ks[3], (D, D), jnp.float32) * s(D), 'bb': jnp.zeros((D,), jnp.float32), 'Wqkv': jax.random.normal(ks[4], (3 * D, D), jnp.float32) * s(D), 'bqkv': jnp.zeros((3 * D,), jnp.float32), 'Wp': jax.random.normal(ks[5], (D, D), jnp.float32) * s(D), 'bp': jnp.zeros((D,), jnp.float32), 'W1': jax.random.normal(ks[6], (F, D), jnp.float32) * s(D), 'b1': jnp.zeros((F,), jnp.float32), 'W2': jax.random.normal(ks[7], (D, F), jnp.float32) * s(F), 'b2': jnp.zeros((D,), jnp.float32), 'num_heads': 16}
        return inp
    _L0_cond_all = _L0_cond_setup()
    _L0_cond_in = {k: v for k, v in _L0_cond_all.items() if k in ('ln_g', 'ln_b', 'Wg', 'bg', 'Wb', 'bb', 'Wqkv', 'bqkv', 'Wp', 'bp', 'W1', 'b1', 'W2', 'b2')}
    del _L0_cond_all

    def _L1_cond_setup():
        import jax, jax.numpy as jnp
        import numpy as np
        B, N, D = (2, 512, 256)
        H, HD = (16, 64)
        E, DD = (8, 1024)
        EPS = 1e-05

        def _ln(x, g, b):
            m = jnp.mean(x, axis=-1, keepdims=True)
            v = jnp.var(x, axis=-1, keepdims=True)
            return (x - m) * jax.lax.rsqrt(v + EPS) * g + b
        key = jax.random.key(seed)
        ks = jax.random.split(key, 16)
        s = 0.02
        return {'x': jax.random.normal(ks[0], (B, N, D), jnp.float32), 't': jax.random.normal(ks[1], (B, 1, D), jnp.float32), 'W_ada': jax.random.normal(ks[2], (D, D), jnp.float32) * s, 'b_ada': jnp.zeros((D,), jnp.float32), 'ln1_g': jnp.ones((D,), jnp.float32), 'ln1_b': jnp.zeros((D,), jnp.float32), 'Wqkv': jax.random.normal(ks[3], (3 * H * HD, D), jnp.float32) * s, 'qn_g': jnp.ones((HD,), jnp.float32), 'qn_b': jnp.zeros((HD,), jnp.float32), 'kn_g': jnp.ones((HD,), jnp.float32), 'kn_b': jnp.zeros((HD,), jnp.float32), 'Wout': jax.random.normal(ks[4], (D, H * HD), jnp.float32) * s, 'mlp_g': jnp.ones((D,), jnp.float32), 'mlp_b': jnp.zeros((D,), jnp.float32), 'Wgate': jax.random.normal(ks[5], (E, D), jnp.float32) * s, 'fc1s': jax.random.normal(ks[6], (E, DD, D), jnp.float32) * s, 'b1s': jnp.zeros((E, DD), jnp.float32), 'fc2s': jax.random.normal(ks[7], (E, D, DD), jnp.float32) * s, 'b2s': jnp.zeros((E, D), jnp.float32)}
    _L1_cond_all = _L1_cond_setup()
    _L1_cond_in = {k: v for k, v in _L1_cond_all.items() if k in ('W_ada', 'b_ada', 'ln1_g', 'ln1_b', 'Wqkv', 'qn_g', 'qn_b', 'kn_g', 'kn_b', 'Wout', 'mlp_g', 'mlp_b', 'Wgate', 'fc1s', 'b1s', 'fc2s', 'b2s')}
    del _L1_cond_all

    def _L2_cond_setup():
        import jax, jax.numpy as jnp
        import numpy as np
        B, T, DIM = (4, 256, 256)
        COND = 256
        HEADS, DH = (16, 64)
        INNER = HEADS * DH
        MLP = 1024
        EPS = 1e-05

        def _layernorm(x):
            mu = jnp.mean(x, axis=-1, keepdims=True)
            var = jnp.mean(jnp.square(x - mu), axis=-1, keepdims=True)
            return (x - mu) * jax.lax.rsqrt(var + EPS)

        def _modulate(x, shift, scale):
            return x * (1.0 + scale) + shift

        def _attention(x, W_qkv, W_out, b_out):
            Bq, Tq, _ = x.shape
            qkv = x @ W_qkv
            q, k, v = jnp.split(qkv, 3, axis=-1)
            q = q.reshape(Bq, Tq, HEADS, DH)
            k = k.reshape(Bq, Tq, HEADS, DH)
            v = v.reshape(Bq, Tq, HEADS, DH)
            scale = DH ** (-0.5)
            attn = jnp.einsum('bqhd,bkhd->bhqk', q, k) * scale
            attn = jax.nn.softmax(attn, axis=-1)
            out = jnp.einsum('bhqk,bkhd->bqhd', attn, v).reshape(Bq, Tq, INNER)
            return out @ W_out + b_out

        def _ff(x, W1, b1, W2, b2):
            return jax.nn.gelu(x @ W1 + b1, approximate=False) @ W2 + b2
        key = jax.random.key(seed)
        ks = jax.random.split(key, 12)
        s = 0.02
        return {'x': jax.random.normal(ks[0], (B, T, DIM), jnp.float32), 'c': jax.random.normal(ks[1], (B, 1, COND), jnp.float32), 'W_mod': jax.random.normal(ks[2], (COND, 6 * DIM), jnp.float32) * s, 'b_mod': jax.random.normal(ks[3], (6 * DIM,), jnp.float32) * s, 'W_qkv': jax.random.normal(ks[4], (DIM, 3 * INNER), jnp.float32) * s, 'W_out': jax.random.normal(ks[5], (INNER, DIM), jnp.float32) * s, 'b_out': jax.random.normal(ks[6], (DIM,), jnp.float32) * s, 'W1': jax.random.normal(ks[7], (DIM, MLP), jnp.float32) * s, 'b1': jax.random.normal(ks[8], (MLP,), jnp.float32) * s, 'W2': jax.random.normal(ks[9], (MLP, DIM), jnp.float32) * s, 'b2': jax.random.normal(ks[10], (DIM,), jnp.float32) * s}
    _L2_cond_all = _L2_cond_setup()
    _L2_cond_in = {k: v for k, v in _L2_cond_all.items() if k in ('W_mod', 'b_mod', 'W_qkv', 'W_out', 'b_out', 'W1', 'b1', 'W2', 'b2')}
    del _L2_cond_all

    def _L3_cond_setup():
        import jax, jax.numpy as jnp
        import numpy as np
        D_MODEL = 256
        N_HEADS = 16
        HEAD_DIM = D_MODEL // N_HEADS
        D_FF = 1024
        EPS = 1e-05
        THETA = 10000.0
        B, S = (2, 512)

        def _rope_cache(seq_len, head_dim, theta=THETA):
            inv_freq = 1.0 / theta ** (jnp.arange(0, head_dim, 2, dtype=jnp.float32) / head_dim)
            t = jnp.arange(seq_len, dtype=jnp.float32)
            freqs = jnp.einsum('i,j->ij', t, inv_freq)
            emb = jnp.concatenate([freqs, freqs], axis=-1)
            return (jnp.cos(emb), jnp.sin(emb))

        def _rotate_half(x):
            x1, x2 = jnp.split(x, 2, axis=-1)
            return jnp.concatenate([-x2, x1], axis=-1)

        def _ada_rmsnorm(x, time_emb, weight, w1, b1, w2, b2):
            h = jax.nn.silu(time_emb @ w1 + b1)
            scale, shift = jnp.split(h @ w2 + b2, 2, axis=-1)
            norm = x * jax.lax.rsqrt(jnp.mean(x * x, axis=-1, keepdims=True) + EPS)
            return norm * weight * (1.0 + scale[:, None, :]) + shift[:, None, :]
        key = jax.random.key(seed)
        ks = jax.random.split(key, 24)
        rn = lambda k, shp: jax.random.normal(k, shp, dtype=jnp.float32) * 0.02
        return {'x': jax.random.normal(ks[0], (B, S, D_MODEL), dtype=jnp.float32), 'time_emb': jax.random.normal(ks[1], (B, D_MODEL), dtype=jnp.float32), 'w_norm1': jnp.ones((D_MODEL,), jnp.float32), 't1_w1': rn(ks[2], (D_MODEL, D_MODEL)), 't1_b1': jnp.zeros((D_MODEL,), jnp.float32), 't1_w2': rn(ks[3], (D_MODEL, 2 * D_MODEL)), 't1_b2': jnp.zeros((2 * D_MODEL,), jnp.float32), 'w_norm2': jnp.ones((D_MODEL,), jnp.float32), 't2_w1': rn(ks[4], (D_MODEL, D_MODEL)), 't2_b1': jnp.zeros((D_MODEL,), jnp.float32), 't2_w2': rn(ks[5], (D_MODEL, 2 * D_MODEL)), 't2_b2': jnp.zeros((2 * D_MODEL,), jnp.float32), 'wq': rn(ks[6], (D_MODEL, D_MODEL)), 'bq': jnp.zeros((D_MODEL,), jnp.float32), 'wk': rn(ks[7], (D_MODEL, D_MODEL)), 'bk': jnp.zeros((D_MODEL,), jnp.float32), 'wv': rn(ks[8], (D_MODEL, D_MODEL)), 'bv': jnp.zeros((D_MODEL,), jnp.float32), 'wo': rn(ks[9], (D_MODEL, D_MODEL)), 'bo': jnp.zeros((D_MODEL,), jnp.float32), 'w_gate': rn(ks[10], (D_MODEL, D_FF)), 'w_up': rn(ks[11], (D_MODEL, D_FF)), 'w_down': rn(ks[12], (D_FF, D_MODEL))}
    _L3_cond_all = _L3_cond_setup()
    _L3_cond_in = {k: v for k, v in _L3_cond_all.items() if k in ('w_norm1', 't1_w1', 't1_b1', 't1_w2', 't1_b2', 'w_norm2', 't2_w1', 't2_b1', 't2_w2', 't2_b2', 'wq', 'bq', 'wk', 'bk', 'wv', 'bv', 'wo', 'bo', 'w_gate', 'w_up', 'w_down')}
    del _L3_cond_all
    return {'x': x, 'cond_1024': cond_1024, 'L0_cond_ln_g': _L0_cond_in['ln_g'], 'L0_cond_ln_b': _L0_cond_in['ln_b'], 'L0_cond_Wg': _L0_cond_in['Wg'], 'L0_cond_bg': _L0_cond_in['bg'], 'L0_cond_Wb': _L0_cond_in['Wb'], 'L0_cond_bb': _L0_cond_in['bb'], 'L0_cond_Wqkv': _L0_cond_in['Wqkv'], 'L0_cond_bqkv': _L0_cond_in['bqkv'], 'L0_cond_Wp': _L0_cond_in['Wp'], 'L0_cond_bp': _L0_cond_in['bp'], 'L0_cond_W1': _L0_cond_in['W1'], 'L0_cond_b1': _L0_cond_in['b1'], 'L0_cond_W2': _L0_cond_in['W2'], 'L0_cond_b2': _L0_cond_in['b2'], 'L1_cond_W_ada': _L1_cond_in['W_ada'], 'L1_cond_b_ada': _L1_cond_in['b_ada'], 'L1_cond_ln1_g': _L1_cond_in['ln1_g'], 'L1_cond_ln1_b': _L1_cond_in['ln1_b'], 'L1_cond_Wqkv': _L1_cond_in['Wqkv'], 'L1_cond_qn_g': _L1_cond_in['qn_g'], 'L1_cond_qn_b': _L1_cond_in['qn_b'], 'L1_cond_kn_g': _L1_cond_in['kn_g'], 'L1_cond_kn_b': _L1_cond_in['kn_b'], 'L1_cond_Wout': _L1_cond_in['Wout'], 'L1_cond_mlp_g': _L1_cond_in['mlp_g'], 'L1_cond_mlp_b': _L1_cond_in['mlp_b'], 'L1_cond_Wgate': _L1_cond_in['Wgate'], 'L1_cond_fc1s': _L1_cond_in['fc1s'], 'L1_cond_b1s': _L1_cond_in['b1s'], 'L1_cond_fc2s': _L1_cond_in['fc2s'], 'L1_cond_b2s': _L1_cond_in['b2s'], 'L2_cond_W_mod': _L2_cond_in['W_mod'], 'L2_cond_b_mod': _L2_cond_in['b_mod'], 'L2_cond_W_qkv': _L2_cond_in['W_qkv'], 'L2_cond_W_out': _L2_cond_in['W_out'], 'L2_cond_b_out': _L2_cond_in['b_out'], 'L2_cond_W1': _L2_cond_in['W1'], 'L2_cond_b1': _L2_cond_in['b1'], 'L2_cond_W2': _L2_cond_in['W2'], 'L2_cond_b2': _L2_cond_in['b2'], 'L3_cond_w_norm1': _L3_cond_in['w_norm1'], 'L3_cond_t1_w1': _L3_cond_in['t1_w1'], 'L3_cond_t1_b1': _L3_cond_in['t1_b1'], 'L3_cond_t1_w2': _L3_cond_in['t1_w2'], 'L3_cond_t1_b2': _L3_cond_in['t1_b2'], 'L3_cond_w_norm2': _L3_cond_in['w_norm2'], 'L3_cond_t2_w1': _L3_cond_in['t2_w1'], 'L3_cond_t2_b1': _L3_cond_in['t2_b1'], 'L3_cond_t2_w2': _L3_cond_in['t2_w2'], 'L3_cond_t2_b2': _L3_cond_in['t2_b2'], 'L3_cond_wq': _L3_cond_in['wq'], 'L3_cond_bq': _L3_cond_in['bq'], 'L3_cond_wk': _L3_cond_in['wk'], 'L3_cond_bk': _L3_cond_in['bk'], 'L3_cond_wv': _L3_cond_in['wv'], 'L3_cond_bv': _L3_cond_in['bv'], 'L3_cond_wo': _L3_cond_in['wo'], 'L3_cond_bo': _L3_cond_in['bo'], 'L3_cond_w_gate': _L3_cond_in['w_gate'], 'L3_cond_w_up': _L3_cond_in['w_up'], 'L3_cond_w_down': _L3_cond_in['w_down']}

def reference(x, cond_1024, L0_cond_ln_g, L0_cond_ln_b, L0_cond_Wg, L0_cond_bg, L0_cond_Wb, L0_cond_bb, L0_cond_Wqkv, L0_cond_bqkv, L0_cond_Wp, L0_cond_bp, L0_cond_W1, L0_cond_b1, L0_cond_W2, L0_cond_b2, L1_cond_W_ada, L1_cond_b_ada, L1_cond_ln1_g, L1_cond_ln1_b, L1_cond_Wqkv, L1_cond_qn_g, L1_cond_qn_b, L1_cond_kn_g, L1_cond_kn_b, L1_cond_Wout, L1_cond_mlp_g, L1_cond_mlp_b, L1_cond_Wgate, L1_cond_fc1s, L1_cond_b1s, L1_cond_fc2s, L1_cond_b2s, L2_cond_W_mod, L2_cond_b_mod, L2_cond_W_qkv, L2_cond_W_out, L2_cond_b_out, L2_cond_W1, L2_cond_b1, L2_cond_W2, L2_cond_b2, L3_cond_w_norm1, L3_cond_t1_w1, L3_cond_t1_b1, L3_cond_t1_w2, L3_cond_t1_b2, L3_cond_w_norm2, L3_cond_t2_w1, L3_cond_t2_b1, L3_cond_t2_w2, L3_cond_t2_b2, L3_cond_wq, L3_cond_bq, L3_cond_wk, L3_cond_bk, L3_cond_wv, L3_cond_bv, L3_cond_wo, L3_cond_bo, L3_cond_w_gate, L3_cond_w_up, L3_cond_w_down):
    import jax
    import jax.numpy as jnp

    def _L0_cond_ref(hidden, w, ln_g, ln_b, Wg, bg, Wb, bb, Wqkv, bqkv, Wp, bp, W1, b1, W2, b2, num_heads):
        import jax, jax.numpy as jnp
        import numpy as np
        EPS = 1e-05

        def _sln(h, w, ln_g, ln_b, Wg, bg, Wb, bb):
            mu = jnp.mean(h, axis=-1, keepdims=True)
            var = jnp.mean((h - mu) ** 2, axis=-1, keepdims=True)
            ln = (h - mu) / jnp.sqrt(var + EPS) * ln_g + ln_b
            gamma = (w @ Wg.T + bg)[:, None, :]
            beta = (w @ Wb.T + bb)[:, None, :]
            return gamma * ln + beta
        B, N, D = hidden.shape
        hd = D // num_heads
        h = _sln(hidden, w, ln_g, ln_b, Wg, bg, Wb, bb)
        qkv = (h @ Wqkv.T + bqkv).reshape(B, N, num_heads, hd, 3)
        q = jnp.moveaxis(qkv[..., 0], 2, 1)
        k = jnp.moveaxis(qkv[..., 1], 2, 1)
        v = jnp.moveaxis(qkv[..., 2], 2, 1)
        energy = jnp.einsum('bhqd,bhkd->bhqk', q, k)
        att = jax.nn.softmax(energy, axis=-1) / D ** 0.5
        out = jnp.einsum('bhqk,bhkd->bhqd', att, v)
        out = jnp.moveaxis(out, 1, 2).reshape(B, N, D)
        out = out @ Wp.T + bp
        h1 = out + hidden
        h2 = _sln(h1, w, ln_g, ln_b, Wg, bg, Wb, bb)
        return h2 + h1

    def _L1_cond_ref(x, t, W_ada, b_ada, ln1_g, ln1_b, Wqkv, qn_g, qn_b, kn_g, kn_b, Wout, mlp_g, mlp_b, Wgate, fc1s, b1s, fc2s, b2s):
        import jax, jax.numpy as jnp
        import numpy as np
        B, N, D = (2, 512, 256)
        H, HD = (16, 64)
        E, DD = (8, 1024)
        EPS = 1e-05

        def _ln(x, g, b):
            m = jnp.mean(x, axis=-1, keepdims=True)
            v = jnp.var(x, axis=-1, keepdims=True)
            return (x - m) * jax.lax.rsqrt(v + EPS) * g + b
        b, n, d = x.shape
        shift = jax.nn.silu(t) @ W_ada.T + b_ada
        h = _ln(x, ln1_g, ln1_b) + shift
        qkv = (h @ Wqkv.T).reshape(b, n, 3, H, HD)
        q = _ln(qkv[:, :, 0].transpose(0, 2, 1, 3), qn_g, qn_b)
        k = _ln(qkv[:, :, 1].transpose(0, 2, 1, 3), kn_g, kn_b)
        v = qkv[:, :, 2].transpose(0, 2, 1, 3)
        scores = jnp.einsum('bhnd,bhmd->bhnm', q, k) / jnp.sqrt(jnp.float32(HD))
        attn = jax.nn.softmax(scores, axis=-1)
        o = jnp.einsum('bhnm,bhmd->bhnd', attn, v)
        o = o.transpose(0, 2, 1, 3).reshape(b, n, H * HD)
        x = x + o @ Wout.T
        tok = x.reshape(-1, d)
        bs = tok.shape[0]
        gate = jax.nn.softmax(tok @ Wgate.T, axis=-1)
        k_cap = bs // E
        vals, idx = jax.lax.top_k(gate.T, k_cap)
        idx_flat = idx.T.reshape(-1)
        w = vals.T
        g = _ln(tok[idx_flat], mlp_g, mlp_b).reshape(k_cap, E, d)
        y = jnp.einsum('ked,ehd->keh', g, fc1s) + b1s
        y = jax.nn.gelu(y, approximate=True)
        y = jnp.einsum('keh,edh->ked', y, fc2s) + b2s
        y = y * w[..., None]
        tok = tok.at[idx_flat].add(y.reshape(-1, d))
        return tok.reshape(x.shape)

    def _L2_cond_ref(x, c, W_mod, b_mod, W_qkv, W_out, b_out, W1, b1, W2, b2):
        import jax, jax.numpy as jnp
        import numpy as np
        B, T, DIM = (4, 256, 256)
        COND = 256
        HEADS, DH = (16, 64)
        INNER = HEADS * DH
        MLP = 1024
        EPS = 1e-05

        def _layernorm(x):
            mu = jnp.mean(x, axis=-1, keepdims=True)
            var = jnp.mean(jnp.square(x - mu), axis=-1, keepdims=True)
            return (x - mu) * jax.lax.rsqrt(var + EPS)

        def _modulate(x, shift, scale):
            return x * (1.0 + scale) + shift

        def _attention(x, W_qkv, W_out, b_out):
            Bq, Tq, _ = x.shape
            qkv = x @ W_qkv
            q, k, v = jnp.split(qkv, 3, axis=-1)
            q = q.reshape(Bq, Tq, HEADS, DH)
            k = k.reshape(Bq, Tq, HEADS, DH)
            v = v.reshape(Bq, Tq, HEADS, DH)
            scale = DH ** (-0.5)
            attn = jnp.einsum('bqhd,bkhd->bhqk', q, k) * scale
            attn = jax.nn.softmax(attn, axis=-1)
            out = jnp.einsum('bhqk,bkhd->bqhd', attn, v).reshape(Bq, Tq, INNER)
            return out @ W_out + b_out

        def _ff(x, W1, b1, W2, b2):
            return jax.nn.gelu(x @ W1 + b1, approximate=False) @ W2 + b2
        mod = jax.nn.silu(c) @ W_mod + b_mod
        sh_msa, sc_msa, g_msa, sh_mlp, sc_mlp, g_mlp = jnp.split(mod, 6, axis=-1)
        x = x + g_msa * _attention(_modulate(_layernorm(x), sh_msa, sc_msa), W_qkv, W_out, b_out)
        x = x + g_mlp * _ff(_modulate(_layernorm(x), sh_mlp, sc_mlp), W1, b1, W2, b2)
        return x

    def _L3_cond_ref(x, time_emb, w_norm1, t1_w1, t1_b1, t1_w2, t1_b2, w_norm2, t2_w1, t2_b1, t2_w2, t2_b2, wq, bq, wk, bk, wv, bv, wo, bo, w_gate, w_up, w_down):
        import jax, jax.numpy as jnp
        import numpy as np
        D_MODEL = 256
        N_HEADS = 16
        HEAD_DIM = D_MODEL // N_HEADS
        D_FF = 1024
        EPS = 1e-05
        THETA = 10000.0
        B, S = (2, 512)

        def _rope_cache(seq_len, head_dim, theta=THETA):
            inv_freq = 1.0 / theta ** (jnp.arange(0, head_dim, 2, dtype=jnp.float32) / head_dim)
            t = jnp.arange(seq_len, dtype=jnp.float32)
            freqs = jnp.einsum('i,j->ij', t, inv_freq)
            emb = jnp.concatenate([freqs, freqs], axis=-1)
            return (jnp.cos(emb), jnp.sin(emb))

        def _rotate_half(x):
            x1, x2 = jnp.split(x, 2, axis=-1)
            return jnp.concatenate([-x2, x1], axis=-1)

        def _ada_rmsnorm(x, time_emb, weight, w1, b1, w2, b2):
            h = jax.nn.silu(time_emb @ w1 + b1)
            scale, shift = jnp.split(h @ w2 + b2, 2, axis=-1)
            norm = x * jax.lax.rsqrt(jnp.mean(x * x, axis=-1, keepdims=True) + EPS)
            return norm * weight * (1.0 + scale[:, None, :]) + shift[:, None, :]
        b, s, _ = x.shape
        cos, sin = _rope_cache(s, HEAD_DIM)
        nx = _ada_rmsnorm(x, time_emb, w_norm1, t1_w1, t1_b1, t1_w2, t1_b2)
        q = (nx @ wq + bq).reshape(b, s, N_HEADS, HEAD_DIM)
        k = (nx @ wk + bk).reshape(b, s, N_HEADS, HEAD_DIM)
        v = (nx @ wv + bv).reshape(b, s, N_HEADS, HEAD_DIM)
        c = cos[:, None, :]
        si = sin[:, None, :]
        q = q * c + _rotate_half(q) * si
        k = k * c + _rotate_half(k) * si
        scores = jnp.einsum('bshd,bthd->bhst', q, k) / jnp.sqrt(jnp.float32(HEAD_DIM))
        probs = jax.nn.softmax(scores, axis=-1)
        attn = jnp.einsum('bhst,bthd->bshd', probs, v).reshape(b, s, D_MODEL)
        x = x + attn @ wo + bo
        nx = _ada_rmsnorm(x, time_emb, w_norm2, t2_w1, t2_b1, t2_w2, t2_b2)
        gate = jax.nn.gelu(nx @ w_gate, approximate=False)
        ff = gate * (nx @ w_up) @ w_down
        return x + ff
    x = _L0_cond_ref(x, cond_1024, L0_cond_ln_g, L0_cond_ln_b, L0_cond_Wg, L0_cond_bg, L0_cond_Wb, L0_cond_bb, L0_cond_Wqkv, L0_cond_bqkv, L0_cond_Wp, L0_cond_bp, L0_cond_W1, L0_cond_b1, L0_cond_W2, L0_cond_b2, 16)
    x = _L1_cond_ref(x, cond_1024[:, None, :], L1_cond_W_ada, L1_cond_b_ada, L1_cond_ln1_g, L1_cond_ln1_b, L1_cond_Wqkv, L1_cond_qn_g, L1_cond_qn_b, L1_cond_kn_g, L1_cond_kn_b, L1_cond_Wout, L1_cond_mlp_g, L1_cond_mlp_b, L1_cond_Wgate, L1_cond_fc1s, L1_cond_b1s, L1_cond_fc2s, L1_cond_b2s)
    x = _L2_cond_ref(x, cond_1024[:, None, :], L2_cond_W_mod, L2_cond_b_mod, L2_cond_W_qkv, L2_cond_W_out, L2_cond_b_out, L2_cond_W1, L2_cond_b1, L2_cond_W2, L2_cond_b2)
    x = _L3_cond_ref(x, cond_1024, L3_cond_w_norm1, L3_cond_t1_w1, L3_cond_t1_b1, L3_cond_t1_w2, L3_cond_t1_b2, L3_cond_w_norm2, L3_cond_t2_w1, L3_cond_t2_b1, L3_cond_t2_w2, L3_cond_t2_b2, L3_cond_wq, L3_cond_bq, L3_cond_wk, L3_cond_bk, L3_cond_wv, L3_cond_bv, L3_cond_wo, L3_cond_bo, L3_cond_w_gate, L3_cond_w_up, L3_cond_w_down)
    return x

_drawn_inputs = setup_inputs


def setup_inputs(seed=0):
    import zlib

    import numpy as np

    out = dict(_drawn_inputs(seed))
    spreads = {'L0_cond_ln_g': (1.0, 0.2),
     'L0_cond_ln_b': (0.0, 0.1),
     'L0_cond_bg': (0.0, 0.1),
     'L0_cond_bb': (0.0, 0.1),
     'L0_cond_bqkv': (0.0, 0.8),
     'L0_cond_bp': (0.0, 0.1),
     'L0_cond_b1': (0.0, 0.1),
     'L0_cond_b2': (0.0, 0.1),
     'L1_cond_b_ada': (0.0, 0.616),
     'L1_cond_ln1_g': (1.0, 0.6),
     'L1_cond_ln1_b': (0.0, 0.765),
     'L1_cond_qn_g': (1.0, 0.6),
     'L1_cond_qn_b': (0.0, 0.8),
     'L1_cond_kn_g': (1.0, 0.6),
     'L1_cond_kn_b': (0.0, 2.0),
     'L1_cond_mlp_g': (1.0, 0.6),
     'L1_cond_mlp_b': (0.0, 0.8),
     'L1_cond_b1s': (0.0, 0.8),
     'L1_cond_b2s': (0.0, 0.571),
     'L3_cond_w_norm1': (1.0, 0.6),
     'L3_cond_t1_b1': (0.0, 0.8),
     'L3_cond_t1_b2': (0.0, 0.8),
     'L3_cond_w_norm2': (1.0, 0.6),
     'L3_cond_t2_b1': (0.0, 0.8),
     'L3_cond_t2_b2': (0.0, 0.8),
     'L3_cond_bq': (0.0, 0.8),
     'L3_cond_bk': (0.0, 2.0),
     'L3_cond_bv': (0.0, 0.416),
     'L3_cond_bo': (0.0, 0.1)}
    factors = {'L1_cond_fc1s': 3.388,
     'L1_cond_fc2s': 3.164,
     'L2_cond_W_mod': 2.989,
     'L2_cond_b_mod': 8.0,
     'L2_cond_W_qkv': 4.007,
     'L2_cond_W_out': 3.97,
     'L2_cond_b_out': 8.0,
     'L2_cond_W1': 4.638,
     'L2_cond_b1': 8.0,
     'L2_cond_W2': 4.521,
     'L2_cond_b2': 8.0,
     'L3_cond_t1_w1': 8.0,
     'L3_cond_t1_w2': 8.0,
     'L3_cond_t2_w1': 8.0,
     'L3_cond_t2_w2': 8.0,
     'L3_cond_wq': 8.0,
     'L3_cond_wk': 8.0}
    for name, (base, spread) in spreads.items():
        noise = np.random.default_rng([zlib.crc32(name.encode()), seed]).standard_normal(out[name].shape)
        drawn = base * np.exp(spread * noise) if base else spread * noise
        out[name] = jnp.asarray(drawn.astype(out[name].dtype))
    for name, factor in factors.items():
        out[name] = (out[name] * factor).astype(out[name].dtype)
    return out
```

```python
import numpy as np
from contextlib import ExitStack
from math import prod

import concourse.bass as bass
from concourse import mybir

FP32 = mybir.dt.float32
BF16 = mybir.dt.bfloat16
I32 = mybir.dt.int32
ALU = mybir.AluOpType
ACT = mybir.ActivationFunctionType
AX = mybir.AxisListType

P = 128
B, N, D = 64, 64, 256
T = B * N
NT = T // P
KC = D // P
H = 16
HJ = H // 2
F = 1024
FJ = F // P
E8 = 8
CAP = T // E8
NG = T // 512
ROW = D + E8
EPS = 1e-5

COLS = {}
_at = 0
for _name, _n in [("l0_g", 2), ("l0_b", 2), ("l0_bgb", 4), ("l0_bqk", 4), ("l0_bv", 2),
                  ("l1_bada", 2), ("l1_g", 2), ("l1_b", 2), ("l1_qn", 4), ("l1_mlp", 4),
                  ("l2_bmod", 12), ("l2_bout", 2), ("l2_b1", 8), ("l2_b2", 2),
                  ("l3_w1", 2), ("l3_w2", 2), ("l3_tb1", 4), ("l3_tb2", 8),
                  ("l3_bqk", 4), ("l3_bqkr", 4), ("l3_bv", 2)]:
    COLS[_name] = (_at, _n)
    _at += _n
NCOL = _at

TABS = ["g0", "b0", "g1", "b1", "g2", "b2", "gate2", "g2f", "b2f", "gate2f", "g3", "b3", "g3f", "b3f"]
LAST_STAGE = 8

CONSTS = {}
_at = 0
for _name, _n in [("ident", P), ("ones", P), ("lower", P), ("trig", 2 * N), ("par", 2), ("iota16", 16),
                  ("iota32", 32), ("pidx", 1), ("tidx", NT)]:
    CONSTS[_name] = (_at, _n)
    _at += _n
NCONST = _at


class Chain:

    def __init__(self, eng, sem):
        self.eng, self.sem, self.n = eng, sem, 0

    def reset(self):
        self.eng.sem_clear(self.sem)
        self.n = 0

    def link(self, ins):
        self.n += 1
        ins.then_inc(self.sem, 1)
        self.eng.wait_ge(self.sem, self.n)


class Signal:

    def __init__(self, sem, base):
        self.sem, self.base = sem, base


def after(eng, signal, count):
    if isinstance(count, int) and count <= 0:
        return
    eng.wait_ge(signal.sem, count + signal.base)


def after_all(eng, done, waits):
    values = []
    for signal, count in waits:
        if isinstance(count, int):
            if count > 0:
                values.append((signal, count + signal.base))
        else:
            values.append((signal, eng.to_reg(count + signal.base)))
    eng.wait_ge(done, 1)
    for signal, value in values:
        eng.wait_ge(signal.sem, value)


def tiles(eng, count, first, step):
    first()
    step(0, True)
    with eng.Fori(1, count - 1) as t:
        step(t, True)
    step(count - 1, False)


def pairs(eng, count, first, step):
    first()
    step(0, 0, 0, True)
    with eng.Fori(0, (count - 2) // 2) as i:
        step(i * 2 + 1, 1, i, True)
        step(i * 2 + 2, 0, i + 1, True)
    step(count - 1, (count - 1) % 2, (count - 1) // 2, False)


def build_program(nc, A, out, stage=LAST_STAGE):
    ctx = ExitStack()
    with ctx:
        def sb(name, shape, dt=FP32):
            return ctx.enter_context(nc.sbuf_tensor(name, shape, dt))

        def sem(name):
            return ctx.enter_context(nc.semaphore(name))

        def sems(prefix, names):
            return {n: sem(f"{prefix}_{n}") for n in names.split()}

        shared = {}

        def signals(names, total):
            out = {}
            for n in names.split():
                if n not in shared:
                    shared[n] = [sem(n), 0]
                out[n] = Signal(*shared[n])
                shared[n][1] += total
            return out

        x = sb("x", [P, NT, D])
        col = sb("col", [P, NCOL])
        tab = sb("tab", [P, len(TABS), KC, B])
        gates = sb("gates", [P, NT, E8])
        moments = sb("moments", [P, NT, 2])
        rstd = sb("rstd", [P, NT])
        stat6 = sb("stat6", [P, 4, 6])
        mv = sb("mv", [P, 4, 2])
        newton = sb("newton", [P, 4, NT])
        bias_row = sb("bias_row", [P, 2, D])
        r1 = sb("r1", [P, 12288])
        r2 = sb("r2", [P, 9216])
        work = sb("work", [P, 11264])

        def c(name, i=0, n=1):
            at, _ = COLS[name]
            return col[:, at + i:at + i + n]

        def table(name):
            return tab[:, TABS.index(name), :, :]

        class Region:

            def __init__(self, region):
                self.region, self.at = region, 0

            def take(self, *shape):
                n = prod(shape)
                ap = self.region[:, self.at:self.at + n]
                self.at += n
                assert self.at <= self.region.shape[1], self.at
                if len(shape) == 2:
                    ap = ap.rearrange("p (a b) -> p a b", b=shape[1])
                if len(shape) == 3:
                    ap = ap.rearrange("p (a b c) -> p a b c", b=shape[1], c=shape[2])
                return ap

        R = Region(r1)
        l0_w, l0_wp = R.take(KC, 768), R.take(KC, D)
        l1_w, l1_wout, l1_wgate = R.take(KC, 3 * F), R.take(FJ, D), R.take(KC, E8)
        R = Region(r1)
        l2_w, l2_wout, l2_w1, l2_w2 = R.take(KC, 3 * F), R.take(FJ, D), R.take(KC, F), R.take(FJ, D)
        R = Region(r2)
        m0, m1, m2 = R.take(KC, 512), R.take(KC, D), R.take(KC, 1536)
        m3a, m3b = R.take(2 * KC, D), R.take(2 * KC, 512)
        R = Region(r2)
        fc1 = [R.take(KC, F) for _ in range(2)]
        fc2 = [R.take(FJ, D) for _ in range(2)]
        R = Region(r2)
        l3_w, l3_wo = R.take(KC, 1280), R.take(KC, D)
        l3_gate, l3_up, l3_down = R.take(KC, F), R.take(KC, F), R.take(FJ, D)

        def pb(name, banks):
            return ctx.enter_context(nc.psum_tensor(name, [P, 512 * banks], FP32))

        psS, psP, psO, psW0, psW1 = pb("psS", 2), pb("psP", 2), pb("psO", 2), pb("psW0", 1), pb("psW1", 1)

        gather_table = nc.dram_tensor("gather_table", [T, ROW], FP32, kind="Internal").ap()
        moe_sum = nc.dram_tensor("moe_sum", [T, D], FP32, kind="Internal").ap()
        slot_token = nc.dram_tensor("slot_token", [E8 * CAP], I32, kind="Internal").ap()

        ld = sems("ld", "small modw x l0 l1 l2 l3 back rows")
        st = sems("st", "out tab gates idx")
        chain_dve = sem("chain_dve")
        su = sems("su", "mm silu table hidden mm2 ones center")

        class Attention:

            def __init__(self, li):
                self.li = li
                self.wide = li in (1, 2)
                W = Region(work)
                self.xn = W.take(D)
                self.hT = W.take(KC, P)
                self.tmpT = W.take(KC, P)
                self.qk = W.take(16, P) if self.wide else W.take(4, P)
                self.v = W.take(F) if self.wide else W.take(H, 17)
                self.E = W.take(16, N)
                self.PT = W.take(HJ, P)
                self.mx = W.take(16)
                self.rs = W.take(16)
                self.oT = W.take(FJ, P) if self.wide else W.take(KC, P)
                if li == 1:
                    self.sq = [W.take(8, 64) for _ in range(2)]
                    self.qn = [W.take(8, 64) for _ in range(4)]
                    self.ss = W.take(4, 8)
                if self.wide:
                    self.x1 = W.take(D)
                    self.x1T = W.take(KC, P)
                else:
                    self.qe, self.qo = W.take(KC, P), W.take(KC, P)
                    self.o16 = W.take(D)
                    self.rot = W.take(4, P)
                    self.rot2 = W.take(4, P)
                self.g, self.b = table(f"g{li}"), table(f"b{li}")
                self.s = signals("xn a h s sub exp ta tb pta ptb pv ote y xupd v"
                              + {0: " qk qke mask half vp on ot xb",
                                 1: " prob rsum i0 i1 i2 i3 cp0 cp1 cp2 cp3 sq0 sq1 sq2 sq3 r0 r1 r2 r3"
                                    " n0 n1 n2 n3 t0 t1 t2 t3 e0 e1 e2 e3 v0 v1 v0e x1t x1e lg gate",
                                 2: " prob rsum i0 i1 i2 i3 e0 e1 e2 e3 v0 v1 v0e yt bk",
                                 3: " qk qke mask half vp on ot xb"}[li], NT)
                self.loads = {0: 2, 1: 3, 2: 4, 3: 5}[li]
                self.ready = {0: ld["l0"], 1: ld["l1"], 2: ld["l2"], 3: ld["l3"]}[li]

        def pe_transpose_x(pe, L, n):
            after(pe, L.s["xn"], n + 1)
            if L.wide:
                after(pe, L.s["e3"], n)
            else:
                after(pe, L.s["qke"], n)
            for k in range(KC):
                ins = nc.tensor.transpose(psW0[:, k * P:(k + 1) * P], L.xn[:, k * P:(k + 1) * P], ident)
            ins.then_inc(L.s["a"].sem, 1)

        def pe_project(L, ps, w, lo, chunks):
            for q in range(chunks):
                for k in range(KC):
                    ins = nc.tensor.matmul(ps[:, q * P:(q + 1) * P], w[:, k, lo + q * P:lo + (q + 1) * P],
                                           L.hT[:, k, :], start=(k == 0), stop=(k == KC - 1))
            return ins

        def pe_project_tokens(L, ps, w, lo, width):
            for k in range(KC):
                ins = nc.tensor.matmul(ps[:, 0:width], L.hT[:, k, :], w[:, k, lo:lo + width],
                                       start=(k == 0), stop=(k == KC - 1))
            return ins

        def pe_narrow_qk(pe, L, n):
            after(pe, L.s["h"], n + 1)
            after(pe, L.s["v"], n)
            if L.li == 0:
                pe_project(L, psW1, l0_w, 0, 4).then_inc(L.s["qk"].sem, 1)
            else:
                pe_project(L, psW1, l3_w, 0, 4)
                pe_project(L, psW0, l3_w, 512, 4).then_inc(L.s["qk"].sem, 1)

        def pe_narrow_v(pe, L, n):
            after(pe, L.s["qke"], n + 1)
            w, lo = (l0_w, 512) if L.li == 0 else (l3_w, 1024)
            pe_project_tokens(L, psW1, w, lo, D).then_inc(L.s["vp"].sem, 1)

        def pe_l1_qk(pe, L, n):
            after(pe, L.s["h"], n + 1)
            after(pe, L.s["e2"], n)
            for i in range(4):
                if i >= 2:
                    after(pe, L.s[f"cp{i - 2}"], n + 1)
                pe_project_tokens(L, (psW0 if i % 2 else psW1)[:, :], l1_w, 512 * i, 512).then_inc(L.s[f"i{i}"].sem, 1)

        def pe_l1_turn(pe, L, n):
            for i in range(4):
                after(pe, L.s[f"n{i}"], n + 1)
                if i < 2:
                    after(pe, L.s[f"cp{i + 2}"], n + 1)
                else:
                    after(pe, L.s[f"e{i - 2}"], n + 1)
                ps = psW0 if i % 2 else psW1
                for j in range(4):
                    ins = nc.tensor.transpose(ps[:, j * P:(j + 1) * P], L.qn[i][:, 2 * j:2 * j + 2, :], ident)
                ins.then_inc(L.s[f"t{i}"].sem, 1)

        def pe_l2_qk(pe, L, n):
            after(pe, L.s["h"], n + 1)
            after(pe, L.s["e2"], n)
            pe_project(L, psW1, l2_w, 0, 4).then_inc(L.s["i0"].sem, 1)
            pe_project(L, psW0, l2_w, 512, 4).then_inc(L.s["i1"].sem, 1)
            after(pe, L.s["e0"], n + 1)
            pe_project(L, psW1, l2_w, 1024, 4).then_inc(L.s["i2"].sem, 1)
            after(pe, L.s["e1"], n + 1)
            pe_project(L, psW0, l2_w, 1536, 4).then_inc(L.s["i3"].sem, 1)

        def pe_wide_v(pe, L, n):
            w = l1_w if L.li == 1 else l2_w
            after(pe, L.s["ote"], n)
            pe_project_tokens(L, psO[:, 0:512], w, 2048, 512).then_inc(L.s["v0"].sem, 1)
            pe_project_tokens(L, psO[:, 512:1024], w, 2560, 512).then_inc(L.s["v1"].sem, 1)

        def pe_scores(pe, L, t):
            ready = {0: ("mask",), 1: ("e3",), 2: ("e2", "e3"), 3: ("mask",)}[L.li]
            after_all(pe, su["table"], [(L.s[r], t + 1) for r in ready] + [(L.s["sub"], t)])
            if L.wide:
                for j in range(HJ):
                    for b in range(2):
                        for hp in range(2):
                            rows = slice(64 * hp, 64 * hp + 64)
                            ins = nc.tensor.matmul(psS[rows, (2 * j + b) * N:(2 * j + b + 1) * N],
                                                   L.qk[rows, j, b * N:(b + 1) * N],
                                                   L.qk[rows, HJ + j, b * N:(b + 1) * N], start=True, stop=True)
            else:
                for half in range(2):
                    if half:
                        after_all(pe, su["table"], [(L.s["half"], t + 1)])
                    for ch in range(KC):
                        for b in range(2):
                            for hp, q in enumerate((L.qe, L.qo)):
                                for r in (2 * half, 2 * half + 1):
                                    rows = slice(32 * r, 32 * r + 32)
                                    at = narrow_block(r, ch, b) * N
                                    ins = nc.tensor.matmul(psS[64 * hp:64 * hp + 64, at:at + N],
                                                           q[rows, ch, b * N:(b + 1) * N],
                                                           L.qk[rows, KC + ch, b * N:(b + 1) * N],
                                                           start=True, stop=True)
                    if half == 0:
                        ins.then_inc(L.s["half"].sem, 1)
            ins.then_inc(L.s["s"].sem, 1)

        def narrow_block(r, ch, b):
            return (((r % 2) * 2 + r // 2) * 2 + ch) * 2 + b

        def narrow_pair(j):
            rp, rh, ch = j // 4, (j // 2) % 2, j % 2
            return 8 * ch + 2 * (2 * rh + rp)

        def pe_transpose_probs(pe, L, t):
            after(pe, L.s["prob" if L.wide else "exp"], t + 1)
            after(pe, L.s[{0: "ptb", 1: "gate", 2: "xupd", 3: "ptb"}[L.li]], t)
            for j in range(HJ):
                ins = nc.tensor.transpose(psP[:, j * P:(j + 1) * P], L.E[:, 2 * j:2 * j + 2, :], ident)
                if j == 3:
                    ins.then_inc(L.s["ta"].sem, 1)
            ins.then_inc(L.s["tb"].sem, 1)

        def pe_narrow_pv(pe, L, t):
            after_all(pe, su["table"], [(L.s["v"], t + 1), (L.s["xupd"], t), (L.s["pta"], t + 1)])
            for j in range(HJ):
                if j == 4:
                    after_all(pe, su["table"], [(L.s["ptb"], t + 1)])
                for b in range(2):
                    rows = slice(64 * b, 64 * b + 64)
                    for hp in range(2):
                        h = narrow_pair(j) + hp
                        ins = nc.tensor.matmul(psO[rows, h * 17:(h + 1) * 17], L.PT[rows, j, 64 * hp:64 * hp + 64],
                                               L.v[rows, h, :], start=True, stop=True)
            ins.then_inc(L.s["pv"].sem, 1)

        def pe_wide_pv(pe, L, t):
            after_all(pe, su["table"], [(L.s["v"], t + 1), (L.s["pta"], t + 1)])
            for j in range(HJ):
                if j == 4:
                    after_all(pe, su["table"], [(L.s["ptb"], t + 1)])
                for b in range(2):
                    rows = slice(64 * b, 64 * b + 64)
                    for hp in range(2):
                        h = 2 * j + hp
                        ins = nc.tensor.matmul(psO[64 * hp:64 * hp + 64, b * 512 + j * N:b * 512 + (j + 1) * N],
                                               L.v[rows, h * 64:(h + 1) * 64], L.PT[rows, j, 64 * hp:64 * hp + 64],
                                               start=True, stop=True)
            ins.then_inc(L.s["pv"].sem, 1)

        def pe_narrow_out(pe, L, t):
            after(pe, L.s["on"], t + 1)
            for k in range(KC):
                ins = nc.tensor.transpose(psO[:, 512 + k * P:512 + (k + 1) * P], L.o16[:, k * P:(k + 1) * P],
                                          ident)
            ins.then_inc(L.s["ot"].sem, 1)
            w = l0_wp if L.li == 0 else l3_wo
            after(pe, L.s["ote"], t + 1)
            for k in range(KC):
                ins = nc.tensor.matmul(psO[:, 0:D], L.oT[:, k, :], w[:, k, :], start=(k == 0), stop=(k == KC - 1))
            ins.then_inc(L.s["y"].sem, 1)

        def pe_l1_out(pe, L, t):
            after(pe, L.s["ote"], t + 1)
            for j in range(FJ):
                ins = nc.tensor.matmul(psP[:, 0:D], L.oT[:, j, :], l1_wout[:, j, :], start=(j == 0), stop=(j == FJ - 1))
            ins.then_inc(L.s["y"].sem, 1)
            after(pe, L.s["xupd"], t + 1)
            for k in range(KC):
                ins = nc.tensor.transpose(psP[:, 512 + k * P:512 + (k + 1) * P], L.x1[:, k * P:(k + 1) * P], ident)
            ins.then_inc(L.s["x1t"].sem, 1)
            after(pe, L.s["x1e"], t + 1)
            for k in range(KC):
                ins = nc.tensor.matmul(psP[:, 0:E8], L.x1T[:, k, :], l1_wgate[:, k, :], start=(k == 0), stop=(k == KC - 1))
            ins.then_inc(L.s["lg"].sem, 1)

        def pe_l2_out(pe, L, t):
            after(pe, L.s["ote"], t + 1)
            for q in range(KC):
                for j in range(FJ):
                    ins = nc.tensor.matmul(psP[:, q * P:(q + 1) * P], l2_wout[:, j, q * P:(q + 1) * P], L.oT[:, j, :],
                                           start=(j == 0), stop=(j == FJ - 1))
            ins.then_inc(L.s["y"].sem, 1)
            after(pe, L.s["yt"], t + 1)
            for k in range(KC):
                ins = nc.tensor.transpose(psP[:, 512 + k * P:512 + (k + 1) * P], L.x1T[:, k, :], ident)
            ins.then_inc(L.s["bk"].sem, 1)

        def pe_attention(pe, L):
            qk = {0: pe_narrow_qk, 1: pe_l1_qk, 2: pe_l2_qk, 3: pe_narrow_qk}[L.li]
            v = pe_wide_v if L.wide else pe_narrow_v
            pv = pe_wide_pv if L.wide else pe_narrow_pv
            pe.wait_ge(L.ready, 16 * L.loads)
            if not L.wide:
                pe.wait_ge(su["ones"], 1 if L.li == 0 else 2)
            if L.li == 1:
                pe.wait_ge(su["center"], 1)

            def first():
                pe_transpose_x(pe, L, 0)
                qk(pe, L, 0)
                if L.li == 1:
                    pe_l1_turn(pe, L, 0)
                v(pe, L, 0)

            def step(t, more):
                pe_scores(pe, L, t)
                if more:
                    pe_transpose_x(pe, L, t + 1)
                    qk(pe, L, t + 1)
                pe_transpose_probs(pe, L, t)
                pv(pe, L, t)
                if more:
                    if L.li == 1:
                        pe_l1_turn(pe, L, t + 1)
                    v(pe, L, t + 1)
                if not L.wide:
                    pe_narrow_out(pe, L, t)
                elif L.li == 1:
                    pe_l1_out(pe, L, t)
                else:
                    pe_l2_out(pe, L, t)

            tiles(pe, NT, first, step)

        def batches(ap, n, count=2):
            return ap[:, :, bass.ds(n * count, count)].unsqueeze(3).broadcast_to([P, KC, count, N])

        def four(ap):
            return ap.rearrange("p k (b n) -> p k b n", n=N)

        def dve_rsqrt(ch, out, var):
            shape = var.shape
            n = prod(shape[1:])
            v, y, q, g = (newton[:, i, 0:n] for i in range(4))
            if len(shape) == 3:
                v3, o3 = v.rearrange("p (a b) -> p a b", b=shape[2]), y.rearrange("p (a b) -> p a b", b=shape[2])
            else:
                v3, o3 = v, y
            ch.link(nc.vector.tensor_scalar(v3, var, EPS, None, ALU.add))
            ch.link(nc.vector.tensor_scalar(g.bitcast(I32), v.bitcast(I32), 1, None, ALU.logical_shift_right))
            ch.link(nc.vector.tensor_scalar(y.bitcast(I32), g.bitcast(I32), -1.0, float(0x5F3759DF), ALU.mult, ALU.add))
            for i in range(3):
                ch.link(nc.vector.tensor_tensor(q, y, y, ALU.mult))
                ch.link(nc.vector.tensor_tensor(q, q, v, ALU.mult))
                ch.link(nc.vector.tensor_scalar(q, q, -0.5, 1.5, ALU.mult, ALU.add))
                if i < 2:
                    ch.link(nc.vector.tensor_tensor(y, y, q, ALU.mult))
            ch.link(nc.vector.tensor_tensor(out, o3, q.rearrange("p (a b) -> p a b", b=shape[2])
                                            if len(shape) == 3 else q, ALU.mult))

        def dve_moments(ch, t):
            ch.link(nc.vector.bn_stats(stat6[:, 0, :], x[:, t, :]))
            ch.link(nc.vector.bn_aggr(mv[:, 0, :], stat6[:, 0, :]))
            ch.link(nc.vector.tensor_copy(moments[:, t, :], mv[:, 0, :]))

        def dve_rstd(ch, rms=False):
            mean, var = moments[:, :, 0], moments[:, :, 1]
            if rms:
                ch.link(nc.vector.tensor_tensor(rstd[:, :], mean, mean, ALU.mult))
                ch.link(nc.vector.tensor_tensor(rstd[:, :], rstd[:, :], var, ALU.add))
                var = rstd[:, :]
            dve_rsqrt(ch, rstd[:, :], var)

        def dve_normalise(out, src, n, rms=False):
            if rms:
                return nc.vector.tensor_scalar(out, src, rstd[:, bass.ds(n, 1)], None, ALU.mult)
            return nc.vector.tensor_scalar(out, src, moments[:, n, 0:1], rstd[:, bass.ds(n, 1)],
                                           ALU.subtract, ALU.mult)

        def dve_norm(v, ch, L, n):
            after(v, L.s["a"], n)
            dve_normalise(L.xn, x[:, n, :], n, rms=L.li == 3).then_inc(L.s["xn"].sem, 1)

        def dve_modulate(v, ch, L, n):
            after(v, L.s["a"], n + 1)
            ps = psW0[:, 0:D].rearrange("p (k b n) -> p k b n", k=KC, n=N)
            ch.link(nc.vector.tensor_tensor(four(L.tmpT), ps, batches(L.g, n), ALU.mult))
            after(v, L.s["v1" if L.wide else "vp"], n)
            nc.vector.tensor_tensor(four(L.hT), four(L.tmpT), batches(L.b, n), ALU.add).then_inc(L.s["h"].sem, 1)

        def dve_softmax(v, ch, L, t):
            after(v, L.s["s"], t + 1)
            ps = psS[:, :].rearrange("p (a b) -> p a b", b=N)
            ch.link(nc.vector.tensor_reduce(L.mx, ps, AX.X, ALU.max))
            after(v, L.s["tb"], t)
            nc.vector.tensor_tensor(L.E, ps, L.mx.unsqueeze(2).broadcast_to([P, 16, N]),
                                    ALU.subtract).then_inc(L.s["sub"].sem, 1)

        def dve_prob_sums(v, ch, L, t):
            after(v, L.s["exp"], t + 1)
            ch.link(nc.vector.tensor_reduce(L.mx, L.E, AX.X, ALU.add))
            after(v, L.s["prob"], t)
            nc.vector.reciprocal(L.rs, L.mx).then_inc(L.s["rsum"].sem, 1)

        def dve_narrow_qk(v, ch, L, n):
            after(v, L.s["qk"], n + 1)
            ps = psW1[:, :].rearrange("p (a b) -> p a b", b=P)

            def bias(name):
                return c(name, 0, 4).unsqueeze(2).broadcast_to([P, 4, P])

            if L.li == 0:
                after(v, L.s["s"], n)
                nc.vector.tensor_tensor(L.qk, ps, bias("l0_bqk"), ALU.add).then_inc(L.s["qke"].sem, 1)
                return

            def angles(i):
                return trig[:, i * N:(i + 1) * N].unsqueeze(1).broadcast_to([P, 8, N])

            def eight(ap):
                return ap.rearrange("p a (b n) -> p (a b) n", n=N)

            ps2 = psW0[:, :].rearrange("p (a b) -> p a b", b=P)
            ch.link(nc.vector.tensor_tensor(L.rot, ps2, bias("l3_bqkr"), ALU.add))
            ch.link(nc.vector.tensor_tensor(L.rot2, ps, bias("l3_bqk"), ALU.add))
            ch.link(nc.vector.tensor_tensor(eight(L.rot), eight(L.rot), angles(1), ALU.mult))
            ch.link(nc.vector.tensor_tensor(eight(L.rot2), eight(L.rot2), angles(0), ALU.mult))
            after(v, L.s["s"], n)
            nc.vector.tensor_tensor(L.qk, L.rot, L.rot2, ALU.add).then_inc(L.s["qke"].sem, 1)

        def dve_narrow_o(v, ch, L, t):
            after(v, L.s["pv"], t + 1)
            o = psO[:, 0:272].rearrange("p (h d) -> p h d", d=17)
            ch.link(nc.vector.reciprocal(L.rs.unsqueeze(2), o[:, :, 16:17]))
            nc.vector.tensor_tensor(L.o16.rearrange("p (h d) -> p h d", d=16), o[:, :, 0:16],
                                    L.rs.unsqueeze(2).broadcast_to([P, H, 16]), ALU.mult).then_inc(L.s["on"].sem, 1)
            after(v, L.s["xb"], t + 1)
            after(v, L.s["y"], t + 1)
            nc.vector.tensor_tensor(x[:, t, :], x[:, t, :], psO[:, 0:D], ALU.add).then_inc(L.s["xupd"].sem, 1)
            after_all(v, su["table"], [(L.s["xupd"], t + 1)])
            dve_moments(ch, t)

        def dve_l1_qk(v, ch, L, n):
            for i in range(4):
                after(v, L.s[f"sq{i}"], n + 1)
                ins = nc.vector.tensor_reduce(L.ss[:, i, :], L.sq[i % 2], AX.X, ALU.add)
                ins.then_inc(L.s[f"r{i}"].sem, 1)
            after(v, L.s["r3"], n + 1)
            ch.link(nc.vector.tensor_scalar(L.ss, L.ss, 1.0 / 64, None, ALU.mult))
            dve_rsqrt(ch, L.ss, L.ss)
            for i in range(4):
                nc.vector.tensor_tensor(L.qn[i], L.qn[i], L.ss[:, i, :].unsqueeze(2).broadcast_to([P, 8, 64]),
                                        ALU.mult).then_inc(L.s[f"n{i}"].sem, 1)

        def dve_l2_qk(v, ch, L, n):
            after(v, L.s["s"], n)
            for i in (1, 3):
                after(v, L.s[f"i{i}"], n + 1)
                nc.vector.tensor_copy(L.qk[:, 4 * i:4 * i + 4, :], psW0[:, :].rearrange("p (a b) -> p a b", b=P)
                                      ).then_inc(L.s[f"e{i}"].sem, 1)

        def dve_l1_out(v, ch, L, t):
            after(v, L.s["y"], t + 1)
            after(v, L.s["x1t"], t)
            v.wait_ge(st["tab"], t * 32) if not isinstance(t, int) or t > 0 else None
            nc.vector.tensor_tensor(L.x1, x[:, t, :], psP[:, 0:D], ALU.add).then_inc(L.s["xupd"].sem, 1)
            after(v, L.s["lg"], t + 1)
            nc.vector.tensor_copy(gates[:, t, :], psP[:, 0:E8]).then_inc(L.s["gate"].sem, 1)

        def dve_l2_out(v, ch, L, t):
            after(v, L.s["y"], t + 1)
            yT = L.x1T
            ps = psP[:, 0:D].rearrange("p (k n) -> p k n", n=P)
            ch.link(nc.vector.tensor_tensor(yT, ps, c("l2_bout", 0, 2).unsqueeze(2).broadcast_to([P, KC, P]), ALU.add))
            nc.vector.tensor_tensor(four(yT), four(yT), batches(table("gate2"), t), ALU.mult).then_inc(L.s["yt"].sem, 1)
            after(v, L.s["bk"], t + 1)
            nc.vector.tensor_tensor(x[:, t, :], x[:, t, :], psP[:, 512:512 + D], ALU.add).then_inc(L.s["xupd"].sem, 1)
            after_all(v, su["table"], [(L.s["xupd"], t + 1)])
            dve_moments(ch, t)

        def dve_attention(v, ch, L):
            qk = {0: dve_narrow_qk, 1: dve_l1_qk, 2: dve_l2_qk, 3: dve_narrow_qk}[L.li]

            def first():
                ch.reset()
                dve_rstd(ch, rms=L.li == 3)
                dve_norm(v, ch, L, 0)
                dve_modulate(v, ch, L, 0)
                qk(v, ch, L, 0)

            def step(t, more):
                ch.reset()
                if more:
                    dve_norm(v, ch, L, t + 1)
                dve_softmax(v, ch, L, t)
                if more:
                    dve_modulate(v, ch, L, t + 1)
                if L.wide:
                    dve_prob_sums(v, ch, L, t)
                if more:
                    qk(v, ch, L, t + 1)
                if L.li == 1:
                    dve_l1_out(v, ch, L, t)
                elif L.li == 2:
                    dve_l2_out(v, ch, L, t)
                else:
                    dve_narrow_o(v, ch, L, t)

            tiles(v, NT, first, step)

        def act_qk(a, L, n):
            if L.li == 1:
                for i in range(4):
                    after(a, L.s[f"i{i}"], n + 1)
                    after(a, L.s[f"t{i}"], n)
                    ps = (psW0 if i % 2 else psW1)[:, :].rearrange("p (a b) -> p a b", b=64)
                    nc.scalar.activation(L.qn[i], ps, ACT.Copy).then_inc(L.s[f"cp{i}"].sem, 1)
                    after(a, L.s[f"cp{i}"], n + 1)
                    after(a, L.s[f"r{(i + 2) % 4}"], n if i < 2 else n + 1)
                    nc.scalar.activation(L.sq[i % 2], L.qn[i], ACT.Square).then_inc(L.s[f"sq{i}"].sem, 1)
            if L.li == 2:
                for i in (0, 2):
                    after(a, L.s[f"i{i}"], n + 1)
                    if i == 0:
                        after(a, L.s["s"], n)
                    nc.scalar.activation(L.qk[:, 4 * i:4 * i + 4, :], psW1[:, :].rearrange("p (a b) -> p a b", b=P),
                                         ACT.Copy).then_inc(L.s[f"e{i}"].sem, 1)

        def act_l1_turned(a, L, n, i):
            after(a, L.s[f"t{i}"], n + 1)
            if i == 0:
                after(a, L.s["s"], n)
            ps = (psW0 if i % 2 else psW1)[:, :].rearrange("p (a b) -> p a b", b=P)
            g = 2 * (i // 2)
            nc.scalar.activation(L.qk[:, 4 * i:4 * i + 4, :], ps, ACT.Identity, bias=c("l1_qn", g + 1),
                                 scale=c("l1_qn", g)).then_inc(L.s[f"e{i}"].sem, 1)

        def act_v(a, L, n):
            if L.wide:
                after(a, L.s["v0"], n + 1)
                after(a, L.s["pv"], n)
                nc.scalar.activation(L.v[:, 0:512], psO[:, 0:512], ACT.Copy).then_inc(L.s["v0e"].sem, 1)
                after(a, L.s["v1"], n + 1)
                nc.scalar.activation(L.v[:, 512:1024], psO[:, 512:1024], ACT.Copy).then_inc(L.s["v"].sem, 1)
            else:
                after(a, L.s["vp"], n + 1)
                after(a, L.s["pv"], n)
                nc.scalar.activation(L.v[:, :, 0:16], psW1[:, 0:D].rearrange("p (h d) -> p h d", d=16),
                                     ACT.Copy).then_inc(L.s["v"].sem, 1)

        def act_attention(a, L):
            scale = {0: 1.0, 1: 0.125, 2: 0.125, 3: 0.25}[L.li]

            def turned(n):
                if L.li == 1:
                    for i in range(4):
                        act_l1_turned(a, L, n, i)

            def first():
                act_qk(a, L, 0)
                turned(0)
                act_v(a, L, 0)

            def step(t, more):
                after(a, L.s["sub"], t + 1)
                nc.scalar.activation(L.E, L.E, ACT.Exp, scale=scale).then_inc(L.s["exp"].sem, 1)
                if more:
                    act_qk(a, L, t + 1)
                after(a, L.s["ta"], t + 1)
                after(a, L.s["pv"], t)
                psp = psP[:, :].rearrange("p (a b) -> p a b", b=P)
                nc.scalar.activation(L.PT[:, 0:4, :], psp[:, 0:4, :], ACT.Copy).then_inc(L.s["pta"].sem, 1)
                after(a, L.s["tb"], t + 1)
                nc.scalar.activation(L.PT[:, 4:8, :], psp[:, 4:8, :], ACT.Copy).then_inc(L.s["ptb"].sem, 1)
                if L.wide:
                    after(a, L.s["pv"], t + 1)
                    after(a, L.s["y"], t)
                    for b in range(2):
                        ins = nc.scalar.activation(L.oT[:, :, b * N:(b + 1) * N],
                                                   psO[:, b * 512:(b + 1) * 512].rearrange("p (j n) -> p j n", n=N),
                                                   ACT.Copy)
                    ins.then_inc(L.s["ote"].sem, 1)
                if more:
                    turned(t + 1)
                    act_v(a, L, t + 1)
                if not L.wide:
                    after(a, L.s["ot"], t + 1)
                    after(a, L.s["y"], t)
                    for k in range(KC):
                        ins = nc.scalar.activation(L.oT[:, k, :], psO[:, 512 + k * P:512 + (k + 1) * P], ACT.Identity,
                                                   bias=c(f"l{L.li}_bv", k), scale=0.0625 if L.li == 0 else 1.0)
                    ins.then_inc(L.s["ote"].sem, 1)
                if L.li == 1:
                    after(a, L.s["x1t"], t + 1)
                    nc.scalar.activation(L.x1T, psP[:, 512:512 + D].rearrange("p (k n) -> p k n", n=P),
                                         ACT.Copy).then_inc(L.s["x1e"].sem, 1)

            tiles(a, NT, first, step)

        def pool_attention(g, L):
            def masks(n):
                after(g, L.s["qke"], n + 1)
                for i, q in enumerate((L.qe, L.qo)):
                    ins = nc.gpsimd.tensor_tensor(q, L.qk[:, 0:KC, :], par[:, i:i + 1].unsqueeze(2)
                                                  .broadcast_to([P, KC, P]), ALU.mult)
                ins.then_inc(L.s["mask"].sem, 1)

            def first():
                if not L.wide:
                    nc.gpsimd.memset(L.v[:, :, 16:17], 1.0).then_inc(su["ones"], 1)
                    masks(0)

            def step(t, more):
                if L.wide:
                    after(g, L.s["rsum"], t + 1)
                    nc.gpsimd.tensor_tensor(L.E, L.E, L.rs.unsqueeze(2).broadcast_to([P, 16, N]),
                                            ALU.mult).then_inc(L.s["prob"].sem, 1)
                    return
                after(g, L.s["xn"], t + 1)
                nc.gpsimd.tensor_tensor(x[:, t, :], x[:, t, :], bias_row[:, 0 if L.li == 0 else 1, :],
                                        ALU.add).then_inc(L.s["xb"].sem, 1)
                if more:
                    masks(t + 1)

            tiles(g, NT, first, step)

        class FeedForward:

            def __init__(self, kind):
                self.kind = kind
                W = Region(work)
                self.xn = W.take(4, D)
                self.stat = W.take(4, 3)
                self.gT = W.take(KC, 512)
                self.tmp = W.take(512)
                self.hid = W.take(FJ, 512)
                if kind == "moe":
                    self.xg = [W.take(4, ROW) for _ in range(2)]
                    self.y = W.take(4, D)
                    self.wcol = W.take(4)
                    self.b1 = [W.take(FJ) for _ in range(2)]
                    self.b2 = [W.take(D) for _ in range(2)]
                    self.idx = [W.take(4).bitcast(I32) for _ in range(2)]
                    self.w1, self.w2 = fc1, fc2
                elif kind == "l2":
                    self.yT = W.take(KC, 512)
                    self.w1, self.w2 = [l2_w1] * 2, [l2_w2] * 2
                else:
                    self.act = [W.take(512) for _ in range(2)]
                    self.w1, self.w2 = [l3_gate] * 2, [l3_down] * 2
                self.s = signals("f_xn f_a f_h f_y f_done" + {"moe": "", "l2": " f_yt f_bk", "l3": ""}[kind], NG)
                self.s |= signals("f_hd f_he" + (" f_act" if kind == "l3" else ""), NG * FJ)
                if kind == "moe":
                    self.s |= signals("f_sc", NG * 64)
                    self.s |= signals("f_in0 f_in1 f_ga0 f_ga1", NG // 2 * 64)
                    self.s |= signals("f_idx0 f_idx1", NG // 2 * 16)

        class SecondNorm:

            def __init__(self):
                W = Region(work)
                self.xn, self.hT = W.take(4, D), W.take(KC, 512)
                self.s = signals("p_xn p_a p_h p_bk p_x", NG)

        def pe_second_norm(pe, Z):
            def turn(n):
                after(pe, Z.s["p_xn"], n + 1)
                after(pe, Z.s["p_h"], n)
                for k, ps in enumerate((psW0, psW1)):
                    for r in range(4):
                        ins = nc.tensor.transpose(ps[:, r * P:(r + 1) * P], Z.xn[:, r, k * P:(k + 1) * P], ident)
                ins.then_inc(Z.s["p_a"].sem, 1)

            def step(t, more):
                after(pe, Z.s["p_h"], t + 1)
                after(pe, Z.s["p_x"], t)
                for r in range(4):
                    for k in range(KC):
                        ins = nc.tensor.transpose(psP[:, r * D + k * P:r * D + (k + 1) * P],
                                                  Z.hT[:, k, r * P:(r + 1) * P], ident)
                ins.then_inc(Z.s["p_bk"].sem, 1)
                if more:
                    turn(t + 1)

            tiles(pe, NG, lambda: turn(0), step)

        def dve_second_norm(v, ch, Z):
            def norm(n):
                after(v, Z.s["p_a"], n)
                for r in range(4):
                    ins = dve_normalise(Z.xn[:, r, :], x[:, n * 4 + r, :], n * 4 + r)
                    if r < 3:
                        ch.link(ins)
                ins.then_inc(Z.s["p_xn"].sem, 1)

            def first():
                ch.reset()
                dve_rstd(ch)
                norm(0)

            def step(t, more):
                ch.reset()
                after(v, Z.s["p_a"], t + 1)
                after(v, Z.s["p_bk"], t)
                for k, ps in enumerate((psW0, psW1)):
                    def of(name):
                        return table(name)[:, k, bass.ds(t * 8, 8)].unsqueeze(2).broadcast_to([P, 8, N])
                    h8 = Z.hT[:, k, :].rearrange("p (b n) -> p b n", n=N)
                    ch.link(nc.vector.tensor_tensor(h8, ps[:, :].rearrange("p (b n) -> p b n", n=N), of("g0"), ALU.mult))
                    ins = nc.vector.tensor_tensor(h8, h8, of("b0"), ALU.add)
                    if k == 0:
                        ch.link(ins)
                ins.then_inc(Z.s["p_h"].sem, 1)
                if more:
                    norm(t + 1)
                after(v, Z.s["p_bk"], t + 1)
                xs = x[:, bass.ds(t * 4, 4), :]
                nc.vector.tensor_tensor(xs, xs, psP[:, :].rearrange("p (r d) -> p r d", d=D), ALU.add
                                        ).then_inc(Z.s["p_x"].sem, 1)
                after_all(v, su["table"], [(Z.s["p_x"], t + 1)])
                for r in range(4):
                    dve_moments(ch, t * 4 + r)

            tiles(v, NG, first, step)

        HB = [psP[:, 0:512], psP[:, 512:1024], psO[:, 0:512], psO[:, 512:1024]]

        def pe_ff(pe, Q):
            def turn(n):
                after(pe, Q.s["f_xn"], n + 1)
                after(pe, Q.s["f_h"], n)
                for k, ps in enumerate((psW0, psW1)):
                    for r in range(4):
                        ins = nc.tensor.transpose(ps[:, r * P:(r + 1) * P], Q.xn[:, r, k * P:(k + 1) * P], ident)
                ins.then_inc(Q.s["f_a"].sem, 1)

            def hidden(t, u, half):
                after(pe, Q.s["f_h"], t + 1)
                if Q.kind == "moe":
                    after(pe, Q.s[f"f_in{u}"], (half + 1) * 64)
                for j in range(FJ):
                    if Q.kind == "l3":
                        after(pe, Q.s["f_he"], t * FJ + (j - 1))
                        for ps, w in ((HB[j % 2], l3_gate), (HB[2 + j % 2], l3_up)):
                            for k in range(KC):
                                ins = nc.tensor.matmul(ps, w[:, k, j * P:(j + 1) * P], Q.gT[:, k, :],
                                                       start=(k == 0), stop=(k == KC - 1))
                        ins.then_inc(Q.s["f_hd"].sem, 1)
                        continue
                    after(pe, Q.s["f_he"], t * FJ + (j - 3))
                    if Q.kind == "l2" and j == 0:
                        after(pe, Q.s["f_done"], t)
                    for k in range(KC):
                        ins = nc.tensor.matmul(HB[j % 4], Q.w1[u][:, k, j * P:(j + 1) * P], Q.gT[:, k, :],
                                               start=(k == 0), stop=(k == KC - 1))
                    ins.then_inc(Q.s["f_hd"].sem, 1)

            def result(t, u):
                after(pe, Q.s["f_he"], t * FJ + FJ)
                after(pe, Q.s["f_yt" if Q.kind == "l2" else "f_done"], t)
                if Q.kind == "l2":
                    for q in range(KC):
                        for j in range(FJ):
                            ins = nc.tensor.matmul(psS[:, q * 512:(q + 1) * 512], Q.w2[u][:, j, q * P:(q + 1) * P],
                                                   Q.hid[:, j, :], start=(j == 0), stop=(j == FJ - 1))
                    ins.then_inc(Q.s["f_y"].sem, 1)
                    after(pe, Q.s["f_yt"], t + 1)
                    for r in range(4):
                        for k in range(KC):
                            ins = nc.tensor.transpose(psP[:, r * D + k * P:r * D + (k + 1) * P],
                                                      Q.yT[:, k, r * P:(r + 1) * P], ident)
                    ins.then_inc(Q.s["f_bk"].sem, 1)
                    return
                for r in range(4):
                    for j in range(FJ):
                        ins = nc.tensor.matmul(psS[:, r * D:(r + 1) * D], Q.hid[:, j, r * P:(r + 1) * P],
                                               Q.w2[u][:, j, :], start=(j == 0), stop=(j == FJ - 1))
                ins.then_inc(Q.s["f_y"].sem, 1)

            def step(t, u, half, more):
                hidden(t, u, half)
                if more:
                    turn(t + 1)
                result(t, u)

            pairs(pe, NG, lambda: turn(0), step)

        def dve_ff(v, ch, Q):
            def norm(n, u, half):
                if Q.kind == "moe":
                    after_all(v, su["table"], [(Q.s[f"f_ga{u}"], (half + 1) * 64)])
                    for r in range(4):
                        ch.link(nc.vector.bn_stats(stat6[:, r, :], Q.xg[u][:, r, 0:D]))
                        ch.link(nc.vector.bn_aggr(Q.stat[:, r, 0:2], stat6[:, r, :]))
                    dve_rsqrt(ch, Q.stat[:, :, 2], Q.stat[:, :, 1])
                after(v, Q.s["f_a"], n)
                for r in range(4):
                    if Q.kind == "moe":
                        ins = nc.vector.tensor_scalar(Q.xn[:, r, :], Q.xg[u][:, r, 0:D], Q.stat[:, r, 0:1],
                                                      Q.stat[:, r, 2:3], ALU.subtract, ALU.mult)
                    else:
                        ins = dve_normalise(Q.xn[:, r, :], x[:, n * 4 + r, :], n * 4 + r, rms=Q.kind == "l3")
                    if r < 3:
                        ch.link(ins)
                ins.then_inc(Q.s["f_xn"].sem, 1)

            def modulate(n):
                after(v, Q.s["f_a"], n + 1)
                after(v, Q.s["f_hd"], n * FJ)
                for k, ps in enumerate((psW0, psW1)):
                    if Q.kind == "moe":
                        ins = nc.vector.tensor_scalar(Q.gT[:, k, :], ps[:, :], c("l1_mlp", k), c("l1_mlp", 2 + k),
                                                      ALU.mult, ALU.add)
                        if k == 0:
                            ch.link(ins)
                        continue
                    g, b = table("g2f" if Q.kind == "l2" else "g3f"), table("b2f" if Q.kind == "l2" else "b3f")

                    def of(tb):
                        return tb[:, k, bass.ds(n * 8, 8)].unsqueeze(2).broadcast_to([P, 8, N])

                    def eight(ap):
                        return ap.rearrange("p (b n) -> p b n", n=N)

                    ch.link(nc.vector.tensor_tensor(eight(Q.gT[:, k, :]), eight(ps[:, :]), of(g), ALU.mult))
                    ins = nc.vector.tensor_tensor(eight(Q.gT[:, k, :]), eight(Q.gT[:, k, :]), of(b), ALU.add)
                    if k == 0:
                        ch.link(ins)
                ins.then_inc(Q.s["f_h"].sem, 1)

            def products(t):
                for j in range(FJ):
                    after(v, Q.s["f_act"], t * FJ + (j + 1))
                    if j == 0:
                        after(v, Q.s["f_y"], t)
                    nc.vector.tensor_tensor(Q.hid[:, j, :], Q.act[j % 2], HB[2 + j % 2], ALU.mult).then_inc(Q.s["f_he"].sem, 1)

            def result(t, u):
                after(v, Q.s["f_y"], t + 1)
                if Q.kind == "l2":
                    for q in range(KC):
                        gate = table("gate2f")[:, q, bass.ds(t * 8, 8)].unsqueeze(2).broadcast_to([P, 8, N])
                        yT = Q.yT[:, q, :]
                        ch.link(nc.vector.tensor_scalar(yT, psS[:, q * 512:(q + 1) * 512], c("l2_b2", q), None, ALU.add))
                        y3 = yT.rearrange("p (b n) -> p b n", n=N)
                        ins = nc.vector.tensor_tensor(y3, y3, gate, ALU.mult)
                        if q == 0:
                            ch.link(ins)
                    ins.then_inc(Q.s["f_yt"].sem, 1)
                    after(v, Q.s["f_bk"], t + 1)
                    xs = x[:, bass.ds(t * 4, 4), :]
                    nc.vector.tensor_tensor(xs, xs, psP[:, :].rearrange("p (r d) -> p r d", d=D), ALU.add
                                            ).then_inc(Q.s["f_done"].sem, 1)
                    after_all(v, su["table"], [(Q.s["f_done"], t + 1)])
                    for r in range(4):
                        dve_moments(ch, t * 4 + r)
                elif Q.kind == "l3":
                    xs = x[:, bass.ds(t * 4, 4), :]
                    nc.vector.tensor_tensor(xs, xs, psS[:, :].rearrange("p (r d) -> p r d", d=D), ALU.add
                                            ).then_inc(Q.s["f_done"].sem, 1)
                else:
                    ch.link(nc.vector.tensor_copy(Q.wcol.unsqueeze(2), Q.xg[u][:, :, bass.ds(t + D, 1)]))
                    after(v, Q.s["f_sc"], t * 64)
                    ch.link(nc.vector.tensor_tensor(Q.y, psS[:, :].rearrange("p (r d) -> p r d", d=D),
                                                    Q.b2[u].unsqueeze(1).broadcast_to([P, 4, D]), ALU.add))
                    nc.vector.tensor_tensor(Q.y, Q.y, Q.wcol.unsqueeze(2).broadcast_to([P, 4, D]), ALU.mult
                                            ).then_inc(Q.s["f_done"].sem, 1)

            def first():
                ch.reset()
                if Q.kind != "moe":
                    dve_rstd(ch, rms=Q.kind == "l3")
                norm(0, 0, 0)
                modulate(0)

            def step(t, u, half, more):
                ch.reset()
                if more:
                    norm(t + 1, 1 - u, half + u)
                if Q.kind == "l3":
                    products(t)
                if more:
                    modulate(t + 1)
                result(t, u)

            pairs(v, NG, first, step)

        def act_ff(a, Q):
            def step(t, u, half, more):
                if Q.kind == "moe":
                    after(a, Q.s[f"f_in{u}"], (half + 1) * 64)
                for j in range(FJ):
                    after(a, Q.s["f_hd"], t * FJ + (j + 1))
                    if Q.kind == "l3":
                        after(a, Q.s["f_he"], t * FJ + (j - 1))
                        nc.scalar.activation(Q.act[j % 2], HB[j % 2], ACT.Gelu).then_inc(Q.s["f_act"].sem, 1)
                        continue
                    if j == 0:
                        after(a, Q.s["f_y"], t)
                    bias = Q.b1[u][:, j:j + 1] if Q.kind == "moe" else c("l2_b1", j)
                    nc.scalar.activation(Q.hid[:, j, :], HB[j % 4], ACT.Gelu_apprx_tanh if Q.kind == "moe" else ACT.Gelu,
                                         bias=bias).then_inc(Q.s["f_he"].sem, 1)

            pairs(a, NG, lambda: None, step)
        def pool_moe(g, Q):
            def gather(n, u, half):
                after_all(g, su["table"], [(Q.s[f"f_idx{u}"], (half + 1) * 16), (Q.s["f_done"], n - 1)])
                for r in range(4):
                    nc.gpsimd.indirect_dma_start(
                        out=Q.xg[u][:, r, :], out_offset=None, in_=gather_table,
                        in_offset=bass.IndirectOffsetOnAxis(ap=Q.idx[u][:, r:r + 1], axis=0)
                    ).then_inc(Q.s[f"f_ga{u}"].sem, 16)

            def step(t, u, half, more):
                if more:
                    gather(t + 1, 1 - u, half + u)
                after_all(g, su["table"], [(Q.s["f_done"], t + 1), (Q.s["f_sc"], t * 64)])
                for r in range(4):
                    nc.gpsimd.indirect_dma_start(
                        out=moe_sum, out_offset=bass.IndirectOffsetOnAxis(ap=Q.idx[u][:, r:r + 1], axis=0),
                        in_=Q.y[:, r, :], in_offset=None, compute_op=ALU.add
                    ).then_inc(Q.s["f_sc"].sem, 16)

            g.wait_ge(st["gates"], 16)
            pairs(g, NG, lambda: gather(0, 0, 0), step)

        def sp_moe(sp, Q):
            def weights(e, u):
                after(sp, Q.s["f_done"], e - 1)
                sp.dma_start(Q.w1[u], A["l1_fc1"][e].rearrange("(k p) n -> p k n", p=P)).then_inc(Q.s[f"f_in{u}"].sem, 16)
                sp.dma_start(Q.w2[u], A["l1_fc2"][e].rearrange("(k p) n -> p k n", p=P)).then_inc(Q.s[f"f_in{u}"].sem, 16)
                sp.dma_start(Q.b1[u], A["l1_b1"][e]).then_inc(Q.s[f"f_in{u}"].sem, 16)
                sp.dma_start(Q.b2[u], A["l1_b2"][e].broadcast_to([P, D])).then_inc(Q.s[f"f_in{u}"].sem, 16)

            def indices(e, u):
                after(sp, Q.s["f_sc"], (e - 1) * 64)
                sp.dma_start(Q.idx[u], slot_token.rearrange("(e p r) -> e p r", p=P, r=4)[e]
                             ).then_inc(Q.s[f"f_idx{u}"].sem, 16)

            def step(t, u, half, more):
                if more:
                    weights(t + 1, 1 - u)
                    indices(t + 1, 1 - u)

            def first():
                weights(0, 0)
                sp.wait_ge(st["idx"], 16 * E8)
                indices(0, 0)

            pairs(sp, NG, first, step)

        consts = sb("consts", [P, NCONST])
        cc = {n: consts[:, a:a + w] for n, (a, w) in CONSTS.items()}
        ident, trig, lower, iota16, iota32 = cc["ident"], cc["trig"], cc["lower"], cc["iota16"], cc["iota32"]
        ones, par, pidx, tidx = cc["ones"], cc["par"], cc["pidx"], cc["tidx"]
        condT = work[:, 0:KC * B].rearrange("p (k b) -> p k b", b=B)
        silT = work[:, 128:256].rearrange("p (k b) -> p k b", b=B)
        hidT = work[:, 256:512].rearrange("p (k b) -> p k b", b=B)
        mod = work[:, 512:512 + 12 * B].rearrange("p (k b) -> p k b", b=B)

        def pe_setup(pe):
            pe.wait_ge(ld["small"], 48)
            pe.wait_ge(ld["modw"], 80)

            def mm(ps, w, w0, src, n):
                for q in range(n):
                    for k in range(KC):
                        ins = nc.tensor.matmul(ps[:, q * B:(q + 1) * B], w[:, w0 + k, q * P:(q + 1) * P], src[:, k, :],
                                               start=(k == 0), stop=(k == KC - 1))
                return ins

            mm(psS[:, 0:256], m0, 0, condT, 4)
            mm(psW0[:, 0:128], m3a, 0, condT, 2)
            mm(psW0[:, 128:256], m3a, 2, condT, 2).then_inc(su["mm"], 1)
            pe.wait_ge(su["silu"], 1)
            mm(psS[:, 256:384], m1, 0, silT, 2)
            mm(psP[:, 0:512], m2[:, :, 0:1024], 0, silT, 8)
            mm(psP[:, 512:768], m2[:, :, 1024:1536], 0, silT, 4)
            pe.wait_ge(su["hidden"], 1)
            mm(psW1[:, 0:256], m3b, 0, hidT[:, 0:2, :], 4)
            mm(psW1[:, 256:512], m3b, 2, hidT[:, 2:4, :], 4).then_inc(su["mm2"], 1)

        def act_setup(a):
            a.wait_ge(ld["small"], 48)
            nc.scalar.activation(silT, condT, ACT.Silu).then_inc(su["silu"], 1)
            a.wait_ge(su["mm"], 1)
            for i in range(4):
                ins = nc.scalar.activation(hidT[:, i, :], psW0[:, i * B:(i + 1) * B], ACT.Silu, bias=c("l3_tb1", i))
            ins.then_inc(su["hidden"], 1)

        def dve_setup(v, ch):
            v.wait_ge(ld["small"], 48)
            ch.reset()

            def wide(ap):
                return ap.unsqueeze(2).broadcast_to([P, ap.shape[1], B])

            def tt(out, a, b, op=ALU.add):
                ch.link(nc.vector.tensor_tensor(out, a, b, op))

            def psv(ps, lo, n):
                return ps[:, lo * B:(lo + n) * B].rearrange("p (k b) -> p k b", b=B)

            ch.link(nc.vector.tensor_scalar(c("l0_bv", 0, 2), c("l0_bv", 0, 2), 1.0 / 16, None, ALU.mult))
            v.wait_ge(su["mm2"], 1)
            tt(mod[:, 0:4, :], psv(psS, 0, 4), wide(c("l0_bgb", 0, 4)))
            tt(table("g0"), mod[:, 0:2, :], wide(c("l0_g", 0, 2)), ALU.mult)
            tt(mod[:, 4:6, :], mod[:, 0:2, :], wide(c("l0_b", 0, 2)), ALU.mult)
            tt(table("b0"), mod[:, 4:6, :], mod[:, 2:4, :])
            ch.link(nc.vector.tensor_copy(table("g1"), wide(c("l1_g", 0, 2))))
            tt(mod[:, 0:2, :], psv(psS, 4, 2), wide(c("l1_bada", 0, 2)))
            tt(table("b1"), mod[:, 0:2, :], wide(c("l1_b", 0, 2)))
            tt(mod[:, 0:12, :], psv(psP, 0, 12), wide(c("l2_bmod", 0, 12)))
            for i, (b, g, gate) in enumerate((("b2", "g2", "gate2"), ("b2f", "g2f", "gate2f"))):
                ch.link(nc.vector.tensor_copy(table(b), mod[:, 6 * i:6 * i + 2, :]))
                ch.link(nc.vector.tensor_scalar(table(g), mod[:, 6 * i + 2:6 * i + 4, :], 1.0, None, ALU.add))
                ch.link(nc.vector.tensor_copy(table(gate), mod[:, 6 * i + 4:6 * i + 6, :]))
            tt(mod[:, 0:8, :], psv(psW1, 0, 8), wide(c("l3_tb2", 0, 8)))
            for i, (g, b, w) in enumerate((("g3", "b3", "l3_w1"), ("g3f", "b3f", "l3_w2"))):
                ch.link(nc.vector.tensor_scalar(mod[:, 4 * i:4 * i + 2, :], mod[:, 4 * i:4 * i + 2, :], 1.0, None, ALU.add))
                tt(table(g), mod[:, 4 * i:4 * i + 2, :], wide(c(w, 0, 2)), ALU.mult)
                ins = nc.vector.tensor_copy(table(b), mod[:, 4 * i + 2:4 * i + 4, :])
                if i == 0:
                    ch.link(ins)
            ins.then_inc(su["table"], 1)

        def dve_center(v, ch):
            v.wait_ge(ld["l1"], 48)
            ch.reset()
            W = Region(work)
            W.take(9000)
            mean = W.take(32)
            for k in range(KC):
                w = l1_w[:, k, 0:2 * F].rearrange("p (h d) -> p h d", d=64)
                ch.link(nc.vector.tensor_reduce(mean, w, AX.X, ALU.add))
                ch.link(nc.vector.tensor_scalar(mean, mean, 1.0 / 64, None, ALU.mult))
                ins = nc.vector.tensor_tensor(w, w, mean.unsqueeze(2).broadcast_to([P, 32, 64]), ALU.subtract)
                if k == 0:
                    ch.link(ins)
            ins.then_inc(su["center"], 1)

        W = Region(work)
        GE = NT * E8
        cmpT, rank, pre, pre2, sel = (W.take(NT, E8) for _ in range(5))
        cnt, need, eqn = W.take(E8), W.take(E8), W.take(E8)
        gmx = W.take(NT)
        cur, cand, keep, bit = (W.take(E8).bitcast(I32) for _ in range(4))
        bitf = W.take(1)
        ri, ra, rb = (W.take(NT, E8).bitcast(I32) for _ in range(3))
        hotA = W.take(GE * 8).bitcast(BF16).rearrange("p (t e s) -> p t e s", e=E8, s=16)
        hotAp = W.take(GE * 8).bitcast(BF16).rearrange("p (t n) -> p t n", n=P)
        hotAt = W.take(GE * 8).bitcast(BF16).rearrange("p (t n) -> p t n", n=P)
        rt = sems("rt", "shift exp prob cnt tot keep cnt2 tot2 m w hot ix idx")

        def dve_route(v, ch, hotB):
            ch.reset()
            tt = lambda *a: ch.link(nc.vector.tensor_tensor(*a))
            ts = lambda *a: ch.link(nc.vector.tensor_scalar(*a))

            def over_tiles(ap):
                return ap.rearrange("p t e -> p e t")

            def every(ap):
                return ap.unsqueeze(1).broadcast_to([P, NT, E8])

            ch.link(nc.vector.tensor_reduce(gmx, gates[:, :, :], AX.X, ALU.max))
            nc.vector.tensor_tensor(gates[:, :, :], gates[:, :, :], gmx.unsqueeze(2).broadcast_to([P, NT, E8]),
                                    ALU.subtract).then_inc(rt["shift"], 1)
            v.wait_ge(rt["exp"], 1)
            ch.link(nc.vector.tensor_reduce(gmx, gates[:, :, :], AX.X, ALU.add))
            ch.link(nc.vector.reciprocal(gmx, gmx))
            nc.vector.tensor_tensor(gates[:, :, :], gates[:, :, :], gmx.unsqueeze(2).broadcast_to([P, NT, E8]),
                                    ALU.mult).then_inc(rt["prob"], 1)
            v.wait_ge(rt["prob"], 1)
            ch.link(nc.vector.memset(cur, 0))
            ch.link(nc.vector.memset(bit, 1 << 29))
            ch.link(nc.vector.memset(bitf, float(1 << 29)))

            def one_bit(i):
                ch.reset()
                tt(cand, cur, bit, ALU.bitwise_or)
                tt(cmpT, gates[:, :, :], every(cand.bitcast(FP32)), ALU.is_ge)
                nc.vector.tensor_reduce(cnt, over_tiles(cmpT), AX.X, ALU.add).then_inc(rt["cnt"], 1)
                v.wait_ge(rt["tot"], i + 1)
                ts(keep, psW0[:, 0:E8], CAP - 0.5, bitf[:, 0:1], ALU.is_ge, ALU.mult)
                tt(cur, cur, keep, ALU.bitwise_or)
                ts(bit, bit, 1, None, ALU.logical_shift_right)
                nc.vector.tensor_scalar(bitf, bitf, 0.5, None, ALU.mult).then_inc(rt["keep"], 1)
                v.wait_ge(rt["keep"], i + 1)

            with v.Fori(0, 30) as i:
                one_bit(i)
            ch.reset()
            thr = every(cur.bitcast(FP32))
            tt(sel, gates[:, :, :], thr, ALU.is_gt)
            tt(cmpT, gates[:, :, :], thr, ALU.is_equal)
            nc.vector.tensor_reduce(cnt, over_tiles(sel), AX.X, ALU.add).then_inc(rt["cnt2"], 1)

            def ranks(mask, i):
                v.wait_ge(rt["w"], i + 1)
                within = psS[:, 0:GE].rearrange("p (t e) -> p t e", e=E8)
                total = psS[:, 512:512 + GE].rearrange("p (t e) -> p t e", e=E8)
                ch.link(nc.vector.memset(pre[:, 0:1, :], 0.0))
                ch.link(nc.vector.tensor_copy(pre[:, 1:NT, :], total[:, 0:NT - 1, :]))
                src, dst = pre, pre2
                k = 1
                while k < NT:
                    ch.link(nc.vector.tensor_copy(dst[:, 0:k, :], src[:, 0:k, :]))
                    tt(dst[:, k:NT, :], src[:, k:NT, :], src[:, 0:NT - k, :], ALU.add)
                    src, dst, k = dst, src, 2 * k
                tt(rank, within, src, ALU.add)

            v.wait_ge(rt["tot2"], 1)
            nc.vector.tensor_scalar(need, psW0[:, 0:E8], -1.0, float(CAP), ALU.mult, ALU.add).then_inc(rt["m"], 1)
            v.wait_ge(rt["m"], 1)
            ranks(cmpT, 0)
            tt(rank, rank, every(need), ALU.is_lt)
            tt(cmpT, cmpT, rank, ALU.mult)
            nc.vector.tensor_tensor(sel, sel, cmpT, ALU.add).then_inc(rt["m"], 1)
            v.wait_ge(rt["m"], 2)
            ranks(sel, 1)
            ts(rank, rank, 1.0, None, ALU.add)
            tt(rank, rank, sel, ALU.mult)
            ts(ri, rank, -1.0, None, ALU.add)
            ts(ra, ri, 5, None, ALU.arith_shift_right)
            ts(rb, ri, 31, None, ALU.bitwise_and)
            ch.link(nc.vector.tensor_copy(pre, ra))
            ch.link(nc.vector.tensor_copy(pre2, rb))
            flat = lambda ap: ap.rearrange("p t e -> p (t e)")
            tt(hotA.rearrange("p t e s -> p (t e) s"), flat(pre).unsqueeze(2).broadcast_to([P, GE, 16]),
               iota16.unsqueeze(1).broadcast_to([P, GE, 16]), ALU.is_equal)
            tt(hotB.rearrange("p t (e s) -> p (t e) s", s=32), flat(pre2).unsqueeze(2).broadcast_to([P, GE, 32]),
               iota32.unsqueeze(1).broadcast_to([P, GE, 32]), ALU.is_equal)
            hotA3 = hotA.rearrange("p t e s -> p t (e s)")
            ts(hotAp, hotA3, pidx[:, 0:1], None, ALU.mult)
            nc.vector.tensor_tensor(hotAt, hotA3, tidx.unsqueeze(2).broadcast_to([P, NT, P]), ALU.mult
                                    ).then_inc(rt["hot"], 1)
            v.wait_ge(rt["ix"], 1)
            ts(flat(sel), psP[:, 512:512 + GE], 128.0, None, ALU.mult)
            nc.vector.tensor_tensor(flat(ri), flat(sel), psP[:, 0:GE], ALU.add).then_inc(rt["idx"], 1)

        def pe_route(pe, hotB):
            with pe.Fori(0, 30) as i:
                pe.wait_ge(rt["cnt"], i + 1)
                nc.tensor.matmul(psW0[:, 0:E8], ones, cnt, start=True, stop=True).then_inc(rt["tot"], 1)
            pe.wait_ge(rt["cnt2"], 1)
            nc.tensor.matmul(psW0[:, 0:E8], ones, cnt, start=True, stop=True).then_inc(rt["tot2"], 1)
            for i, mask in enumerate((cmpT, sel)):
                pe.wait_ge(rt["m"], i + 1)
                nc.tensor.matmul(psS[:, 0:GE], lower, mask.rearrange("p t e -> p (t e)"), start=True, stop=True)
                nc.tensor.matmul(psS[:, 512:512 + GE], ones, mask.rearrange("p t e -> p (t e)"),
                                 start=True, stop=True).then_inc(rt["w"], 1)
            pe.wait_ge(rt["hot"], 1)
            for lo, hot in ((0, hotAp), (512, hotAt)):
                for t in range(NT):
                    ins = nc.tensor.matmul(psP[:, lo:lo + GE], hot[:, t, :], hotB[:, t, :],
                                           start=(t == 0), stop=(t == NT - 1))
            ins.then_inc(rt["ix"], 1)

        L = [Attention(i) for i in range(4)]
        Z = SecondNorm()
        Q = {k: FeedForward(k) for k in ("moe", "l2", "l3")}
        hotB = r2[:, 4096:4096 + GE * 16].bitcast(BF16).rearrange("p (t n) -> p t n", n=GE)
        assert 4096 + GE * 16 <= 8192

        ENDS = [(Signal(su["table"], 0), 1), (L[0].s["xupd"], NT), (Z.s["p_x"], NG), (L[1].s["gate"], NT), (Signal(rt["idx"], 0), 1),
                (Q["moe"].s["f_done"], NG), (L[2].s["xupd"], NT), (Q["l2"].s["f_done"], NG),
                (L[3].s["xupd"], NT), (Q["l3"].s["f_done"], NG)]

        block = ctx.enter_context(nc.Block())

        def chunked(name):
            return A[name].rearrange("(k p) n -> p k n", p=P)

        def by_tile(ap):
            return ap.rearrange("(t p) d -> p t d", p=P)

        @block.sync
        def _(sp):
            sp.dma_start(consts[:, :], A["consts"]).then_inc(ld["small"], 16)
            sp.dma_start(col[:, :], A["cols"]).then_inc(ld["small"], 16)
            sp.dma_start(condT, chunked("condT")).then_inc(ld["small"], 16)
            for dst, name in ((m0, "l0_mod"), (m1, "l1_mod"), (m2, "l2_mod"), (m3a, "l3_mod1"), (m3b, "l3_mod2")):
                sp.dma_start(dst, chunked(name)).then_inc(ld["modw"], 16)
            for i in range(4):
                sp.dma_start(x[:, 8 * i:8 * i + 8, :], by_tile(A["x"])[:, 8 * i:8 * i + 8, :]).then_inc(ld["x"], 16)
            sp.dma_start(l0_w, chunked("l0_w")).then_inc(ld["l0"], 16)
            sp.dma_start(l0_wp, chunked("l0_wp")).then_inc(ld["l0"], 16)
            for i, name in enumerate(("l0_bp", "l3_bo")):
                sp.dma_start(bias_row[:, i, :], A[name].broadcast_to([P, D])).then_inc(ld["rows"], 16)
            sp.dma_start(l1_w, chunked("l1_w")).then_inc(ld["l1"], 16)
            sp.dma_start(l1_wout, chunked("l1_wout")).then_inc(ld["l1"], 16)
            sp.dma_start(l1_wgate, chunked("l1_wgate")).then_inc(ld["l1"], 16)
            if stage >= 2:
                with sp.Fori(0, NT) as t:
                    after(sp, L[1].s["xupd"], t + 1)
                    sp.dma_start(by_tile(gather_table)[:, t, 0:D], L[1].x1).then_inc(st["tab"], 16)
                    sp.dma_start(by_tile(moe_sum)[:, t, :], L[1].x1).then_inc(st["tab"], 16)
                after(sp, L[1].s["gate"], NT)
                for dst, name in ((l2_w, "l2_w"), (l2_wout, "l2_wout"), (l2_w1, "l2_w1"), (l2_w2, "l2_w2")):
                    sp.dma_start(dst, chunked(name)).then_inc(ld["l2"], 16)
            if stage >= 3:
                sp.wait_ge(rt["prob"], 1)
                sp.dma_start(by_tile(gather_table)[:, :, D:ROW], gates[:, :, :]).then_inc(st["gates"], 16)
                sp.wait_ge(rt["idx"], 1)
                slots = slot_token.rearrange("(e a s) -> e a s", a=16, s=32)
                for e in range(E8):
                    sp.dma_start(slots[e], ri.rearrange("p t e -> p (t e)")[16 * e:16 * e + 16, 32 * e:32 * e + 32]
                                 ).then_inc(st["idx"], 16)
                sp.wait_ge(st["tab"], 32 * NT)
                sp_moe(sp, Q["moe"])
                after(sp, Q["moe"].s["f_sc"], 64 * E8)
            if stage >= 2:
                sp.wait_ge(st["tab"], 32 * NT)
                for i in range(4):
                    sp.dma_start(x[:, 8 * i:8 * i + 8, :], by_tile(moe_sum)[:, 8 * i:8 * i + 8, :]
                                 ).then_inc(ld["back"], 16)
                for dst, name in ((l3_w, "l3_w"), (l3_wo, "l3_wo"), (l3_gate, "l3_gate"), (l3_up, "l3_up"),
                                  (l3_down, "l3_down")):
                    sp.dma_start(dst, chunked(name)).then_inc(ld["l3"], 16)
                sp.wait_ge(ld["back"], 64)
            s, n = ENDS[{1: 2, 2: 3, 3: 5}.get(stage, stage + 1)]
            if stage >= 8:
                for i in range(NG):
                    after(sp, s, i + 1)
                    sp.dma_start(by_tile(out)[:, 4 * i:4 * i + 4, :], x[:, 4 * i:4 * i + 4, :]).then_inc(st["out"], 16)
                sp.wait_ge(st["out"], 16 * NG)
            else:
                after(sp, s, n)
                sp.dma_start(by_tile(out), x[:, :, :]).then_inc(st["out"], 16)
                sp.wait_ge(st["out"], 16)

        def phase(eng, i):
            after(eng, *ENDS[i - 1])

        def phase_from_memory(eng, i):
            phase(eng, i)
            eng.wait_ge(ld["back"], 64)

        @block.tensor
        def _(pe):
            pe_setup(pe)
            phase(pe, 1)
            pe_attention(pe, L[0])
            phase(pe, 2)
            pe_second_norm(pe, Z)
            if stage >= 2:
                phase(pe, 3)
                pe_attention(pe, L[1])
            if stage >= 3:
                phase(pe, 4)
                pe_route(pe, hotB)
                phase(pe, 5)
                pe_ff(pe, Q["moe"])
            if stage >= 5:
                phase(pe, 6)
                pe_attention(pe, L[2])
            if stage >= 6:
                phase(pe, 7)
                pe_ff(pe, Q["l2"])
            if stage >= 7:
                phase(pe, 8)
                pe_attention(pe, L[3])
            if stage >= 8:
                phase(pe, 9)
                pe_ff(pe, Q["l3"])

        @block.vector
        def _(v):
            ch = Chain(v, chain_dve)
            dve_setup(v, ch)
            v.wait_ge(ld["x"], 64)
            v.wait_ge(su["table"], 1)
            ch.reset()
            for i in range(NT):
                dve_moments(ch, i)
            dve_attention(v, ch, L[0])
            phase(v, 2)
            dve_second_norm(v, ch, Z)
            if stage >= 2:
                phase(v, 3)
                dve_center(v, ch)
                dve_attention(v, ch, L[1])
            if stage >= 3:
                phase(v, 4)
                v.wait_ge(st["tab"], 32 * NT)
                dve_route(v, ch, hotB)
                phase(v, 5)
                v.wait_ge(st["idx"], 16 * E8)
                dve_ff(v, ch, Q["moe"])
            if stage >= 5:
                phase_from_memory(v, 6)
                ch.reset()
                for i in range(NT):
                    dve_moments(ch, i)
                v.wait_ge(chain_dve, ch.n)
                dve_attention(v, ch, L[2])
            if stage >= 6:
                phase(v, 7)
                dve_ff(v, ch, Q["l2"])
            if stage >= 7:
                phase(v, 8)
                dve_attention(v, ch, L[3])
            if stage >= 8:
                phase(v, 9)
                dve_ff(v, ch, Q["l3"])

        @block.scalar
        def _(a):
            act_setup(a)
            phase(a, 1)
            act_attention(a, L[0])
            if stage >= 2:
                phase(a, 3)
                act_attention(a, L[1])
            if stage >= 3:
                a.wait_ge(rt["shift"], 1)
                nc.scalar.activation(gates[:, :, :], gates[:, :, :], ACT.Exp).then_inc(rt["exp"], 1)
                phase(a, 5)
                act_ff(a, Q["moe"])
            if stage >= 5:
                phase(a, 6)
                act_attention(a, L[2])
            if stage >= 6:
                phase(a, 7)
                act_ff(a, Q["l2"])
            if stage >= 7:
                phase(a, 8)
                act_attention(a, L[3])
            if stage >= 8:
                phase(a, 9)
                act_ff(a, Q["l3"])

        @block.gpsimd
        def _(g):
            g.wait_ge(ld["small"], 48)
            g.wait_ge(ld["rows"], 32)
            phase(g, 1)
            pool_attention(g, L[0])
            if stage >= 2:
                phase(g, 3)
                pool_attention(g, L[1])
            if stage >= 3:
                phase(g, 5)
                pool_moe(g, Q["moe"])
            if stage >= 5:
                phase(g, 6)
                pool_attention(g, L[2])
            if stage >= 7:
                phase(g, 8)
                pool_attention(g, L[3])


def host_arrays(I):
    a = {k: np.asarray(v) for k, v in I.items()}
    l0 = lambda n: a["L0_cond_" + n]
    l1 = lambda n: a["L1_cond_" + n]
    l2 = lambda n: a["L2_cond_" + n]
    l3 = lambda n: a["L3_cond_" + n]
    cat = np.concatenate
    wqkv = l0("Wqkv").reshape(H, 16, 3, D).transpose(2, 0, 1, 3).reshape(3 * D, D)
    bqkv = l0("bqkv").reshape(H, 16, 3).transpose(2, 0, 1).reshape(3, D)

    def rotated(w):
        return np.roll(w.reshape(w.shape[:-1] + (H, 16)), 8, axis=-1).reshape(w.shape)

    twice = lambda w: cat([w, w])
    vectors = {
        "l0_g": l0("ln_g"), "l0_b": l0("ln_b"), "l0_bgb": cat([l0("bg"), l0("bb")]),
        "l0_bqk": cat([bqkv[0], bqkv[1]]), "l0_bv": bqkv[2],
        "l1_bada": l1("b_ada"), "l1_g": l1("ln1_g"), "l1_b": l1("ln1_b"),
        "l1_qn": cat([twice(l1(n)) for n in ("qn_g", "qn_b", "kn_g", "kn_b")]),
        "l1_mlp": cat([l1("mlp_g"), l1("mlp_b")]),
        "l2_bmod": l2("b_mod"), "l2_bout": l2("b_out"), "l2_b1": l2("b1"), "l2_b2": l2("b2"),
        "l3_w1": l3("w_norm1"), "l3_w2": l3("w_norm2"), "l3_tb1": cat([l3("t1_b1"), l3("t2_b1")]),
        "l3_tb2": cat([l3("t1_b2"), l3("t2_b2")]), "l3_bqk": cat([l3("bq"), l3("bk")]),
        "l3_bqkr": cat([rotated(l3("bq")), rotated(l3("bk"))]), "l3_bv": l3("bv")}
    cols = cat([vectors[n].reshape(k, P).T for n, (_, k) in COLS.items()], axis=1)
    assert cols.shape == (P, NCOL)
    f32 = np.float32
    inv = (f32(1.0) / f32(10000.0) ** (np.arange(0, 16, 2, dtype=f32) / f32(16))).astype(f32)
    angle = (inv[:, None] * np.arange(N, dtype=f32)[None, :]).astype(f32)
    cos = np.tile(cat([np.cos(angle), np.cos(angle)]), (8, 1))
    sin = np.tile(cat([-np.sin(angle), np.sin(angle)]), (8, 1))
    parity = (np.arange(P) // 16) % 2
    blocks = {"ident": np.eye(P), "ones": np.ones((P, P)), "lower": np.triu(np.ones((P, P)), 1),
              "trig": cat([cos, sin], axis=1), "par": np.stack([1 - parity, parity], axis=1),
              "iota16": np.tile(np.arange(16), (P, 1)), "iota32": np.tile(np.arange(32), (P, 1)),
              "pidx": np.arange(P)[:, None], "tidx": np.tile(np.arange(NT), (P, 1))}
    consts = cat([blocks[n].astype(f32) for n in CONSTS], axis=1)
    arrays = {
        "x": a["x"].reshape(T, D), "condT": a["cond_1024"].T, "cols": cols, "consts": consts,
        "l0_mod": cat([l0("Wg").T, l0("Wb").T], axis=1), "l0_w": wqkv.T, "l0_wp": l0("Wp").T,
        "l0_bp": l0("bp")[None, :],
        "l1_mod": l1("W_ada").T, "l1_w": l1("Wqkv").T, "l1_wout": l1("Wout").T, "l1_wgate": l1("Wgate").T,
        "l1_fc1": l1("fc1s").transpose(0, 2, 1), "l1_fc2": l1("fc2s").transpose(0, 2, 1),
        "l1_b1": l1("b1s").reshape(E8, FJ, P).transpose(0, 2, 1), "l1_b2": l1("b2s")[:, None, :],
        "l2_mod": l2("W_mod"), "l2_w": l2("W_qkv"), "l2_wout": l2("W_out"), "l2_w1": l2("W1"), "l2_w2": l2("W2"),
        "l3_mod1": cat([l3("t1_w1"), l3("t2_w1")]), "l3_mod2": cat([l3("t1_w2"), l3("t2_w2")]),
        "l3_w": cat([l3("wq"), l3("wk"), rotated(l3("wq")), rotated(l3("wk")), l3("wv")], axis=1),
        "l3_wo": l3("wo"), "l3_bo": l3("bo")[None, :],
        "l3_gate": l3("w_gate"), "l3_up": l3("w_up"), "l3_down": l3("w_down")}
    return {k: np.ascontiguousarray(v) for k, v in arrays.items()}


def kernel(**inputs):
    import concourse.bacc as bacc
    from concourse.bass_utils import run_bass_kernel_spmd

    nc = bacc.Bacc("TRN2", target_bir_lowering=False, num_devices=1)
    arrays = host_arrays(inputs)
    A = {k: nc.dram_tensor("in_" + k, v.shape, FP32, kind="ExternalInput").ap() for k, v in arrays.items()}
    out = nc.dram_tensor("out", (T, D), FP32, kind="ExternalOutput").ap()
    build_program(nc, A, out)
    r = run_bass_kernel_spmd(nc, [{"in_" + k: v for k, v in arrays.items()}], core_ids=[0])
    return r.results[0]["out"].reshape(B, N, D)
```

```python
import numpy as np
from contextlib import ExitStack
from math import prod

import concourse.bass as bass
from concourse import mybir

FP32 = mybir.dt.float32
BF16 = mybir.dt.bfloat16
I32 = mybir.dt.int32
ALU = mybir.AluOpType
ACT = mybir.ActivationFunctionType
AX = mybir.AxisListType

P = 128
B, N, D = 64, 64, 256
T = B * N
NT = T // P
KC = D // P
H = 16
HJ = H // 2
F = 1024
FJ = F // P
E8 = 8
CAP = T // E8
NG = T // 512
ROW = D + E8
EPS = 1e-5

COLS = {}
_at = 0
for _name, _n in [("l0_g", 2), ("l0_b", 2), ("l0_bgb", 4), ("l0_bqk", 4), ("l0_bv", 2),
                  ("l1_bada", 2), ("l1_g", 2), ("l1_b", 2), ("l1_qn", 4), ("l1_mlp", 4),
                  ("l2_bmod", 12), ("l2_bout", 2), ("l2_b1", 8), ("l2_b2", 2),
                  ("l3_w1", 2), ("l3_w2", 2), ("l3_tb1", 4), ("l3_tb2", 8),
                  ("l3_bqk", 4), ("l3_bqkr", 4), ("l3_bv", 2)]:
    COLS[_name] = (_at, _n)
    _at += _n
NCOL = _at

TABS = ["g0", "b0", "g1", "b1", "g2", "b2", "gate2", "g2f", "b2f", "gate2f", "g3", "b3", "g3f", "b3f"]
LAST_STAGE = 8

CONSTS = {}
_at = 0
for _name, _n in [("ident", P), ("ones", P), ("lower", P), ("trig", 2 * N), ("par", 2), ("iota16", 16),
                  ("iota32", 32), ("pidx", 1), ("tidx", NT)]:
    CONSTS[_name] = (_at, _n)
    _at += _n
NCONST = _at


class Chain:

    def __init__(self, eng, sem):
        self.eng, self.sem, self.n = eng, sem, 0

    def reset(self):
        self.eng.sem_clear(self.sem)
        self.n = 0

    def link(self, ins):
        self.n += 1
        ins.then_inc(self.sem, 1)
        self.eng.wait_ge(self.sem, self.n)


class Signal:

    def __init__(self, sem, base):
        self.sem, self.base = sem, base


def after(eng, signal, count):
    if isinstance(count, int) and count <= 0:
        return
    eng.wait_ge(signal.sem, count + signal.base)


def after_all(eng, done, waits):
    values = []
    for signal, count in waits:
        if isinstance(count, int):
            if count > 0:
                values.append((signal, count + signal.base))
        else:
            values.append((signal, eng.to_reg(count + signal.base)))
    eng.wait_ge(done, 1)
    for signal, value in values:
        eng.wait_ge(signal.sem, value)


def tiles(eng, count, first, step, last=None):
    first()
    step(0, 2, False)
    with eng.Fori(1, count - 2) as t:
        step(t, 2, True)
    step(count - 2, 1, True)
    step(count - 1, 0, True)
    if last:
        last()


def pairs(eng, count, first, step):
    first()
    step(0, 0, 0, True)
    with eng.Fori(0, (count - 2) // 2) as i:
        step(i * 2 + 1, 1, i, True)
        step(i * 2 + 2, 0, i + 1, True)
    step(count - 1, (count - 1) % 2, (count - 1) // 2, False)


def build_program(nc, A, out, stage=LAST_STAGE):
    ctx = ExitStack()
    with ctx:
        def sb(name, shape, dt=FP32):
            return ctx.enter_context(nc.sbuf_tensor(name, shape, dt))

        def sem(name):
            return ctx.enter_context(nc.semaphore(name))

        def sems(prefix, names):
            return {n: sem(f"{prefix}_{n}") for n in names.split()}

        shared = {}

        def signals(names, total):
            out = {}
            for n in names.split():
                if n not in shared:
                    shared[n] = [sem(n), 0]
                out[n] = Signal(*shared[n])
                shared[n][1] += total
            return out

        x = sb("x", [P, NT, D])
        col = sb("col", [P, NCOL])
        tab = sb("tab", [P, len(TABS), KC, B])
        gates = sb("gates", [P, NT, E8])
        moments = sb("moments", [P, NT, 2])
        rstd = sb("rstd", [P, NT])
        stat6 = sb("stat6", [P, 4, 6])
        mv = sb("mv", [P, 4, 2])
        newton = sb("newton", [P, 4, NT])
        bias_row = sb("bias_row", [P, 2, D])
        r1 = sb("r1", [P, 12288])
        r2 = sb("r2", [P, 9216])
        work = sb("work", [P, 11264])

        def c(name, i=0, n=1):
            at, _ = COLS[name]
            return col[:, at + i:at + i + n]

        def table(name):
            return tab[:, TABS.index(name), :, :]

        class Region:

            def __init__(self, region):
                self.region, self.at = region, 0

            def take(self, *shape):
                n = prod(shape)
                ap = self.region[:, self.at:self.at + n]
                self.at += n
                assert self.at <= self.region.shape[1], self.at
                if len(shape) == 2:
                    ap = ap.rearrange("p (a b) -> p a b", b=shape[1])
                if len(shape) == 3:
                    ap = ap.rearrange("p (a b c) -> p a b c", b=shape[1], c=shape[2])
                return ap

        R = Region(r1)
        l0_w, l0_wp = R.take(KC, 768), R.take(KC, D)
        l1_w, l1_wout, l1_wgate = R.take(KC, 3 * F), R.take(FJ, D), R.take(KC, E8)
        R = Region(r1)
        l2_w, l2_wout, l2_w1, l2_w2 = R.take(KC, 3 * F), R.take(FJ, D), R.take(KC, F), R.take(FJ, D)
        R = Region(r2)
        m0, m1, m2 = R.take(KC, 512), R.take(KC, D), R.take(KC, 1536)
        m3a, m3b = R.take(2 * KC, D), R.take(2 * KC, 512)
        R = Region(r2)
        fc1 = [R.take(KC, F) for _ in range(2)]
        fc2 = [R.take(FJ, D) for _ in range(2)]
        R = Region(r2)
        l3_w, l3_wo = R.take(KC, 1280), R.take(KC, D)
        l3_gate, l3_up, l3_down = R.take(KC, F), R.take(KC, F), R.take(FJ, D)

        def pb(name, banks):
            return ctx.enter_context(nc.psum_tensor(name, [P, 512 * banks], FP32))

        psS, psP, psO, psW0, psW1 = pb("psS", 2), pb("psP", 2), pb("psO", 2), pb("psW0", 1), pb("psW1", 1)

        gather_table = nc.dram_tensor("gather_table", [T, ROW], FP32, kind="Internal").ap()
        moe_sum = nc.dram_tensor("moe_sum", [T, D], FP32, kind="Internal").ap()
        slot_token = nc.dram_tensor("slot_token", [E8 * CAP], I32, kind="Internal").ap()

        ld = sems("ld", "small modw x l0 l1 l2 l3 back rows")
        st = sems("st", "out tab gates idx")
        chain_dve = sem("chain_dve")
        su = sems("su", "mm silu table hidden mm2 ones center")

        class Attention:

            def __init__(self, li):
                self.li = li
                self.wide = li in (1, 2)
                W = Region(work)
                self.xn = W.take(D)
                self.hT = W.take(KC, P)
                self.tmpT = W.take(KC, P)
                self.qk = W.take(16, P) if self.wide else W.take(4, P)
                self.v = W.take(F) if self.wide else W.take(H, 17)
                self.E = W.take(16, N)
                self.PT = W.take(HJ, P)
                self.mx = W.take(16)
                self.rs = W.take(16)
                self.oT = W.take(FJ, P) if self.wide else W.take(KC, P)
                if li == 1:
                    self.sq = [W.take(8, 64) for _ in range(2)]
                    self.qn = [W.take(8, 64) for _ in range(4)]
                    self.ss = W.take(4, 8)
                if self.wide:
                    self.x1 = W.take(D)
                    self.x1T = W.take(KC, P)
                else:
                    self.qe, self.qo = W.take(KC, P), W.take(KC, P)
                    self.o16 = W.take(D)
                    self.rot = W.take(4, P)
                    self.rot2 = W.take(4, P)
                self.g, self.b = table(f"g{li}"), table(f"b{li}")
                self.s = signals("xn a h s0 s1 sub0 sub1 exp0 exp1 ta tb pta ptb pv ote y xupd v"
                              + {0: " qk qke mask hr0 hr1 vp on ot xb",
                                 1: " prob0 prob1 rsum0 rsum1 i0 i1 i2 i3 cp0 cp1 cp2 cp3 sq0 sq1 sq2 sq3"
                                    " r0 r1 r2 r3 n0 n1 n2 n3 t0 t1 t2 t3 e0 e1 e2 e3 v0 v1 v0e x1t x1e lg gate",
                                 2: " prob0 prob1 rsum0 rsum1 i0 i1 i2 i3 e0 e1 e2 e3 v0 v1 v0e yt bk",
                                 3: " qk qke mask hr0 hr1 vp on ot xb"}[li], NT)
                self.loads = {0: 2, 1: 3, 2: 4, 3: 5}[li]
                self.ready = {0: ld["l0"], 1: ld["l1"], 2: ld["l2"], 3: ld["l3"]}[li]

        def pe_transpose_x(pe, L, n):
            after(pe, L.s["xn"], n + 1)
            if L.wide:
                after(pe, L.s["v"], n)
            else:
                after(pe, L.s["qke"], n)
            for k in range(KC):
                ins = nc.tensor.transpose(psW0[:, k * P:(k + 1) * P], L.xn[:, k * P:(k + 1) * P], ident)
            ins.then_inc(L.s["a"].sem, 1)

        def pe_project(L, ps, w, lo, chunks):
            for q in range(chunks):
                for k in range(KC):
                    ins = nc.tensor.matmul(ps[:, q * P:(q + 1) * P], w[:, k, lo + q * P:lo + (q + 1) * P],
                                           L.hT[:, k, :], start=(k == 0), stop=(k == KC - 1))
            return ins

        def pe_project_tokens(L, ps, w, lo, width):
            for k in range(KC):
                ins = nc.tensor.matmul(ps[:, 0:width], L.hT[:, k, :], w[:, k, lo:lo + width],
                                       start=(k == 0), stop=(k == KC - 1))
            return ins

        def pe_narrow_qk(pe, L, n):
            after(pe, L.s["h"], n + 1)
            after(pe, L.s["v"], n)
            if L.li == 0:
                pe_project(L, psW1, l0_w, 0, 4).then_inc(L.s["qk"].sem, 1)
            else:
                pe_project(L, psW1, l3_w, 0, 4)
                pe_project(L, psW0, l3_w, 512, 4).then_inc(L.s["qk"].sem, 1)

        def pe_narrow_v(pe, L, n):
            after(pe, L.s["qke"], n + 1)
            w, lo = (l0_w, 512) if L.li == 0 else (l3_w, 1024)
            pe_project_tokens(L, psW1, w, lo, D).then_inc(L.s["vp"].sem, 1)

        def pe_l1_qk(pe, L, n, between=None):
            after(pe, L.s["h"], n + 1)
            after(pe, L.s["v0e"], n)
            for i in range(4):
                if i == 2 and between:
                    between()
                if i >= 2:
                    after(pe, L.s[f"cp{i - 2}"], n + 1)
                pe_project_tokens(L, (psW0 if i % 2 else psW1)[:, :], l1_w, 512 * i, 512).then_inc(L.s[f"i{i}"].sem, 1)

        def pe_l1_turn(pe, L, n):
            after(pe, L.s["ote"], n)
            for i in range(4):
                after(pe, L.s[f"n{i}"], n + 1)
                if i >= 2:
                    after(pe, L.s[f"e{i - 2}"], n + 1)
                at = i % 2 * 512
                for j in range(4):
                    ins = nc.tensor.transpose(psO[:, at + j * P:at + (j + 1) * P], L.qn[i][:, 2 * j:2 * j + 2, :],
                                              ident)
                ins.then_inc(L.s[f"t{i}"].sem, 1)

        def pe_l2_qk(pe, L, n, between=None):
            after(pe, L.s["h"], n + 1)
            after(pe, L.s["v0e"], n)
            pe_project(L, psW1, l2_w, 0, 4).then_inc(L.s["i0"].sem, 1)
            pe_project(L, psW0, l2_w, 512, 4).then_inc(L.s["i1"].sem, 1)
            after(pe, L.s["e0"], n + 1)
            pe_project(L, psW1, l2_w, 1024, 4).then_inc(L.s["i2"].sem, 1)
            after(pe, L.s["e1"], n + 1)
            pe_project(L, psW0, l2_w, 1536, 4).then_inc(L.s["i3"].sem, 1)

        def pe_wide_v(pe, L, n):
            w, k_out = (l1_w, "cp") if L.li == 1 else (l2_w, "e")
            for i, ps in enumerate((psW1, psW0)):
                after(pe, L.s[f"{k_out}{i + 2}"], n + 1)
                pe_project_tokens(L, ps, w, 2048 + 512 * i, 512).then_inc(L.s[f"v{i}"].sem, 1)

        def pe_scores(pe, L, t):
            ready = {0: ("mask",), 1: ("e3",), 2: ("e2", "e3"), 3: ("mask",)}[L.li]
            after_all(pe, su["table"], [(L.s[r], t + 1) for r in ready] + [(L.s["sub1"], t)])
            if L.wide:
                for j in range(HJ):
                    for b in range(2):
                        for hp in range(2):
                            rows = slice(64 * hp, 64 * hp + 64)
                            ins = nc.tensor.matmul(psS[rows, (2 * j + b) * N:(2 * j + b + 1) * N],
                                                   L.qk[rows, j, b * N:(b + 1) * N],
                                                   L.qk[rows, HJ + j, b * N:(b + 1) * N], start=True, stop=True)
                    if j % 4 == 3:
                        ins.then_inc(L.s[f"s{j // 4}"].sem, 1)
                return
            for r in range(4):
                if r >= 2:
                    after_all(pe, su["table"], [(L.s[f"hr{r - 2}"], t + 1)])
                rows = slice(32 * r, 32 * r + 32)
                for ch in range(KC):
                    for b in range(2):
                        at = narrow_block(r, ch, b) * N
                        for hp, q in enumerate((L.qe, L.qo)):
                            ins = nc.tensor.matmul(psS[64 * hp:64 * hp + 64, at:at + N], q[rows, ch, b * N:(b + 1) * N],
                                                   L.qk[rows, KC + ch, b * N:(b + 1) * N], start=True, stop=True)
                ins.then_inc(L.s[f"hr{r}" if r < 2 else f"s{r - 2}"].sem, 1)

        def narrow_block(r, ch, b):
            return (((r % 2) * 2 + r // 2) * 2 + ch) * 2 + b

        def narrow_pair(j):
            rp, rh, ch = j // 4, (j // 2) % 2, j % 2
            return 8 * ch + 2 * (2 * rh + rp)

        def pe_transpose_probs(pe, L, t):
            after(pe, L.s[{0: "ptb", 1: "gate", 2: "xupd", 3: "ptb"}[L.li]], t)
            for j in range(HJ):
                if j % 4 == 0:
                    after(pe, L.s[("prob" if L.wide else "exp") + str(j // 4)], t + 1)
                ins = nc.tensor.transpose(psP[:, j * P:(j + 1) * P], L.E[:, 2 * j:2 * j + 2, :], ident)
                if j == 3:
                    ins.then_inc(L.s["ta"].sem, 1)
            ins.then_inc(L.s["tb"].sem, 1)

        def pe_narrow_pv(pe, L, t):
            after_all(pe, su["table"], [(L.s["v"], t + 1), (L.s["on"], t), (L.s["pta"], t + 1)])
            for j in range(HJ):
                if j == 4:
                    after_all(pe, su["table"], [(L.s["ptb"], t + 1)])
                for hp in range(2):
                    for b in range(2):
                        rows = slice(64 * b, 64 * b + 64)
                        h = narrow_pair(j) + hp
                        ins = nc.tensor.matmul(psO[rows, h * 17:(h + 1) * 17], L.PT[rows, j, 64 * hp:64 * hp + 64],
                                               L.v[rows, h, :], start=True, stop=True)
            ins.then_inc(L.s["pv"].sem, 1)

        def pe_wide_pv(pe, L, t):
            after_all(pe, su["table"], [(L.s["v"], t + 1), (L.s["pta"], t + 1)])
            for j in range(HJ):
                if j == 4:
                    after_all(pe, su["table"], [(L.s["ptb"], t + 1)])
                for b in range(2):
                    rows = slice(64 * b, 64 * b + 64)
                    for hp in range(2):
                        h = 2 * j + hp
                        ins = nc.tensor.matmul(psO[64 * hp:64 * hp + 64, b * 512 + j * N:b * 512 + (j + 1) * N],
                                               L.v[rows, h * 64:(h + 1) * 64], L.PT[rows, j, 64 * hp:64 * hp + 64],
                                               start=True, stop=True)
            ins.then_inc(L.s["pv"].sem, 1)

        def pe_turn_out(pe, L, t):
            if L.wide:
                after(pe, L.s["xupd" if L.li == 1 else "yt"], t + 1)
                for k in range(KC):
                    ins = nc.tensor.transpose(psP[:, 512 + k * P:512 + (k + 1) * P],
                                              L.x1[:, k * P:(k + 1) * P] if L.li == 1 else L.x1T[:, k, :], ident)
                ins.then_inc(L.s["x1t" if L.li == 1 else "bk"].sem, 1)
                return
            after(pe, L.s["xupd"], t)
            after(pe, L.s["on"], t + 1)
            for k in range(KC):
                ins = nc.tensor.transpose(psO[:, 512 + k * P:512 + (k + 1) * P], L.o16[:, k * P:(k + 1) * P],
                                          ident)
            ins.then_inc(L.s["ot"].sem, 1)

        def pe_narrow_y(pe, L, t):
            w = l0_wp if L.li == 0 else l3_wo
            after(pe, L.s["ote"], t + 1)
            for k in range(KC):
                ins = nc.tensor.matmul(psO[:, 512:512 + D], L.oT[:, k, :], w[:, k, :], start=(k == 0), stop=(k == KC - 1))
            ins.then_inc(L.s["y"].sem, 1)

        def pe_wide_y(pe, L, t):
            after(pe, L.s["ote"], t + 1)
            if L.li == 1:
                for j in range(FJ):
                    ins = nc.tensor.matmul(psP[:, 0:D], L.oT[:, j, :], l1_wout[:, j, :], start=(j == 0), stop=(j == FJ - 1))
            else:
                for q in range(KC):
                    for j in range(FJ):
                        ins = nc.tensor.matmul(psP[:, q * P:(q + 1) * P], l2_wout[:, j, q * P:(q + 1) * P], L.oT[:, j, :],
                                               start=(j == 0), stop=(j == FJ - 1))
            ins.then_inc(L.s["y"].sem, 1)

        def pe_l1_logits(pe, L, t):
            after(pe, L.s["x1e"], t + 1)
            for k in range(KC):
                ins = nc.tensor.matmul(psP[:, 0:E8], L.x1T[:, k, :], l1_wgate[:, k, :], start=(k == 0), stop=(k == KC - 1))
            ins.then_inc(L.s["lg"].sem, 1)

        def pe_attention(pe, L):
            pe.wait_ge(L.ready, 16 * L.loads)
            if not L.wide:
                pe.wait_ge(su["ones"], 1 if L.li == 0 else 2)
            if L.li == 1:
                pe.wait_ge(su["center"], 1)

            def wide_qkv(n, logits):
                (pe_l1_qk if L.li == 1 else pe_l2_qk)(pe, L, n, logits)

            def first():
                pe_transpose_x(pe, L, 0)
                if L.wide:
                    wide_qkv(0, None)
                    pe_wide_v(pe, L, 0)
                    if L.li == 1:
                        pe_l1_turn(pe, L, 0)
                else:
                    pe_narrow_qk(pe, L, 0)
                    pe_narrow_v(pe, L, 0)

            def step(t, ahead, behind):
                def logits():
                    if L.li == 1 and behind:
                        pe_l1_logits(pe, L, t - 1)

                if ahead:
                    pe_transpose_x(pe, L, t + 1)
                pe_scores(pe, L, t)
                if behind:
                    pe_turn_out(pe, L, t - 1)
                if L.wide and ahead:
                    wide_qkv(t + 1, logits)
                elif L.wide:
                    logits()
                elif ahead:
                    pe_narrow_qk(pe, L, t + 1)
                if behind and not L.wide:
                    pe_narrow_y(pe, L, t - 1)
                pe_transpose_probs(pe, L, t)
                if L.wide:
                    pe_wide_pv(pe, L, t)
                    if ahead:
                        pe_wide_v(pe, L, t + 1)
                        if L.li == 1:
                            pe_l1_turn(pe, L, t + 1)
                    pe_wide_y(pe, L, t)
                else:
                    pe_narrow_pv(pe, L, t)
                    if ahead:
                        pe_narrow_v(pe, L, t + 1)

            def last():
                pe_turn_out(pe, L, NT - 1)
                if L.li == 1:
                    pe_l1_logits(pe, L, NT - 1)
                if not L.wide:
                    pe_narrow_y(pe, L, NT - 1)

            tiles(pe, NT, first, step, last)

        def batches(ap, n, count=2):
            return ap[:, :, bass.ds(n * count, count)].unsqueeze(3).broadcast_to([P, KC, count, N])

        def four(ap):
            return ap.rearrange("p k (b n) -> p k b n", n=N)

        def dve_rsqrt(ch, out, var):
            shape = var.shape
            n = prod(shape[1:])
            v, y, q, g = (newton[:, i, 0:n] for i in range(4))
            if len(shape) == 3:
                v3, o3 = v.rearrange("p (a b) -> p a b", b=shape[2]), y.rearrange("p (a b) -> p a b", b=shape[2])
            else:
                v3, o3 = v, y
            ch.link(nc.vector.tensor_scalar(v3, var, EPS, None, ALU.add))
            ch.link(nc.vector.tensor_scalar(g.bitcast(I32), v.bitcast(I32), 1, None, ALU.logical_shift_right))
            ch.link(nc.vector.tensor_scalar(y.bitcast(I32), g.bitcast(I32), -1.0, float(0x5F3759DF), ALU.mult, ALU.add))
            for i in range(3):
                ch.link(nc.vector.tensor_tensor(q, y, y, ALU.mult))
                ch.link(nc.vector.tensor_tensor(q, q, v, ALU.mult))
                ch.link(nc.vector.tensor_scalar(q, q, -0.5, 1.5, ALU.mult, ALU.add))
                if i < 2:
                    ch.link(nc.vector.tensor_tensor(y, y, q, ALU.mult))
            ch.link(nc.vector.tensor_tensor(out, o3, q.rearrange("p (a b) -> p a b", b=shape[2])
                                            if len(shape) == 3 else q, ALU.mult))

        def dve_moments(ch, t):
            ch.link(nc.vector.bn_stats(stat6[:, 0, :], x[:, t, :]))
            ch.link(nc.vector.bn_aggr(mv[:, 0, :], stat6[:, 0, :]))
            ch.link(nc.vector.tensor_copy(moments[:, t, :], mv[:, 0, :]))

        def dve_rstd(ch, rms=False):
            mean, var = moments[:, :, 0], moments[:, :, 1]
            if rms:
                ch.link(nc.vector.tensor_tensor(rstd[:, :], mean, mean, ALU.mult))
                ch.link(nc.vector.tensor_tensor(rstd[:, :], rstd[:, :], var, ALU.add))
                var = rstd[:, :]
            dve_rsqrt(ch, rstd[:, :], var)

        def dve_normalise(out, src, n, rms=False):
            if rms:
                return nc.vector.tensor_scalar(out, src, rstd[:, bass.ds(n, 1)], None, ALU.mult)
            return nc.vector.tensor_scalar(out, src, moments[:, n, 0:1], rstd[:, bass.ds(n, 1)],
                                           ALU.subtract, ALU.mult)

        def dve_norm(v, ch, L, n):
            after(v, L.s["a"], n)
            dve_normalise(L.xn, x[:, n, :], n, rms=L.li == 3).then_inc(L.s["xn"].sem, 1)

        def dve_modulate(v, ch, L, n):
            after(v, L.s["a"], n + 1)
            ps = psW0[:, 0:D].rearrange("p (k b n) -> p k b n", k=KC, n=N)
            ch.link(nc.vector.tensor_tensor(four(L.tmpT), ps, batches(L.g, n), ALU.mult))
            after(v, L.s["v1" if L.wide else "vp"], n)
            nc.vector.tensor_tensor(four(L.hT), four(L.tmpT), batches(L.b, n), ALU.add).then_inc(L.s["h"].sem, 1)

        def halves(ap):
            return [ap[:, 0:8], ap[:, 8:16]]

        def dve_softmax(v, ch, L, t):
            for i in range(2):
                ps = psS[:, 512 * i:512 * i + 512].rearrange("p (a b) -> p a b", b=N)
                mx = halves(L.mx)[i]
                after(v, L.s[f"s{i}"], t + 1)
                ch.link(nc.vector.tensor_reduce(mx, ps, AX.X, ALU.max))
                after(v, L.s["tb" if i else "ta"], t)
                nc.vector.tensor_tensor(L.E[:, 8 * i:8 * i + 8, :], ps, mx.unsqueeze(2).broadcast_to([P, 8, N]),
                                        ALU.subtract).then_inc(L.s[f"sub{i}"].sem, 1)

        def dve_prob_sums(v, ch, L, t):
            for i in range(2):
                mx, rs = halves(L.mx)[i], halves(L.rs)[i]
                after(v, L.s[f"exp{i}"], t + 1)
                ch.link(nc.vector.tensor_reduce(mx, L.E[:, 8 * i:8 * i + 8, :], AX.X, ALU.add))
                after(v, L.s[f"prob{i}"], t)
                nc.vector.reciprocal(rs, mx).then_inc(L.s[f"rsum{i}"].sem, 1)

        def dve_narrow_qk(v, ch, L, n):
            after(v, L.s["qk"], n + 1)
            ps = psW1[:, :].rearrange("p (a b) -> p a b", b=P)

            def bias(name):
                return c(name, 0, 4).unsqueeze(2).broadcast_to([P, 4, P])

            if L.li == 0:
                after(v, L.s["s1"], n)
                nc.vector.tensor_tensor(L.qk, ps, bias("l0_bqk"), ALU.add).then_inc(L.s["qke"].sem, 1)
                return

            def angles(i):
                return trig[:, i * N:(i + 1) * N].unsqueeze(1).broadcast_to([P, 8, N])

            def eight(ap):
                return ap.rearrange("p a (b n) -> p (a b) n", n=N)

            ps2 = psW0[:, :].rearrange("p (a b) -> p a b", b=P)
            ch.link(nc.vector.tensor_tensor(L.rot, ps2, bias("l3_bqkr"), ALU.add))
            ch.link(nc.vector.tensor_tensor(L.rot2, ps, bias("l3_bqk"), ALU.add))
            ch.link(nc.vector.tensor_tensor(eight(L.rot), eight(L.rot), angles(1), ALU.mult))
            ch.link(nc.vector.tensor_tensor(eight(L.rot2), eight(L.rot2), angles(0), ALU.mult))
            after(v, L.s["s1"], n)
            nc.vector.tensor_tensor(L.qk, L.rot, L.rot2, ALU.add).then_inc(L.s["qke"].sem, 1)

        def dve_narrow_o(v, ch, L, t):
            after(v, L.s["pv"], t + 1)
            o = psO[:, 0:272].rearrange("p (h d) -> p h d", d=17)
            ch.link(nc.vector.reciprocal(L.rs.unsqueeze(2), o[:, :, 16:17]))
            nc.vector.tensor_tensor(L.o16.rearrange("p (h d) -> p h d", d=16), o[:, :, 0:16],
                                    L.rs.unsqueeze(2).broadcast_to([P, H, 16]), ALU.mult).then_inc(L.s["on"].sem, 1)

        def dve_narrow_x(v, ch, L, t):
            after(v, L.s["xb"], t + 1)
            after(v, L.s["y"], t + 1)
            nc.vector.tensor_tensor(x[:, t, :], x[:, t, :], psO[:, 512:512 + D], ALU.add).then_inc(L.s["xupd"].sem, 1)
            after_all(v, su["table"], [(L.s["xupd"], t + 1)])
            dve_moments(ch, t)

        def dve_l1_qk(v, ch, L, n, between=None):
            for i in range(4):
                after(v, L.s[f"sq{i}"], n + 1)
                ins = nc.vector.tensor_reduce(L.ss[:, i, :], L.sq[i % 2], AX.X, ALU.add)
                ins.then_inc(L.s[f"r{i}"].sem, 1)
                if i == 0 and between:
                    between()
            after(v, L.s["r3"], n + 1)
            ch.link(nc.vector.tensor_scalar(L.ss, L.ss, 1.0 / 64, None, ALU.mult))
            dve_rsqrt(ch, L.ss, L.ss)
            for i in range(4):
                nc.vector.tensor_tensor(L.qn[i], L.qn[i], L.ss[:, i, :].unsqueeze(2).broadcast_to([P, 8, 64]),
                                        ALU.mult).then_inc(L.s[f"n{i}"].sem, 1)

        def dve_l2_qk(v, ch, L, n):
            after(v, L.s["s1"], n)
            for i in (1, 3):
                after(v, L.s[f"i{i}"], n + 1)
                nc.vector.tensor_copy(L.qk[:, 4 * i:4 * i + 4, :], psW0[:, :].rearrange("p (a b) -> p a b", b=P)
                                      ).then_inc(L.s[f"e{i}"].sem, 1)

        def dve_l1_x1(v, ch, L, t):
            after(v, L.s["y"], t + 1)
            after(v, L.s["x1t"], t)
            if not isinstance(t, int) or t > 0:
                v.wait_ge(st["tab"], t * 32)
            nc.vector.tensor_tensor(L.x1, x[:, t, :], psP[:, 0:D], ALU.add).then_inc(L.s["xupd"].sem, 1)

        def dve_l1_gates(v, ch, L, t):
            after(v, L.s["lg"], t + 1)
            nc.vector.tensor_copy(gates[:, t, :], psP[:, 0:E8]).then_inc(L.s["gate"].sem, 1)

        def dve_l2_y(v, ch, L, t):
            after(v, L.s["y"], t + 1)
            yT = L.x1T
            ps = psP[:, 0:D].rearrange("p (k n) -> p k n", n=P)
            ch.link(nc.vector.tensor_tensor(yT, ps, c("l2_bout", 0, 2).unsqueeze(2).broadcast_to([P, KC, P]), ALU.add))
            nc.vector.tensor_tensor(four(yT), four(yT), batches(table("gate2"), t), ALU.mult).then_inc(L.s["yt"].sem, 1)

        def dve_l2_x(v, ch, L, t):
            after(v, L.s["bk"], t + 1)
            nc.vector.tensor_tensor(x[:, t, :], x[:, t, :], psP[:, 512:512 + D], ALU.add).then_inc(L.s["xupd"].sem, 1)
            after_all(v, su["table"], [(L.s["xupd"], t + 1)])
            dve_moments(ch, t)

        def dve_attention(v, ch, L):
            qk = {0: dve_narrow_qk, 1: dve_l1_qk, 2: dve_l2_qk, 3: dve_narrow_qk}[L.li]

            def first():
                ch.reset()
                dve_rstd(ch, rms=L.li == 3)
                dve_norm(v, ch, L, 0)
                dve_modulate(v, ch, L, 0)
                dve_norm(v, ch, L, 1)
                qk(v, ch, L, 0)

            def step(t, ahead, behind):
                def gates_before():
                    if behind:
                        dve_l1_gates(v, ch, L, t - 1)

                ch.reset()
                if ahead:
                    dve_modulate(v, ch, L, t + 1)
                if ahead == 2:
                    dve_norm(v, ch, L, t + 2)
                dve_softmax(v, ch, L, t)
                if L.wide:
                    dve_prob_sums(v, ch, L, t)
                if L.li == 1:
                    if ahead:
                        dve_l1_qk(v, ch, L, t + 1, gates_before)
                    else:
                        gates_before()
                    dve_l1_x1(v, ch, L, t)
                elif L.li == 2:
                    if behind:
                        dve_l2_x(v, ch, L, t - 1)
                    if ahead:
                        dve_l2_qk(v, ch, L, t + 1)
                    dve_l2_y(v, ch, L, t)
                else:
                    if ahead:
                        dve_narrow_qk(v, ch, L, t + 1)
                    if behind:
                        dve_narrow_x(v, ch, L, t - 1)
                    dve_narrow_o(v, ch, L, t)

            def last():
                {0: dve_narrow_x, 1: dve_l1_gates, 2: dve_l2_x, 3: dve_narrow_x}[L.li](v, ch, L, NT - 1)

            tiles(v, NT, first, step, last)

        def act_l1_square(a, L, n, i):
            after(a, L.s[f"cp{i}"], n + 1)
            after(a, L.s[f"r{(i + 2) % 4}"], n if i < 2 else n + 1)
            nc.scalar.activation(L.sq[i % 2], L.qn[i], ACT.Square).then_inc(L.s[f"sq{i}"].sem, 1)

        def act_qk(a, L, n):
            if L.li == 1:
                for i in range(4):
                    after(a, L.s[f"i{i}"], n + 1)
                    after(a, L.s[f"t{i}"], n)
                    ps = (psW0 if i % 2 else psW1)[:, :].rearrange("p (a b) -> p a b", b=64)
                    nc.scalar.activation(L.qn[i], ps, ACT.Copy).then_inc(L.s[f"cp{i}"].sem, 1)
                    if i < 3:
                        act_l1_square(a, L, n, i)
            if L.li == 2:
                for i in (0, 2):
                    after(a, L.s[f"i{i}"], n + 1)
                    if i == 0:
                        after(a, L.s["s1"], n)
                    nc.scalar.activation(L.qk[:, 4 * i:4 * i + 4, :], psW1[:, :].rearrange("p (a b) -> p a b", b=P),
                                         ACT.Copy).then_inc(L.s[f"e{i}"].sem, 1)

        def act_l1_turned(a, L, n, i):
            after(a, L.s[f"t{i}"], n + 1)
            if i == 0:
                after(a, L.s["s1"], n)
            ps = psO[:, i % 2 * 512:i % 2 * 512 + 512].rearrange("p (a b) -> p a b", b=P)
            g = 2 * (i // 2)
            nc.scalar.activation(L.qk[:, 4 * i:4 * i + 4, :], ps, ACT.Identity, bias=c("l1_qn", g + 1),
                                 scale=c("l1_qn", g)).then_inc(L.s[f"e{i}"].sem, 1)

        def act_v(a, L, n):
            if L.wide:
                after(a, L.s["v0"], n + 1)
                after(a, L.s["pv"], n)
                nc.scalar.activation(L.v[:, 0:512], psW1[:, :], ACT.Copy).then_inc(L.s["v0e"].sem, 1)
                after(a, L.s["v1"], n + 1)
                nc.scalar.activation(L.v[:, 512:1024], psW0[:, :], ACT.Copy).then_inc(L.s["v"].sem, 1)
            else:
                after(a, L.s["vp"], n + 1)
                after(a, L.s["pv"], n)
                nc.scalar.activation(L.v[:, :, 0:16], psW1[:, 0:D].rearrange("p (h d) -> p h d", d=16),
                                     ACT.Copy).then_inc(L.s["v"].sem, 1)

        def act_attention(a, L):
            scale = {0: 1.0, 1: 0.125, 2: 0.125, 3: 0.25}[L.li]

            def turned(n):
                if L.li == 1:
                    for i in range(4):
                        act_l1_turned(a, L, n, i)

            def narrow_o(t):
                after(a, L.s["ot"], t + 1)
                after(a, L.s["y"], t)
                for k in range(KC):
                    ins = nc.scalar.activation(L.oT[:, k, :], psO[:, 512 + k * P:512 + (k + 1) * P], ACT.Identity,
                                               bias=c(f"l{L.li}_bv", k), scale=0.0625 if L.li == 0 else 1.0)
                ins.then_inc(L.s["ote"].sem, 1)

            def finish(t):
                if L.li == 1:
                    after(a, L.s["x1t"], t + 1)
                    nc.scalar.activation(L.x1T, psP[:, 512:512 + D].rearrange("p (k n) -> p k n", n=P),
                                         ACT.Copy).then_inc(L.s["x1e"].sem, 1)
                elif not L.wide:
                    narrow_o(t)

            def first():
                act_qk(a, L, 0)
                if L.li == 1:
                    act_l1_square(a, L, 0, 3)
                act_v(a, L, 0)
                turned(0)

            def step(t, ahead, behind):
                for i in range(2):
                    E = L.E[:, 8 * i:8 * i + 8, :]
                    after(a, L.s[f"sub{i}"], t + 1)
                    nc.scalar.activation(E, E, ACT.Exp, scale=scale).then_inc(L.s[f"exp{i}"].sem, 1)
                    if i == 0 and behind:
                        finish(t - 1)
                if ahead:
                    act_qk(a, L, t + 1)
                after(a, L.s["ta"], t + 1)
                after(a, L.s["pv"], t)
                psp = psP[:, :].rearrange("p (a b) -> p a b", b=P)
                nc.scalar.activation(L.PT[:, 0:4, :], psp[:, 0:4, :], ACT.Copy).then_inc(L.s["pta"].sem, 1)
                after(a, L.s["tb"], t + 1)
                nc.scalar.activation(L.PT[:, 4:8, :], psp[:, 4:8, :], ACT.Copy).then_inc(L.s["ptb"].sem, 1)
                if ahead and L.li == 1:
                    act_l1_square(a, L, t + 1, 3)
                if L.wide:
                    after(a, L.s["pv"], t + 1)
                    after(a, L.s["y"], t)
                    for b in range(2):
                        ins = nc.scalar.activation(L.oT[:, :, b * N:(b + 1) * N],
                                                   psO[:, b * 512:(b + 1) * 512].rearrange("p (j n) -> p j n", n=N),
                                                   ACT.Copy)
                    ins.then_inc(L.s["ote"].sem, 1)
                if ahead:
                    act_v(a, L, t + 1)
                    turned(t + 1)

            tiles(a, NT, first, step, lambda: finish(NT - 1))

        def pool_attention(g, L):
            def masks(n):
                after(g, L.s["qke"], n + 1)
                for i, q in enumerate((L.qe, L.qo)):
                    ins = nc.gpsimd.tensor_tensor(q, L.qk[:, 0:KC, :], par[:, i:i + 1].unsqueeze(2)
                                                  .broadcast_to([P, KC, P]), ALU.mult)
                ins.then_inc(L.s["mask"].sem, 1)

            def first():
                if not L.wide:
                    nc.gpsimd.memset(L.v[:, :, 16:17], 1.0).then_inc(su["ones"], 1)
                    masks(0)

            def step(t, ahead, behind):
                if L.wide:
                    for i in range(2):
                        after(g, L.s[f"rsum{i}"], t + 1)
                        E = L.E[:, 8 * i:8 * i + 8, :]
                        nc.gpsimd.tensor_tensor(E, E, halves(L.rs)[i].unsqueeze(2).broadcast_to([P, 8, N]),
                                                ALU.mult).then_inc(L.s[f"prob{i}"].sem, 1)
                    return
                if ahead:
                    masks(t + 1)
                after(g, L.s["xn"], t + 1)
                nc.gpsimd.tensor_tensor(x[:, t, :], x[:, t, :], bias_row[:, 0 if L.li == 0 else 1, :],
                                        ALU.add).then_inc(L.s["xb"].sem, 1)

            tiles(g, NT, first, step)

        class FeedForward:

            def __init__(self, kind):
                self.kind = kind
                W = Region(work)
                self.xn = W.take(4, D)
                self.stat = W.take(4, 3)
                self.gT = W.take(KC, 512)
                self.tmp = W.take(512)
                self.hid = W.take(FJ, 512)
                if kind == "moe":
                    self.xg = [W.take(4, ROW) for _ in range(2)]
                    self.y = W.take(4, D)
                    self.wcol = W.take(4)
                    self.b1 = [W.take(FJ) for _ in range(2)]
                    self.b2 = [W.take(D) for _ in range(2)]
                    self.idx = [W.take(4).bitcast(I32) for _ in range(2)]
                    self.w1, self.w2 = fc1, fc2
                elif kind == "l2":
                    self.yT = W.take(KC, 512)
                    self.w1, self.w2 = [l2_w1] * 2, [l2_w2] * 2
                else:
                    self.act = [W.take(512) for _ in range(2)]
                    self.w1, self.w2 = [l3_gate] * 2, [l3_down] * 2
                self.s = signals("f_xn f_a f_h f_y f_done" + {"moe": "", "l2": " f_yt f_bk", "l3": ""}[kind], NG)
                self.s |= signals("f_hd f_he" + (" f_act" if kind == "l3" else ""), NG * FJ)
                if kind == "moe":
                    self.s |= signals("f_sc", NG * 64)
                    self.s |= signals("f_in0 f_in1 f_ga0 f_ga1", NG // 2 * 64)
                    self.s |= signals("f_idx0 f_idx1", NG // 2 * 16)

        class SecondNorm:

            def __init__(self):
                W = Region(work)
                self.xn, self.hT = W.take(4, D), W.take(KC, 512)
                self.s = signals("p_xn p_a p_h p_bk p_x", NG)

        def pe_second_norm(pe, Z):
            def turn(n):
                after(pe, Z.s["p_xn"], n + 1)
                after(pe, Z.s["p_h"], n)
                for k, ps in enumerate((psW0, psW1)):
                    for r in range(4):
                        ins = nc.tensor.transpose(ps[:, r * P:(r + 1) * P], Z.xn[:, r, k * P:(k + 1) * P], ident)
                ins.then_inc(Z.s["p_a"].sem, 1)

            def step(t, ahead, behind):
                after(pe, Z.s["p_h"], t + 1)
                after(pe, Z.s["p_x"], t)
                for r in range(4):
                    for k in range(KC):
                        ins = nc.tensor.transpose(psP[:, r * D + k * P:r * D + (k + 1) * P],
                                                  Z.hT[:, k, r * P:(r + 1) * P], ident)
                ins.then_inc(Z.s["p_bk"].sem, 1)
                if ahead:
                    turn(t + 1)

            tiles(pe, NG, lambda: turn(0), step)

        def dve_second_norm(v, ch, Z):
            def norm(n):
                after(v, Z.s["p_a"], n)
                for r in range(4):
                    ins = dve_normalise(Z.xn[:, r, :], x[:, n * 4 + r, :], n * 4 + r)
                    if r < 3:
                        ch.link(ins)
                ins.then_inc(Z.s["p_xn"].sem, 1)

            def first():
                ch.reset()
                dve_rstd(ch)
                norm(0)

            def step(t, ahead, behind):
                ch.reset()
                after(v, Z.s["p_a"], t + 1)
                after(v, Z.s["p_bk"], t)
                for k, ps in enumerate((psW0, psW1)):
                    def of(name):
                        return table(name)[:, k, bass.ds(t * 8, 8)].unsqueeze(2).broadcast_to([P, 8, N])
                    h8 = Z.hT[:, k, :].rearrange("p (b n) -> p b n", n=N)
                    ch.link(nc.vector.tensor_tensor(h8, ps[:, :].rearrange("p (b n) -> p b n", n=N), of("g0"), ALU.mult))
                    ins = nc.vector.tensor_tensor(h8, h8, of("b0"), ALU.add)
                    if k == 0:
                        ch.link(ins)
                ins.then_inc(Z.s["p_h"].sem, 1)
                if ahead:
                    norm(t + 1)
                after(v, Z.s["p_bk"], t + 1)
                xs = x[:, bass.ds(t * 4, 4), :]
                nc.vector.tensor_tensor(xs, xs, psP[:, :].rearrange("p (r d) -> p r d", d=D), ALU.add
                                        ).then_inc(Z.s["p_x"].sem, 1)
                after_all(v, su["table"], [(Z.s["p_x"], t + 1)])
                for r in range(4):
                    dve_moments(ch, t * 4 + r)

            tiles(v, NG, first, step)

        HB = [psP[:, 0:512], psP[:, 512:1024], psO[:, 0:512], psO[:, 512:1024]]

        def pe_ff(pe, Q):
            def turn(n):
                after(pe, Q.s["f_xn"], n + 1)
                after(pe, Q.s["f_h"], n)
                for k, ps in enumerate((psW0, psW1)):
                    for r in range(4):
                        ins = nc.tensor.transpose(ps[:, r * P:(r + 1) * P], Q.xn[:, r, k * P:(k + 1) * P], ident)
                ins.then_inc(Q.s["f_a"].sem, 1)

            def hidden(t, u, half):
                after(pe, Q.s["f_h"], t + 1)
                if Q.kind == "moe":
                    after(pe, Q.s[f"f_in{u}"], (half + 1) * 64)
                for j in range(FJ):
                    if Q.kind == "l3":
                        after(pe, Q.s["f_he"], t * FJ + (j - 1))
                        for ps, w in ((HB[j % 2], l3_gate), (HB[2 + j % 2], l3_up)):
                            for k in range(KC):
                                ins = nc.tensor.matmul(ps, w[:, k, j * P:(j + 1) * P], Q.gT[:, k, :],
                                                       start=(k == 0), stop=(k == KC - 1))
                        ins.then_inc(Q.s["f_hd"].sem, 1)
                        continue
                    after(pe, Q.s["f_he"], t * FJ + (j - 3))
                    if Q.kind == "l2" and j == 0:
                        after(pe, Q.s["f_done"], t)
                    for k in range(KC):
                        ins = nc.tensor.matmul(HB[j % 4], Q.w1[u][:, k, j * P:(j + 1) * P], Q.gT[:, k, :],
                                               start=(k == 0), stop=(k == KC - 1))
                    ins.then_inc(Q.s["f_hd"].sem, 1)

            def result(t, u):
                after(pe, Q.s["f_he"], t * FJ + FJ)
                after(pe, Q.s["f_yt" if Q.kind == "l2" else "f_done"], t)
                if Q.kind == "l2":
                    for q in range(KC):
                        for j in range(FJ):
                            ins = nc.tensor.matmul(psS[:, q * 512:(q + 1) * 512], Q.w2[u][:, j, q * P:(q + 1) * P],
                                                   Q.hid[:, j, :], start=(j == 0), stop=(j == FJ - 1))
                    ins.then_inc(Q.s["f_y"].sem, 1)
                    after(pe, Q.s["f_yt"], t + 1)
                    for r in range(4):
                        for k in range(KC):
                            ins = nc.tensor.transpose(psP[:, r * D + k * P:r * D + (k + 1) * P],
                                                      Q.yT[:, k, r * P:(r + 1) * P], ident)
                    ins.then_inc(Q.s["f_bk"].sem, 1)
                    return
                for r in range(4):
                    for j in range(FJ):
                        ins = nc.tensor.matmul(psS[:, r * D:(r + 1) * D], Q.hid[:, j, r * P:(r + 1) * P],
                                               Q.w2[u][:, j, :], start=(j == 0), stop=(j == FJ - 1))
                ins.then_inc(Q.s["f_y"].sem, 1)

            def step(t, u, half, more):
                hidden(t, u, half)
                if more:
                    turn(t + 1)
                result(t, u)

            pairs(pe, NG, lambda: turn(0), step)

        def dve_ff(v, ch, Q):
            def norm(n, u, half):
                if Q.kind == "moe":
                    after_all(v, su["table"], [(Q.s[f"f_ga{u}"], (half + 1) * 64)])
                    for r in range(4):
                        ch.link(nc.vector.bn_stats(stat6[:, r, :], Q.xg[u][:, r, 0:D]))
                        ch.link(nc.vector.bn_aggr(Q.stat[:, r, 0:2], stat6[:, r, :]))
                    dve_rsqrt(ch, Q.stat[:, :, 2], Q.stat[:, :, 1])
                after(v, Q.s["f_a"], n)
                for r in range(4):
                    if Q.kind == "moe":
                        ins = nc.vector.tensor_scalar(Q.xn[:, r, :], Q.xg[u][:, r, 0:D], Q.stat[:, r, 0:1],
                                                      Q.stat[:, r, 2:3], ALU.subtract, ALU.mult)
                    else:
                        ins = dve_normalise(Q.xn[:, r, :], x[:, n * 4 + r, :], n * 4 + r, rms=Q.kind == "l3")
                    if r < 3:
                        ch.link(ins)
                ins.then_inc(Q.s["f_xn"].sem, 1)

            def modulate(n):
                after(v, Q.s["f_a"], n + 1)
                after(v, Q.s["f_hd"], n * FJ)
                for k, ps in enumerate((psW0, psW1)):
                    if Q.kind == "moe":
                        ins = nc.vector.tensor_scalar(Q.gT[:, k, :], ps[:, :], c("l1_mlp", k), c("l1_mlp", 2 + k),
                                                      ALU.mult, ALU.add)
                        if k == 0:
                            ch.link(ins)
                        continue
                    g, b = table("g2f" if Q.kind == "l2" else "g3f"), table("b2f" if Q.kind == "l2" else "b3f")

                    def of(tb):
                        return tb[:, k, bass.ds(n * 8, 8)].unsqueeze(2).broadcast_to([P, 8, N])

                    def eight(ap):
                        return ap.rearrange("p (b n) -> p b n", n=N)

                    ch.link(nc.vector.tensor_tensor(eight(Q.gT[:, k, :]), eight(ps[:, :]), of(g), ALU.mult))
                    ins = nc.vector.tensor_tensor(eight(Q.gT[:, k, :]), eight(Q.gT[:, k, :]), of(b), ALU.add)
                    if k == 0:
                        ch.link(ins)
                ins.then_inc(Q.s["f_h"].sem, 1)

            def products(t):
                for j in range(FJ):
                    after(v, Q.s["f_act"], t * FJ + (j + 1))
                    if j == 0:
                        after(v, Q.s["f_y"], t)
                    nc.vector.tensor_tensor(Q.hid[:, j, :], Q.act[j % 2], HB[2 + j % 2], ALU.mult).then_inc(Q.s["f_he"].sem, 1)

            def result(t, u):
                after(v, Q.s["f_y"], t + 1)
                if Q.kind == "l2":
                    for q in range(KC):
                        gate = table("gate2f")[:, q, bass.ds(t * 8, 8)].unsqueeze(2).broadcast_to([P, 8, N])
                        yT = Q.yT[:, q, :]
                        ch.link(nc.vector.tensor_scalar(yT, psS[:, q * 512:(q + 1) * 512], c("l2_b2", q), None, ALU.add))
                        y3 = yT.rearrange("p (b n) -> p b n", n=N)
                        ins = nc.vector.tensor_tensor(y3, y3, gate, ALU.mult)
                        if q == 0:
                            ch.link(ins)
                    ins.then_inc(Q.s["f_yt"].sem, 1)
                    after(v, Q.s["f_bk"], t + 1)
                    xs = x[:, bass.ds(t * 4, 4), :]
                    nc.vector.tensor_tensor(xs, xs, psP[:, :].rearrange("p (r d) -> p r d", d=D), ALU.add
                                            ).then_inc(Q.s["f_done"].sem, 1)
                    after_all(v, su["table"], [(Q.s["f_done"], t + 1)])
                    for r in range(4):
                        dve_moments(ch, t * 4 + r)
                elif Q.kind == "l3":
                    xs = x[:, bass.ds(t * 4, 4), :]
                    nc.vector.tensor_tensor(xs, xs, psS[:, :].rearrange("p (r d) -> p r d", d=D), ALU.add
                                            ).then_inc(Q.s["f_done"].sem, 1)
                else:
                    ch.link(nc.vector.tensor_copy(Q.wcol.unsqueeze(2), Q.xg[u][:, :, bass.ds(t + D, 1)]))
                    after(v, Q.s["f_sc"], t * 64)
                    ch.link(nc.vector.tensor_tensor(Q.y, psS[:, :].rearrange("p (r d) -> p r d", d=D),
                                                    Q.b2[u].unsqueeze(1).broadcast_to([P, 4, D]), ALU.add))
                    nc.vector.tensor_tensor(Q.y, Q.y, Q.wcol.unsqueeze(2).broadcast_to([P, 4, D]), ALU.mult
                                            ).then_inc(Q.s["f_done"].sem, 1)

            def first():
                ch.reset()
                if Q.kind != "moe":
                    dve_rstd(ch, rms=Q.kind == "l3")
                norm(0, 0, 0)
                modulate(0)

            def step(t, u, half, more):
                ch.reset()
                if more:
                    norm(t + 1, 1 - u, half + u)
                if Q.kind == "l3":
                    products(t)
                if more:
                    modulate(t + 1)
                result(t, u)

            pairs(v, NG, first, step)

        def act_ff(a, Q):
            def step(t, u, half, more):
                if Q.kind == "moe":
                    after(a, Q.s[f"f_in{u}"], (half + 1) * 64)
                for j in range(FJ):
                    after(a, Q.s["f_hd"], t * FJ + (j + 1))
                    if Q.kind == "l3":
                        after(a, Q.s["f_he"], t * FJ + (j - 1))
                        nc.scalar.activation(Q.act[j % 2], HB[j % 2], ACT.Gelu).then_inc(Q.s["f_act"].sem, 1)
                        continue
                    if j == 0:
                        after(a, Q.s["f_y"], t)
                    bias = Q.b1[u][:, j:j + 1] if Q.kind == "moe" else c("l2_b1", j)
                    nc.scalar.activation(Q.hid[:, j, :], HB[j % 4], ACT.Gelu_apprx_tanh if Q.kind == "moe" else ACT.Gelu,
                                         bias=bias).then_inc(Q.s["f_he"].sem, 1)

            pairs(a, NG, lambda: None, step)
        def pool_moe(g, Q):
            def gather(n, u, half):
                after_all(g, su["table"], [(Q.s[f"f_idx{u}"], (half + 1) * 16), (Q.s["f_done"], n - 1)])
                for r in range(4):
                    nc.gpsimd.indirect_dma_start(
                        out=Q.xg[u][:, r, :], out_offset=None, in_=gather_table,
                        in_offset=bass.IndirectOffsetOnAxis(ap=Q.idx[u][:, r:r + 1], axis=0)
                    ).then_inc(Q.s[f"f_ga{u}"].sem, 16)

            def step(t, u, half, more):
                if more:
                    gather(t + 1, 1 - u, half + u)
                after_all(g, su["table"], [(Q.s["f_done"], t + 1), (Q.s["f_sc"], t * 64)])
                for r in range(4):
                    nc.gpsimd.indirect_dma_start(
                        out=moe_sum, out_offset=bass.IndirectOffsetOnAxis(ap=Q.idx[u][:, r:r + 1], axis=0),
                        in_=Q.y[:, r, :], in_offset=None, compute_op=ALU.add
                    ).then_inc(Q.s["f_sc"].sem, 16)

            g.wait_ge(st["gates"], 16)
            pairs(g, NG, lambda: gather(0, 0, 0), step)

        def sp_moe(sp, Q):
            def weights(e, u):
                after(sp, Q.s["f_done"], e - 1)
                sp.dma_start(Q.w1[u], A["l1_fc1"][e].rearrange("(k p) n -> p k n", p=P)).then_inc(Q.s[f"f_in{u}"].sem, 16)
                sp.dma_start(Q.w2[u], A["l1_fc2"][e].rearrange("(k p) n -> p k n", p=P)).then_inc(Q.s[f"f_in{u}"].sem, 16)
                sp.dma_start(Q.b1[u], A["l1_b1"][e]).then_inc(Q.s[f"f_in{u}"].sem, 16)
                sp.dma_start(Q.b2[u], A["l1_b2"][e].broadcast_to([P, D])).then_inc(Q.s[f"f_in{u}"].sem, 16)

            def indices(e, u):
                after(sp, Q.s["f_sc"], (e - 1) * 64)
                sp.dma_start(Q.idx[u], slot_token.rearrange("(e p r) -> e p r", p=P, r=4)[e]
                             ).then_inc(Q.s[f"f_idx{u}"].sem, 16)

            def step(t, u, half, more):
                if more:
                    weights(t + 1, 1 - u)
                    indices(t + 1, 1 - u)

            def first():
                weights(0, 0)
                sp.wait_ge(st["idx"], 16 * E8)
                indices(0, 0)

            pairs(sp, NG, first, step)

        consts = sb("consts", [P, NCONST])
        cc = {n: consts[:, a:a + w] for n, (a, w) in CONSTS.items()}
        ident, trig, lower, iota16, iota32 = cc["ident"], cc["trig"], cc["lower"], cc["iota16"], cc["iota32"]
        ones, par, pidx, tidx = cc["ones"], cc["par"], cc["pidx"], cc["tidx"]
        condT = work[:, 0:KC * B].rearrange("p (k b) -> p k b", b=B)
        silT = work[:, 128:256].rearrange("p (k b) -> p k b", b=B)
        hidT = work[:, 256:512].rearrange("p (k b) -> p k b", b=B)
        mod = work[:, 512:512 + 12 * B].rearrange("p (k b) -> p k b", b=B)

        def pe_setup(pe):
            pe.wait_ge(ld["small"], 48)
            pe.wait_ge(ld["modw"], 80)

            def mm(ps, w, w0, src, n):
                for q in range(n):
                    for k in range(KC):
                        ins = nc.tensor.matmul(ps[:, q * B:(q + 1) * B], w[:, w0 + k, q * P:(q + 1) * P], src[:, k, :],
                                               start=(k == 0), stop=(k == KC - 1))
                return ins

            mm(psS[:, 0:256], m0, 0, condT, 4)
            mm(psW0[:, 0:128], m3a, 0, condT, 2)
            mm(psW0[:, 128:256], m3a, 2, condT, 2).then_inc(su["mm"], 1)
            pe.wait_ge(su["silu"], 1)
            mm(psS[:, 256:384], m1, 0, silT, 2)
            mm(psP[:, 0:512], m2[:, :, 0:1024], 0, silT, 8)
            mm(psP[:, 512:768], m2[:, :, 1024:1536], 0, silT, 4)
            pe.wait_ge(su["hidden"], 1)
            mm(psW1[:, 0:256], m3b, 0, hidT[:, 0:2, :], 4)
            mm(psW1[:, 256:512], m3b, 2, hidT[:, 2:4, :], 4).then_inc(su["mm2"], 1)

        def act_setup(a):
            a.wait_ge(ld["small"], 48)
            nc.scalar.activation(silT, condT, ACT.Silu).then_inc(su["silu"], 1)
            a.wait_ge(su["mm"], 1)
            for i in range(4):
                ins = nc.scalar.activation(hidT[:, i, :], psW0[:, i * B:(i + 1) * B], ACT.Silu, bias=c("l3_tb1", i))
            ins.then_inc(su["hidden"], 1)

        def dve_setup(v, ch):
            v.wait_ge(ld["small"], 48)
            ch.reset()

            def wide(ap):
                return ap.unsqueeze(2).broadcast_to([P, ap.shape[1], B])

            def tt(out, a, b, op=ALU.add):
                ch.link(nc.vector.tensor_tensor(out, a, b, op))

            def psv(ps, lo, n):
                return ps[:, lo * B:(lo + n) * B].rearrange("p (k b) -> p k b", b=B)

            ch.link(nc.vector.tensor_scalar(c("l0_bv", 0, 2), c("l0_bv", 0, 2), 1.0 / 16, None, ALU.mult))
            v.wait_ge(su["mm2"], 1)
            tt(mod[:, 0:4, :], psv(psS, 0, 4), wide(c("l0_bgb", 0, 4)))
            tt(table("g0"), mod[:, 0:2, :], wide(c("l0_g", 0, 2)), ALU.mult)
            tt(mod[:, 4:6, :], mod[:, 0:2, :], wide(c("l0_b", 0, 2)), ALU.mult)
            tt(table("b0"), mod[:, 4:6, :], mod[:, 2:4, :])
            ch.link(nc.vector.tensor_copy(table("g1"), wide(c("l1_g", 0, 2))))
            tt(mod[:, 0:2, :], psv(psS, 4, 2), wide(c("l1_bada", 0, 2)))
            tt(table("b1"), mod[:, 0:2, :], wide(c("l1_b", 0, 2)))
            tt(mod[:, 0:12, :], psv(psP, 0, 12), wide(c("l2_bmod", 0, 12)))
            for i, (b, g, gate) in enumerate((("b2", "g2", "gate2"), ("b2f", "g2f", "gate2f"))):
                ch.link(nc.vector.tensor_copy(table(b), mod[:, 6 * i:6 * i + 2, :]))
                ch.link(nc.vector.tensor_scalar(table(g), mod[:, 6 * i + 2:6 * i + 4, :], 1.0, None, ALU.add))
                ch.link(nc.vector.tensor_copy(table(gate), mod[:, 6 * i + 4:6 * i + 6, :]))
            tt(mod[:, 0:8, :], psv(psW1, 0, 8), wide(c("l3_tb2", 0, 8)))
            for i, (g, b, w) in enumerate((("g3", "b3", "l3_w1"), ("g3f", "b3f", "l3_w2"))):
                ch.link(nc.vector.tensor_scalar(mod[:, 4 * i:4 * i + 2, :], mod[:, 4 * i:4 * i + 2, :], 1.0, None, ALU.add))
                tt(table(g), mod[:, 4 * i:4 * i + 2, :], wide(c(w, 0, 2)), ALU.mult)
                ins = nc.vector.tensor_copy(table(b), mod[:, 4 * i + 2:4 * i + 4, :])
                if i == 0:
                    ch.link(ins)
            ins.then_inc(su["table"], 1)

        def dve_center(v, ch):
            v.wait_ge(ld["l1"], 48)
            ch.reset()
            W = Region(work)
            W.take(9000)
            mean = W.take(32)
            for k in range(KC):
                w = l1_w[:, k, 0:2 * F].rearrange("p (h d) -> p h d", d=64)
                ch.link(nc.vector.tensor_reduce(mean, w, AX.X, ALU.add))
                ch.link(nc.vector.tensor_scalar(mean, mean, 1.0 / 64, None, ALU.mult))
                ins = nc.vector.tensor_tensor(w, w, mean.unsqueeze(2).broadcast_to([P, 32, 64]), ALU.subtract)
                if k == 0:
                    ch.link(ins)
            ins.then_inc(su["center"], 1)

        W = Region(work)
        GE = NT * E8
        cmpT, rank, pre, pre2, sel = (W.take(NT, E8) for _ in range(5))
        cnt, need, eqn = W.take(E8), W.take(E8), W.take(E8)
        gmx = W.take(NT)
        cur, cand, keep, bit = (W.take(E8).bitcast(I32) for _ in range(4))
        bitf = W.take(1)
        ri, ra, rb = (W.take(NT, E8).bitcast(I32) for _ in range(3))
        hotA = W.take(GE * 8).bitcast(BF16).rearrange("p (t e s) -> p t e s", e=E8, s=16)
        hotAp = W.take(GE * 8).bitcast(BF16).rearrange("p (t n) -> p t n", n=P)
        hotAt = W.take(GE * 8).bitcast(BF16).rearrange("p (t n) -> p t n", n=P)
        rt = sems("rt", "shift exp prob cnt tot keep cnt2 tot2 m w hot ix idx")

        def dve_route(v, ch, hotB):
            ch.reset()
            tt = lambda *a: ch.link(nc.vector.tensor_tensor(*a))
            ts = lambda *a: ch.link(nc.vector.tensor_scalar(*a))

            def over_tiles(ap):
                return ap.rearrange("p t e -> p e t")

            def every(ap):
                return ap.unsqueeze(1).broadcast_to([P, NT, E8])

            ch.link(nc.vector.tensor_reduce(gmx, gates[:, :, :], AX.X, ALU.max))
            nc.vector.tensor_tensor(gates[:, :, :], gates[:, :, :], gmx.unsqueeze(2).broadcast_to([P, NT, E8]),
                                    ALU.subtract).then_inc(rt["shift"], 1)
            v.wait_ge(rt["exp"], 1)
            ch.link(nc.vector.tensor_reduce(gmx, gates[:, :, :], AX.X, ALU.add))
            ch.link(nc.vector.reciprocal(gmx, gmx))
            nc.vector.tensor_tensor(gates[:, :, :], gates[:, :, :], gmx.unsqueeze(2).broadcast_to([P, NT, E8]),
                                    ALU.mult).then_inc(rt["prob"], 1)
            v.wait_ge(rt["prob"], 1)
            ch.link(nc.vector.memset(cur, 0))
            ch.link(nc.vector.memset(bit, 1 << 29))
            ch.link(nc.vector.memset(bitf, float(1 << 29)))

            def one_bit(i):
                ch.reset()
                tt(cand, cur, bit, ALU.bitwise_or)
                tt(cmpT, gates[:, :, :], every(cand.bitcast(FP32)), ALU.is_ge)
                nc.vector.tensor_reduce(cnt, over_tiles(cmpT), AX.X, ALU.add).then_inc(rt["cnt"], 1)
                v.wait_ge(rt["tot"], i + 1)
                ts(keep, psW0[:, 0:E8], CAP - 0.5, bitf[:, 0:1], ALU.is_ge, ALU.mult)
                tt(cur, cur, keep, ALU.bitwise_or)
                ts(bit, bit, 1, None, ALU.logical_shift_right)
                nc.vector.tensor_scalar(bitf, bitf, 0.5, None, ALU.mult).then_inc(rt["keep"], 1)
                v.wait_ge(rt["keep"], i + 1)

            with v.Fori(0, 30) as i:
                one_bit(i)
            ch.reset()
            thr = every(cur.bitcast(FP32))
            tt(sel, gates[:, :, :], thr, ALU.is_gt)
            tt(cmpT, gates[:, :, :], thr, ALU.is_equal)
            nc.vector.tensor_reduce(cnt, over_tiles(sel), AX.X, ALU.add).then_inc(rt["cnt2"], 1)

            def ranks(mask, i):
                v.wait_ge(rt["w"], i + 1)
                within = psS[:, 0:GE].rearrange("p (t e) -> p t e", e=E8)
                total = psS[:, 512:512 + GE].rearrange("p (t e) -> p t e", e=E8)
                ch.link(nc.vector.memset(pre[:, 0:1, :], 0.0))
                ch.link(nc.vector.tensor_copy(pre[:, 1:NT, :], total[:, 0:NT - 1, :]))
                src, dst = pre, pre2
                k = 1
                while k < NT:
                    ch.link(nc.vector.tensor_copy(dst[:, 0:k, :], src[:, 0:k, :]))
                    tt(dst[:, k:NT, :], src[:, k:NT, :], src[:, 0:NT - k, :], ALU.add)
                    src, dst, k = dst, src, 2 * k
                tt(rank, within, src, ALU.add)

            v.wait_ge(rt["tot2"], 1)
            nc.vector.tensor_scalar(need, psW0[:, 0:E8], -1.0, float(CAP), ALU.mult, ALU.add).then_inc(rt["m"], 1)
            v.wait_ge(rt["m"], 1)
            ranks(cmpT, 0)
            tt(rank, rank, every(need), ALU.is_lt)
            tt(cmpT, cmpT, rank, ALU.mult)
            nc.vector.tensor_tensor(sel, sel, cmpT, ALU.add).then_inc(rt["m"], 1)
            v.wait_ge(rt["m"], 2)
            ranks(sel, 1)
            ts(rank, rank, 1.0, None, ALU.add)
            tt(rank, rank, sel, ALU.mult)
            ts(ri, rank, -1.0, None, ALU.add)
            ts(ra, ri, 5, None, ALU.arith_shift_right)
            ts(rb, ri, 31, None, ALU.bitwise_and)
            ch.link(nc.vector.tensor_copy(pre, ra))
            ch.link(nc.vector.tensor_copy(pre2, rb))
            flat = lambda ap: ap.rearrange("p t e -> p (t e)")
            tt(hotA.rearrange("p t e s -> p (t e) s"), flat(pre).unsqueeze(2).broadcast_to([P, GE, 16]),
               iota16.unsqueeze(1).broadcast_to([P, GE, 16]), ALU.is_equal)
            tt(hotB.rearrange("p t (e s) -> p (t e) s", s=32), flat(pre2).unsqueeze(2).broadcast_to([P, GE, 32]),
               iota32.unsqueeze(1).broadcast_to([P, GE, 32]), ALU.is_equal)
            hotA3 = hotA.rearrange("p t e s -> p t (e s)")
            ts(hotAp, hotA3, pidx[:, 0:1], None, ALU.mult)
            nc.vector.tensor_tensor(hotAt, hotA3, tidx.unsqueeze(2).broadcast_to([P, NT, P]), ALU.mult
                                    ).then_inc(rt["hot"], 1)
            v.wait_ge(rt["ix"], 1)
            ts(flat(sel), psP[:, 512:512 + GE], 128.0, None, ALU.mult)
            nc.vector.tensor_tensor(flat(ri), flat(sel), psP[:, 0:GE], ALU.add).then_inc(rt["idx"], 1)

        def pe_route(pe, hotB):
            with pe.Fori(0, 30) as i:
                pe.wait_ge(rt["cnt"], i + 1)
                nc.tensor.matmul(psW0[:, 0:E8], ones, cnt, start=True, stop=True).then_inc(rt["tot"], 1)
            pe.wait_ge(rt["cnt2"], 1)
            nc.tensor.matmul(psW0[:, 0:E8], ones, cnt, start=True, stop=True).then_inc(rt["tot2"], 1)
            for i, mask in enumerate((cmpT, sel)):
                pe.wait_ge(rt["m"], i + 1)
                nc.tensor.matmul(psS[:, 0:GE], lower, mask.rearrange("p t e -> p (t e)"), start=True, stop=True)
                nc.tensor.matmul(psS[:, 512:512 + GE], ones, mask.rearrange("p t e -> p (t e)"),
                                 start=True, stop=True).then_inc(rt["w"], 1)
            pe.wait_ge(rt["hot"], 1)
            for lo, hot in ((0, hotAp), (512, hotAt)):
                for t in range(NT):
                    ins = nc.tensor.matmul(psP[:, lo:lo + GE], hot[:, t, :], hotB[:, t, :],
                                           start=(t == 0), stop=(t == NT - 1))
            ins.then_inc(rt["ix"], 1)

        L = [Attention(i) for i in range(4)]
        Z = SecondNorm()
        Q = {k: FeedForward(k) for k in ("moe", "l2", "l3")}
        hotB = r2[:, 4096:4096 + GE * 16].bitcast(BF16).rearrange("p (t n) -> p t n", n=GE)
        assert 4096 + GE * 16 <= 8192

        ENDS = [(Signal(su["table"], 0), 1), (L[0].s["xupd"], NT), (Z.s["p_x"], NG), (L[1].s["gate"], NT), (Signal(rt["idx"], 0), 1),
                (Q["moe"].s["f_done"], NG), (L[2].s["xupd"], NT), (Q["l2"].s["f_done"], NG),
                (L[3].s["xupd"], NT), (Q["l3"].s["f_done"], NG)]

        block = ctx.enter_context(nc.Block())

        def chunked(name):
            return A[name].rearrange("(k p) n -> p k n", p=P)

        def by_tile(ap):
            return ap.rearrange("(t p) d -> p t d", p=P)

        @block.sync
        def _(sp):
            sp.dma_start(consts[:, :], A["consts"]).then_inc(ld["small"], 16)
            sp.dma_start(col[:, :], A["cols"]).then_inc(ld["small"], 16)
            sp.dma_start(condT, chunked("condT")).then_inc(ld["small"], 16)
            for dst, name in ((m0, "l0_mod"), (m1, "l1_mod"), (m2, "l2_mod"), (m3a, "l3_mod1"), (m3b, "l3_mod2")):
                sp.dma_start(dst, chunked(name)).then_inc(ld["modw"], 16)
            for i in range(4):
                sp.dma_start(x[:, 8 * i:8 * i + 8, :], by_tile(A["x"])[:, 8 * i:8 * i + 8, :]).then_inc(ld["x"], 16)
            sp.dma_start(l0_w, chunked("l0_w")).then_inc(ld["l0"], 16)
            sp.dma_start(l0_wp, chunked("l0_wp")).then_inc(ld["l0"], 16)
            for i, name in enumerate(("l0_bp", "l3_bo")):
                sp.dma_start(bias_row[:, i, :], A[name].broadcast_to([P, D])).then_inc(ld["rows"], 16)
            sp.dma_start(l1_w, chunked("l1_w")).then_inc(ld["l1"], 16)
            sp.dma_start(l1_wout, chunked("l1_wout")).then_inc(ld["l1"], 16)
            sp.dma_start(l1_wgate, chunked("l1_wgate")).then_inc(ld["l1"], 16)
            if stage >= 2:
                with sp.Fori(0, NT) as t:
                    after(sp, L[1].s["xupd"], t + 1)
                    sp.dma_start(by_tile(gather_table)[:, t, 0:D], L[1].x1).then_inc(st["tab"], 16)
                    sp.dma_start(by_tile(moe_sum)[:, t, :], L[1].x1).then_inc(st["tab"], 16)
                after(sp, L[1].s["gate"], NT)
                for dst, name in ((l2_w, "l2_w"), (l2_wout, "l2_wout"), (l2_w1, "l2_w1"), (l2_w2, "l2_w2")):
                    sp.dma_start(dst, chunked(name)).then_inc(ld["l2"], 16)
            if stage >= 3:
                sp.wait_ge(rt["prob"], 1)
                sp.dma_start(by_tile(gather_table)[:, :, D:ROW], gates[:, :, :]).then_inc(st["gates"], 16)
                sp.wait_ge(rt["idx"], 1)
                slots = slot_token.rearrange("(e a s) -> e a s", a=16, s=32)
                for e in range(E8):
                    sp.dma_start(slots[e], ri.rearrange("p t e -> p (t e)")[16 * e:16 * e + 16, 32 * e:32 * e + 32]
                                 ).then_inc(st["idx"], 16)
                sp.wait_ge(st["tab"], 32 * NT)
                sp_moe(sp, Q["moe"])
                after(sp, Q["moe"].s["f_sc"], 64 * E8)
            if stage >= 2:
                sp.wait_ge(st["tab"], 32 * NT)
                for i in range(4):
                    sp.dma_start(x[:, 8 * i:8 * i + 8, :], by_tile(moe_sum)[:, 8 * i:8 * i + 8, :]
                                 ).then_inc(ld["back"], 16)
                for dst, name in ((l3_w, "l3_w"), (l3_wo, "l3_wo"), (l3_gate, "l3_gate"), (l3_up, "l3_up"),
                                  (l3_down, "l3_down")):
                    sp.dma_start(dst, chunked(name)).then_inc(ld["l3"], 16)
                sp.wait_ge(ld["back"], 64)
            s, n = ENDS[{1: 2, 2: 3, 3: 5}.get(stage, stage + 1)]
            if stage >= 8:
                for i in range(NG):
                    after(sp, s, i + 1)
                    sp.dma_start(by_tile(out)[:, 4 * i:4 * i + 4, :], x[:, 4 * i:4 * i + 4, :]).then_inc(st["out"], 16)
                sp.wait_ge(st["out"], 16 * NG)
            else:
                after(sp, s, n)
                sp.dma_start(by_tile(out), x[:, :, :]).then_inc(st["out"], 16)
                sp.wait_ge(st["out"], 16)

        def phase(eng, i):
            after(eng, *ENDS[i - 1])

        def phase_from_memory(eng, i):
            phase(eng, i)
            eng.wait_ge(ld["back"], 64)

        @block.tensor
        def _(pe):
            pe_setup(pe)
            phase(pe, 1)
            pe_attention(pe, L[0])
            phase(pe, 2)
            pe_second_norm(pe, Z)
            if stage >= 2:
                phase(pe, 3)
                pe_attention(pe, L[1])
            if stage >= 3:
                phase(pe, 4)
                pe_route(pe, hotB)
                phase(pe, 5)
                pe_ff(pe, Q["moe"])
            if stage >= 5:
                phase(pe, 6)
                pe_attention(pe, L[2])
            if stage >= 6:
                phase(pe, 7)
                pe_ff(pe, Q["l2"])
            if stage >= 7:
                phase(pe, 8)
                pe_attention(pe, L[3])
            if stage >= 8:
                phase(pe, 9)
                pe_ff(pe, Q["l3"])

        @block.vector
        def _(v):
            ch = Chain(v, chain_dve)
            dve_setup(v, ch)
            v.wait_ge(ld["x"], 64)
            v.wait_ge(su["table"], 1)
            ch.reset()
            for i in range(NT):
                dve_moments(ch, i)
            dve_attention(v, ch, L[0])
            phase(v, 2)
            dve_second_norm(v, ch, Z)
            if stage >= 2:
                phase(v, 3)
                dve_center(v, ch)
                dve_attention(v, ch, L[1])
            if stage >= 3:
                phase(v, 4)
                v.wait_ge(st["tab"], 32 * NT)
                dve_route(v, ch, hotB)
                phase(v, 5)
                v.wait_ge(st["idx"], 16 * E8)
                dve_ff(v, ch, Q["moe"])
            if stage >= 5:
                phase_from_memory(v, 6)
                ch.reset()
                for i in range(NT):
                    dve_moments(ch, i)
                v.wait_ge(chain_dve, ch.n)
                dve_attention(v, ch, L[2])
            if stage >= 6:
                phase(v, 7)
                dve_ff(v, ch, Q["l2"])
            if stage >= 7:
                phase(v, 8)
                dve_attention(v, ch, L[3])
            if stage >= 8:
                phase(v, 9)
                dve_ff(v, ch, Q["l3"])

        @block.scalar
        def _(a):
            act_setup(a)
            phase(a, 1)
            act_attention(a, L[0])
            if stage >= 2:
                phase(a, 3)
                act_attention(a, L[1])
            if stage >= 3:
                a.wait_ge(rt["shift"], 1)
                nc.scalar.activation(gates[:, :, :], gates[:, :, :], ACT.Exp).then_inc(rt["exp"], 1)
                phase(a, 5)
                act_ff(a, Q["moe"])
            if stage >= 5:
                phase(a, 6)
                act_attention(a, L[2])
            if stage >= 6:
                phase(a, 7)
                act_ff(a, Q["l2"])
            if stage >= 7:
                phase(a, 8)
                act_attention(a, L[3])
            if stage >= 8:
                phase(a, 9)
                act_ff(a, Q["l3"])

        @block.gpsimd
        def _(g):
            g.wait_ge(ld["small"], 48)
            g.wait_ge(ld["rows"], 32)
            phase(g, 1)
            pool_attention(g, L[0])
            if stage >= 2:
                phase(g, 3)
                pool_attention(g, L[1])
            if stage >= 3:
                phase(g, 5)
                pool_moe(g, Q["moe"])
            if stage >= 5:
                phase(g, 6)
                pool_attention(g, L[2])
            if stage >= 7:
                phase(g, 8)
                pool_attention(g, L[3])


def host_arrays(I):
    a = {k: np.asarray(v) for k, v in I.items()}
    l0 = lambda n: a["L0_cond_" + n]
    l1 = lambda n: a["L1_cond_" + n]
    l2 = lambda n: a["L2_cond_" + n]
    l3 = lambda n: a["L3_cond_" + n]
    cat = np.concatenate
    wqkv = l0("Wqkv").reshape(H, 16, 3, D).transpose(2, 0, 1, 3).reshape(3 * D, D)
    bqkv = l0("bqkv").reshape(H, 16, 3).transpose(2, 0, 1).reshape(3, D)

    def rotated(w):
        return np.roll(w.reshape(w.shape[:-1] + (H, 16)), 8, axis=-1).reshape(w.shape)

    twice = lambda w: cat([w, w])
    vectors = {
        "l0_g": l0("ln_g"), "l0_b": l0("ln_b"), "l0_bgb": cat([l0("bg"), l0("bb")]),
        "l0_bqk": cat([bqkv[0], bqkv[1]]), "l0_bv": bqkv[2],
        "l1_bada": l1("b_ada"), "l1_g": l1("ln1_g"), "l1_b": l1("ln1_b"),
        "l1_qn": cat([twice(l1(n)) for n in ("qn_g", "qn_b", "kn_g", "kn_b")]),
        "l1_mlp": cat([l1("mlp_g"), l1("mlp_b")]),
        "l2_bmod": l2("b_mod"), "l2_bout": l2("b_out"), "l2_b1": l2("b1"), "l2_b2": l2("b2"),
        "l3_w1": l3("w_norm1"), "l3_w2": l3("w_norm2"), "l3_tb1": cat([l3("t1_b1"), l3("t2_b1")]),
        "l3_tb2": cat([l3("t1_b2"), l3("t2_b2")]), "l3_bqk": cat([l3("bq"), l3("bk")]),
        "l3_bqkr": cat([rotated(l3("bq")), rotated(l3("bk"))]), "l3_bv": l3("bv")}
    cols = cat([vectors[n].reshape(k, P).T for n, (_, k) in COLS.items()], axis=1)
    assert cols.shape == (P, NCOL)
    f32 = np.float32
    inv = (f32(1.0) / f32(10000.0) ** (np.arange(0, 16, 2, dtype=f32) / f32(16))).astype(f32)
    angle = (inv[:, None] * np.arange(N, dtype=f32)[None, :]).astype(f32)
    cos = np.tile(cat([np.cos(angle), np.cos(angle)]), (8, 1))
    sin = np.tile(cat([-np.sin(angle), np.sin(angle)]), (8, 1))
    parity = (np.arange(P) // 16) % 2
    blocks = {"ident": np.eye(P), "ones": np.ones((P, P)), "lower": np.triu(np.ones((P, P)), 1),
              "trig": cat([cos, sin], axis=1), "par": np.stack([1 - parity, parity], axis=1),
              "iota16": np.tile(np.arange(16), (P, 1)), "iota32": np.tile(np.arange(32), (P, 1)),
              "pidx": np.arange(P)[:, None], "tidx": np.tile(np.arange(NT), (P, 1))}
    consts = cat([blocks[n].astype(f32) for n in CONSTS], axis=1)
    arrays = {
        "x": a["x"].reshape(T, D), "condT": a["cond_1024"].T, "cols": cols, "consts": consts,
        "l0_mod": cat([l0("Wg").T, l0("Wb").T], axis=1), "l0_w": wqkv.T, "l0_wp": l0("Wp").T,
        "l0_bp": l0("bp")[None, :],
        "l1_mod": l1("W_ada").T, "l1_w": l1("Wqkv").T, "l1_wout": l1("Wout").T, "l1_wgate": l1("Wgate").T,
        "l1_fc1": l1("fc1s").transpose(0, 2, 1), "l1_fc2": l1("fc2s").transpose(0, 2, 1),
        "l1_b1": l1("b1s").reshape(E8, FJ, P).transpose(0, 2, 1), "l1_b2": l1("b2s")[:, None, :],
        "l2_mod": l2("W_mod"), "l2_w": l2("W_qkv"), "l2_wout": l2("W_out"), "l2_w1": l2("W1"), "l2_w2": l2("W2"),
        "l3_mod1": cat([l3("t1_w1"), l3("t2_w1")]), "l3_mod2": cat([l3("t1_w2"), l3("t2_w2")]),
        "l3_w": cat([l3("wq"), l3("wk"), rotated(l3("wq")), rotated(l3("wk")), l3("wv")], axis=1),
        "l3_wo": l3("wo"), "l3_bo": l3("bo")[None, :],
        "l3_gate": l3("w_gate"), "l3_up": l3("w_up"), "l3_down": l3("w_down")}
    return {k: np.ascontiguousarray(v) for k, v in arrays.items()}


def kernel(**inputs):
    import concourse.bacc as bacc
    from concourse.bass_utils import run_bass_kernel_spmd

    nc = bacc.Bacc("TRN2", target_bir_lowering=False, num_devices=1)
    arrays = host_arrays(inputs)
    A = {k: nc.dram_tensor("in_" + k, v.shape, FP32, kind="ExternalInput").ap() for k, v in arrays.items()}
    out = nc.dram_tensor("out", (T, D), FP32, kind="ExternalOutput").ap()
    build_program(nc, A, out)
    r = run_bass_kernel_spmd(nc, [{"in_" + k: v for k, v in arrays.items()}], core_ids=[0])
    return r.results[0]["out"].reshape(B, N, D)
```

```python
import numpy as np
from contextlib import ExitStack
from math import prod

import concourse.bass as bass
from concourse import mybir

FP32 = mybir.dt.float32
BF16 = mybir.dt.bfloat16
I32 = mybir.dt.int32
ALU = mybir.AluOpType
ACT = mybir.ActivationFunctionType
AX = mybir.AxisListType

P = 128
B, N, D = 64, 64, 256
T = B * N
NT = T // P
KC = D // P
H = 16
HJ = H // 2
F = 1024
FJ = F // P
E8 = 8
CAP = T // E8
NG = T // 512
ROW = D + E8
EPS = 1e-5

COLS = {}
_at = 0
for _name, _n in [("l0_g", 2), ("l0_b", 2), ("l0_bgb", 4), ("l0_bqk", 4), ("l0_bv", 2),
                  ("l1_bada", 2), ("l1_g", 2), ("l1_b", 2), ("l1_qn", 4), ("l1_mlp", 4),
                  ("l2_bmod", 12), ("l2_bout", 2), ("l2_b1", 8), ("l2_b2", 2),
                  ("l3_w1", 2), ("l3_w2", 2), ("l3_tb1", 4), ("l3_tb2", 8),
                  ("l3_bqk", 4), ("l3_bv", 2)]:
    COLS[_name] = (_at, _n)
    _at += _n
NCOL = _at

TABS = ["g0", "b0", "g1", "b1", "g2", "b2", "gate2", "g2f", "b2f", "gate2f", "g3", "b3", "g3f", "b3f"]
LAST_STAGE = 8

CONSTS = {}
_at = 0
for _name, _n in [("ident", P), ("ones", P), ("lower", P), ("trig", 2 * N), ("par", 2), ("iota16", 16),
                  ("iota32", 32), ("pidx", 1), ("tidx", NT)]:
    CONSTS[_name] = (_at, _n)
    _at += _n
NCONST = _at


class Chain:

    def __init__(self, eng, sem):
        self.eng, self.sem, self.n = eng, sem, 0

    def reset(self):
        self.eng.sem_clear(self.sem)
        self.n = 0

    def link(self, ins):
        self.n += 1
        ins.then_inc(self.sem, 1)
        self.eng.wait_ge(self.sem, self.n)


class Signal:

    def __init__(self, sem, base):
        self.sem, self.base = sem, base


def after(eng, signal, count):
    if isinstance(count, int) and count <= 0:
        return
    eng.wait_ge(signal.sem, count + signal.base)


def after_all(eng, done, waits):
    values = []
    for signal, count in waits:
        if isinstance(count, int):
            if count > 0:
                values.append((signal, count + signal.base))
        else:
            values.append((signal, eng.to_reg(count + signal.base)))
    eng.wait_ge(done, 1)
    for signal, value in values:
        eng.wait_ge(signal.sem, value)


def tiles(eng, count, first, step, last=None):
    first()
    step(0, 3, False)
    with eng.Fori(1, count - 3) as t:
        step(t, 3, True)
    for t in range(count - 3, count):
        step(t, count - 1 - t, True)
    if last:
        last()


def pairs(eng, count, first, step):
    first()
    step(0, 0, 0, 2)
    with eng.Fori(0, (count - 4) // 2) as i:
        step(i * 2 + 1, 1, i, 2)
        step(i * 2 + 2, 0, i + 1, 2)
    for t in range(count - 3, count):
        step(t, t % 2, t // 2, min(2, count - 1 - t))


def build_program(nc, A, out, stage=LAST_STAGE):
    ctx = ExitStack()
    with ctx:
        def sb(name, shape, dt=FP32):
            return ctx.enter_context(nc.sbuf_tensor(name, shape, dt))

        def sem(name):
            return ctx.enter_context(nc.semaphore(name))

        def sems(prefix, names):
            return {n: sem(f"{prefix}_{n}") for n in names.split()}

        shared = {}

        def signals(names, total):
            out = {}
            for n in names.split():
                if n not in shared:
                    shared[n] = [sem(n), 0]
                out[n] = Signal(*shared[n])
                shared[n][1] += total
            return out

        x = sb("x", [P, NT, D])
        col = sb("col", [P, NCOL])
        tab = sb("tab", [P, len(TABS), KC, B])
        gates = sb("gates", [P, NT, E8])
        moments = sb("moments", [P, NT, 2])
        rstd = sb("rstd", [P, NT])
        stat6 = sb("stat6", [P, 4, 6])
        mv = sb("mv", [P, 4, 2])
        newton = sb("newton", [P, 4, NT + 1])
        bias_row = sb("bias_row", [P, 2, D])
        r1 = sb("r1", [P, 12288])
        r2 = sb("r2", [P, 9216])
        work = sb("work", [P, 11264])

        def c(name, i=0, n=1):
            at, _ = COLS[name]
            return col[:, at + i:at + i + n]

        def table(name):
            return tab[:, TABS.index(name), :, :]

        class Region:

            def __init__(self, region):
                self.region, self.at = region, 0

            def take(self, *shape):
                n = prod(shape)
                ap = self.region[:, self.at:self.at + n]
                self.at += n
                assert self.at <= self.region.shape[1], self.at
                if len(shape) == 2:
                    ap = ap.rearrange("p (a b) -> p a b", b=shape[1])
                if len(shape) == 3:
                    ap = ap.rearrange("p (a b c) -> p a b c", b=shape[1], c=shape[2])
                return ap

        R = Region(r1)
        l0_w, l0_wp = R.take(KC, 768), R.take(KC, D)
        l1_w, l1_wout, l1_wgate = R.take(KC, 3 * F), R.take(FJ, D), R.take(KC, E8)
        R = Region(r1)
        l2_w, l2_wout, l2_w1, l2_w2 = R.take(KC, 3 * F), R.take(FJ, D), R.take(KC, F), R.take(FJ, D)
        R = Region(r2)
        m0, m1, m2 = R.take(KC, 512), R.take(KC, D), R.take(KC, 1536)
        m3a, m3b = R.take(2 * KC, D), R.take(2 * KC, 512)
        R = Region(r2)
        fc1 = [R.take(KC, F) for _ in range(2)]
        fc2 = [R.take(FJ, D) for _ in range(2)]
        R = Region(r2)
        l3_w, l3_wo = R.take(KC, 768), R.take(KC, D)
        l3_gate, l3_up, l3_down = R.take(KC, F), R.take(KC, F), R.take(FJ, D)

        def pb(name, banks):
            return ctx.enter_context(nc.psum_tensor(name, [P, 512 * banks], FP32))

        psS, psP, psO, psW0, psW1 = pb("psS", 2), pb("psP", 2), pb("psO", 2), pb("psW0", 1), pb("psW1", 1)

        gather_table = nc.dram_tensor("gather_table", [T, ROW], FP32, kind="Internal").ap()
        moe_sum = nc.dram_tensor("moe_sum", [T, D], FP32, kind="Internal").ap()
        mod_rows = nc.dram_tensor("mod_rows", [B, 2 * D], FP32, kind="Internal").ap()
        slot_token = nc.dram_tensor("slot_token", [E8 * CAP], I32, kind="Internal").ap()

        ld = sems("ld", "small modw x0 x1 x2 x3 back0 back1 back2 back3 l0 l1 l2 l3 rows")
        st = sems("st", "out tab gates idx rows")
        chain_dve = sem("chain_dve")
        su = sems("su", "mm silu table hidden mm2 ones center turned_rows rows")

        class Attention:

            def __init__(self, li):
                self.li = li
                self.wide = li in (1, 2)
                W = Region(work)
                self.xn = W.take(D)
                self.hT = W.take(KC, P)
                self.tmpT = W.take(KC, P)
                self.qk = W.take(16, P) if self.wide else W.take(4, P)
                self.v = W.take(F) if self.wide else W.take(H, 17)
                self.E = W.take(16, N)
                self.PT = W.take(HJ, P)
                self.mx = W.take(16)
                self.rs = W.take(16)
                self.oT = W.take(FJ, P) if self.wide else W.take(KC, P)
                if li == 1:
                    self.sq = [W.take(8, 64) for _ in range(2)]
                    self.qn = [W.take(8, 64) for _ in range(4)]
                    self.ss33 = W.take(33)
                    self.ss = self.ss33[:, 0:32].rearrange("p (a b) -> p a b", b=8)
                if self.wide:
                    self.x1 = W.take(D)
                    self.x1T = W.take(KC, P)
                if li == 1:
                    self.rows = W.take(2 * D)
                    self.rstd0 = W.take(NT)
                else:
                    self.qe, self.qo = W.take(KC, P), W.take(KC, P)
                    self.o16 = W.take(D)
                    self.rot = W.take(4, P)
                    self.rot2 = W.take(4, P)
                self.g, self.b = table(f"g{li}"), table(f"b{li}")
                self.s = signals("xn a h s0 s1 sub0 sub1 exp0 exp1 ta tb pta ptb pv ote y xupd v"
                              + {0: " qk qke mask hr0 hr1 vp on ot xb",
                                 1: " prob0 prob1 rsum0 rsum1 i0 i1 i2 i3 cp0 cp1 cp2 cp3 sq0 sq1 sq2 sq3"
                                    " r0 r1 r2 r3 n0 n1 n2 n3 t0 t1 t2 t3 e0 e1 e2 e3 v0 v1 v0e x1t x1e lg gate sn",
                                 2: " prob0 prob1 rsum0 rsum1 i0 i1 i2 i3 e0 e1 e2 e3 v0 v1 v0e yt bk",
                                 3: " qk qke mask hr0 hr1 vp on ot xb"}[li], NT)
                if li == 1:
                    self.s |= signals("rows_in", NT * 32)
                self.loads = {0: 2, 1: 3, 2: 4, 3: 5}[li]
                self.ready = {0: ld["l0"], 1: ld["l1"], 2: ld["l2"], 3: ld["l3"]}[li]

        def pe_transpose_x(pe, L, n):
            after(pe, L.s["xn"], n + 1)
            after(pe, L.s["v" if L.wide else "h"], n)
            for k in range(KC):
                ins = nc.tensor.transpose(psW0[:, k * P:(k + 1) * P], L.xn[:, k * P:(k + 1) * P], ident)
            ins.then_inc(L.s["a"].sem, 1)

        def pe_project(L, ps, w, lo, chunks):
            for q in range(chunks):
                for k in range(KC):
                    ins = nc.tensor.matmul(ps[:, q * P:(q + 1) * P], w[:, k, lo + q * P:lo + (q + 1) * P],
                                           L.hT[:, k, :], start=(k == 0), stop=(k == KC - 1))
            return ins

        def pe_project_tokens(L, ps, w, lo, width):
            for k in range(KC):
                ins = nc.tensor.matmul(ps[:, 0:width], L.hT[:, k, :], w[:, k, lo:lo + width],
                                       start=(k == 0), stop=(k == KC - 1))
            return ins

        def pe_narrow_qk(pe, L, n):
            after(pe, L.s["h"], n + 1)
            after(pe, L.s["v"], n)
            pe_project(L, psW1, l0_w if L.li == 0 else l3_w, 0, 4).then_inc(L.s["qk"].sem, 1)

        def pe_narrow_v(pe, L, n):
            after(pe, L.s["qke"], n + 1)
            pe_project_tokens(L, psW1, l0_w if L.li == 0 else l3_w, 512, D).then_inc(L.s["vp"].sem, 1)

        def pe_l1_qk(pe, L, n, between):
            after(pe, L.s["h"], n + 1)
            after(pe, L.s["v0e"], n)
            for i in range(4):
                if i == 2:
                    between()
                if i >= 2:
                    after(pe, L.s[f"cp{i - 2}"], n + 1)
                pe_project_tokens(L, (psW0 if i % 2 else psW1)[:, :], l1_w, 512 * i, 512).then_inc(L.s[f"i{i}"].sem, 1)

        def pe_l1_turn(pe, L, n):
            after(pe, L.s["ote"], n)
            for i in range(4):
                after(pe, L.s[f"n{i}"], n + 1)
                if i >= 2:
                    after(pe, L.s[f"e{i - 2}"], n + 1)
                at = i % 2 * 512
                for j in range(4):
                    ins = nc.tensor.transpose(psO[:, at + j * P:at + (j + 1) * P], L.qn[i][:, 2 * j:2 * j + 2, :],
                                              ident)
                ins.then_inc(L.s[f"t{i}"].sem, 1)

        def pe_l2_qk(pe, L, n, between):
            after(pe, L.s["h"], n + 1)
            after(pe, L.s["v0e"], n)
            pe_project(L, psW1, l2_w, 0, 4).then_inc(L.s["i0"].sem, 1)
            pe_project(L, psW0, l2_w, 512, 4).then_inc(L.s["i1"].sem, 1)
            between()
            after(pe, L.s["e0"], n + 1)
            pe_project(L, psW1, l2_w, 1024, 4).then_inc(L.s["i2"].sem, 1)
            after(pe, L.s["e1"], n + 1)
            pe_project(L, psW0, l2_w, 1536, 4).then_inc(L.s["i3"].sem, 1)

        def pe_wide_v(pe, L, n, i):
            w, k_out = (l1_w, "cp") if L.li == 1 else (l2_w, "e")
            after(pe, L.s[f"{k_out}{i + 2}"], n + 1)
            pe_project_tokens(L, (psW1, psW0)[i], w, 2048 + 512 * i, 512).then_inc(L.s[f"v{i}"].sem, 1)

        def pe_scores(pe, L, t):
            ready = {0: ("mask",), 1: ("e3",), 2: ("e2", "e3"), 3: ("mask",)}[L.li]
            after_all(pe, su["table"], [(L.s[r], t + 1) for r in ready] + [(L.s["sub1"], t)])
            if L.wide:
                for j in range(HJ):
                    for b in range(2):
                        for hp in range(2):
                            rows = slice(64 * hp, 64 * hp + 64)
                            ins = nc.tensor.matmul(psS[rows, (2 * j + b) * N:(2 * j + b + 1) * N],
                                                   L.qk[rows, j, b * N:(b + 1) * N],
                                                   L.qk[rows, HJ + j, b * N:(b + 1) * N], start=True, stop=True)
                    if j % 4 == 3:
                        ins.then_inc(L.s[f"s{j // 4}"].sem, 1)
                return
            for r in range(4):
                if r >= 2:
                    after_all(pe, su["table"], [(L.s[f"hr{r - 2}"], t + 1)])
                rows = slice(32 * r, 32 * r + 32)
                for ch in range(KC):
                    for b in range(2):
                        at = narrow_block(r, ch, b) * N
                        for hp, q in enumerate((L.qe, L.qo)):
                            ins = nc.tensor.matmul(psS[64 * hp:64 * hp + 64, at:at + N], q[rows, ch, b * N:(b + 1) * N],
                                                   L.qk[rows, KC + ch, b * N:(b + 1) * N], start=True, stop=True)
                ins.then_inc(L.s[f"hr{r}" if r < 2 else f"s{r - 2}"].sem, 1)

        def narrow_block(r, ch, b):
            return (((r % 2) * 2 + r // 2) * 2 + ch) * 2 + b

        def narrow_pair(j):
            rp, rh, ch = j // 4, (j // 2) % 2, j % 2
            return 8 * ch + 2 * (2 * rh + rp)

        def pe_transpose_probs(pe, L, t):
            after(pe, L.s[{0: "ptb", 1: "gate", 2: "xupd", 3: "ptb"}[L.li]], t)
            for j in range(HJ):
                if j % 4 == 0:
                    after(pe, L.s[("prob" if L.wide else "exp") + str(j // 4)], t + 1)
                ins = nc.tensor.transpose(psP[:, j * P:(j + 1) * P], L.E[:, 2 * j:2 * j + 2, :], ident)
                if j == 3:
                    ins.then_inc(L.s["ta"].sem, 1)
            ins.then_inc(L.s["tb"].sem, 1)

        def pe_narrow_pv(pe, L, t):
            after_all(pe, su["table"], [(L.s["v"], t + 1), (L.s["on"], t), (L.s["pta"], t + 1)])
            for j in range(HJ):
                if j == 4:
                    after_all(pe, su["table"], [(L.s["ptb"], t + 1)])
                for hp in range(2):
                    for b in range(2):
                        rows = slice(64 * b, 64 * b + 64)
                        h = narrow_pair(j) + hp
                        ins = nc.tensor.matmul(psO[rows, h * 17:(h + 1) * 17], L.PT[rows, j, 64 * hp:64 * hp + 64],
                                               L.v[rows, h, :], start=True, stop=True)
            ins.then_inc(L.s["pv"].sem, 1)

        def pe_wide_pv(pe, L, t):
            after_all(pe, su["table"], [(L.s["v"], t + 1), (L.s["pta"], t + 1)])
            for j in range(HJ):
                if j == 4:
                    after_all(pe, su["table"], [(L.s["ptb"], t + 1)])
                for b in range(2):
                    rows = slice(64 * b, 64 * b + 64)
                    for hp in range(2):
                        h = 2 * j + hp
                        ins = nc.tensor.matmul(psO[64 * hp:64 * hp + 64, b * 512 + j * N:b * 512 + (j + 1) * N],
                                               L.v[rows, h * 64:(h + 1) * 64], L.PT[rows, j, 64 * hp:64 * hp + 64],
                                               start=True, stop=True)
            ins.then_inc(L.s["pv"].sem, 1)

        def pe_turn_out(pe, L, t):
            if L.wide:
                after(pe, L.s["xupd" if L.li == 1 else "yt"], t + 1)
                for k in range(KC):
                    ins = nc.tensor.transpose(psP[:, 512 + k * P:512 + (k + 1) * P],
                                              L.x1[:, k * P:(k + 1) * P] if L.li == 1 else L.x1T[:, k, :], ident)
                ins.then_inc(L.s["x1t" if L.li == 1 else "bk"].sem, 1)
                return
            after(pe, L.s["xupd"], t)
            after(pe, L.s["on"], t + 1)
            for k in range(KC):
                ins = nc.tensor.transpose(psO[:, 512 + k * P:512 + (k + 1) * P], L.o16[:, k * P:(k + 1) * P],
                                          ident)
            ins.then_inc(L.s["ot"].sem, 1)

        def pe_narrow_y(pe, L, t):
            w = l0_wp if L.li == 0 else l3_wo
            after(pe, L.s["ote"], t + 1)
            for k in range(KC):
                ins = nc.tensor.matmul(psO[:, 512:512 + D], L.oT[:, k, :], w[:, k, :], start=(k == 0), stop=(k == KC - 1))
            ins.then_inc(L.s["y"].sem, 1)

        def pe_wide_y(pe, L, t):
            after(pe, L.s["ote"], t + 1)
            if L.li == 1:
                for j in range(FJ):
                    ins = nc.tensor.matmul(psP[:, 0:D], L.oT[:, j, :], l1_wout[:, j, :], start=(j == 0), stop=(j == FJ - 1))
            else:
                for q in range(KC):
                    for j in range(FJ):
                        ins = nc.tensor.matmul(psP[:, q * P:(q + 1) * P], l2_wout[:, j, q * P:(q + 1) * P], L.oT[:, j, :],
                                               start=(j == 0), stop=(j == FJ - 1))
            ins.then_inc(L.s["y"].sem, 1)

        def pe_l1_logits(pe, L, t):
            after(pe, L.s["x1e"], t + 1)
            for k in range(KC):
                ins = nc.tensor.matmul(psP[:, 0:E8], L.x1T[:, k, :], l1_wgate[:, k, :], start=(k == 0), stop=(k == KC - 1))
            ins.then_inc(L.s["lg"].sem, 1)

        def pe_attention(pe, L):
            pe.wait_ge(L.ready, 16 * L.loads)
            if not L.wide:
                pe.wait_ge(su["ones"], 1 if L.li == 0 else 2)
            if L.li == 1:
                pe.wait_ge(su["center"], KC)

            wide_qk = pe_l1_qk if L.li == 1 else pe_l2_qk

            def first():
                pe_transpose_x(pe, L, 0)
                if L.wide:
                    wide_qk(pe, L, 0, lambda: None)
                    pe_wide_v(pe, L, 0, 0)
                    pe_wide_v(pe, L, 0, 1)
                    if L.li == 1:
                        pe_l1_turn(pe, L, 0)
                else:
                    pe_narrow_qk(pe, L, 0)
                    pe_narrow_v(pe, L, 0)

            def step(t, ahead, behind):
                def finish_before():
                    if L.li == 1 and behind:
                        pe_l1_logits(pe, L, t - 1)
                    if L.li == 2 and behind:
                        pe_turn_out(pe, L, t - 1)

                if ahead:
                    pe_transpose_x(pe, L, t + 1)
                pe_scores(pe, L, t)
                if behind and L.li != 2:
                    pe_turn_out(pe, L, t - 1)
                if L.wide:
                    if ahead:
                        wide_qk(pe, L, t + 1, finish_before)
                    else:
                        finish_before()
                    pe_transpose_probs(pe, L, t)
                    if ahead:
                        pe_wide_v(pe, L, t + 1, 0)
                    pe_wide_pv(pe, L, t)
                    if ahead:
                        pe_wide_v(pe, L, t + 1, 1)
                        if L.li == 1:
                            pe_l1_turn(pe, L, t + 1)
                    pe_wide_y(pe, L, t)
                    return
                if ahead:
                    pe_narrow_qk(pe, L, t + 1)
                pe_transpose_probs(pe, L, t)
                if behind:
                    pe_narrow_y(pe, L, t - 1)
                pe_narrow_pv(pe, L, t)
                if ahead:
                    pe_narrow_v(pe, L, t + 1)

            def last():
                pe_turn_out(pe, L, NT - 1)
                if L.li == 1:
                    pe_l1_logits(pe, L, NT - 1)
                if not L.wide:
                    pe_narrow_y(pe, L, NT - 1)

            tiles(pe, NT, first, step, last)

        def batches(ap, n, count=2):
            return ap[:, :, bass.ds(n * count, count)].unsqueeze(3).broadcast_to([P, KC, count, N])

        def four(ap):
            return ap.rearrange("p k (b n) -> p k b n", n=N)

        def dve_rsqrt(ch, out, var):
            shape = var.shape
            n = prod(shape[1:])
            v, y, q, g = (newton[:, i, 0:n] for i in range(4))
            if len(shape) == 3:
                v3, o3 = v.rearrange("p (a b) -> p a b", b=shape[2]), y.rearrange("p (a b) -> p a b", b=shape[2])
            else:
                v3, o3 = v, y
            ch.link(nc.vector.tensor_scalar(v3, var, EPS, None, ALU.add))
            ch.link(nc.vector.tensor_scalar(g.bitcast(I32), v.bitcast(I32), 1, None, ALU.logical_shift_right))
            ch.link(nc.vector.tensor_scalar(y.bitcast(I32), g.bitcast(I32), -1.0, float(0x5F3759DF), ALU.mult, ALU.add))
            for i in range(3):
                ch.link(nc.vector.tensor_tensor(q, y, y, ALU.mult))
                ch.link(nc.vector.tensor_tensor(q, q, v, ALU.mult))
                ch.link(nc.vector.tensor_scalar(q, q, -0.5, 1.5, ALU.mult, ALU.add))
                if i < 2:
                    ch.link(nc.vector.tensor_tensor(y, y, q, ALU.mult))
            ch.link(nc.vector.tensor_tensor(out, o3, q.rearrange("p (a b) -> p a b", b=shape[2])
                                            if len(shape) == 3 else q, ALU.mult))

        def dve_moments(ch, t):
            ch.link(nc.vector.bn_stats(stat6[:, 0, :], x[:, t, :]))
            ch.link(nc.vector.bn_aggr(mv[:, 0, :], stat6[:, 0, :]))
            ch.link(nc.vector.tensor_copy(moments[:, t, :], mv[:, 0, :]))

        def dve_group_moments(ch, t):
            for r in range(4):
                ins = nc.vector.bn_stats(stat6[:, r, :], x[:, t * 4 + r, :])
            ch.link(ins)
            for r in range(4):
                ins = nc.vector.bn_aggr(mv[:, r, :], stat6[:, r, :])
            ch.link(ins)
            ch.link(nc.vector.tensor_copy(moments[:, bass.ds(t * 4, 4), :], mv[:, :, :]))

        def dve_all_moments(v, ch, loads):
            ch.reset()
            for i in range(NG):
                if i % 2 == 0:
                    v.wait_ge(loads[i // 2], 16)
                dve_group_moments(ch, i)

        def dve_rstd(ch, rms=False):
            mean, var = moments[:, :, 0], moments[:, :, 1]
            if rms:
                ch.link(nc.vector.tensor_tensor(rstd[:, :], mean, mean, ALU.mult))
                ch.link(nc.vector.tensor_tensor(rstd[:, :], rstd[:, :], var, ALU.add))
                var = rstd[:, :]
            dve_rsqrt(ch, rstd[:, :], var)

        def dve_normalise(out, src, n, rms=False):
            if rms:
                return nc.vector.tensor_scalar(out, src, rstd[:, bass.ds(n, 1)], None, ALU.mult)
            return nc.vector.tensor_scalar(out, src, moments[:, n, 0:1], rstd[:, bass.ds(n, 1)],
                                           ALU.subtract, ALU.mult)

        def dve_norm(v, ch, L, n):
            after(v, L.s["a"], n)
            dve_normalise(L.xn, x[:, n, :], n, rms=L.li == 3).then_inc(L.s["xn"].sem, 1)

        def dve_modulate(v, ch, L, n):
            after(v, L.s["a"], n + 1)
            ps = psW0[:, 0:D].rearrange("p (k b n) -> p k b n", k=KC, n=N)
            ch.link(nc.vector.tensor_tensor(four(L.tmpT), ps, batches(L.g, n), ALU.mult))
            after(v, L.s["v1" if L.wide else "vp"], n)
            nc.vector.tensor_tensor(four(L.hT), four(L.tmpT), batches(L.b, n), ALU.add).then_inc(L.s["h"].sem, 1)

        def halves(ap):
            return [ap[:, 0:8], ap[:, 8:16]]

        def dve_softmax(v, ch, L, t):
            for i in range(2):
                ps = psS[:, 512 * i:512 * i + 512].rearrange("p (a b) -> p a b", b=N)
                mx = halves(L.mx)[i]
                after(v, L.s[f"s{i}"], t + 1)
                ch.link(nc.vector.tensor_reduce(mx, ps, AX.X, ALU.max))
                after(v, L.s["tb" if i else "ta"], t)
                nc.vector.tensor_tensor(L.E[:, 8 * i:8 * i + 8, :], ps, mx.unsqueeze(2).broadcast_to([P, 8, N]),
                                        ALU.subtract).then_inc(L.s[f"sub{i}"].sem, 1)

        def dve_prob_sums(v, ch, L, t):
            for i in range(2):
                mx, rs = halves(L.mx)[i], halves(L.rs)[i]
                after(v, L.s[f"exp{i}"], t + 1)
                ch.link(nc.vector.tensor_reduce(mx, L.E[:, 8 * i:8 * i + 8, :], AX.X, ALU.add))
                after(v, L.s[f"prob{i}"], t)
                nc.vector.reciprocal(rs, mx).then_inc(L.s[f"rsum{i}"].sem, 1)

        def dve_narrow_qk(v, ch, L, n):
            after(v, L.s["qk"], n + 1)
            ps = psW1[:, :].rearrange("p (a b) -> p a b", b=P)

            def bias(name):
                return c(name, 0, 4).unsqueeze(2).broadcast_to([P, 4, P])

            if L.li == 0:
                after(v, L.s["s1"], n)
                nc.vector.tensor_tensor(L.qk, ps, bias("l0_bqk"), ALU.add).then_inc(L.s["qke"].sem, 1)
                return

            def angles(i):
                return trig[:, i * N:(i + 1) * N].unsqueeze(1).broadcast_to([P, 8, N])

            def eight(ap):
                return ap.rearrange("p a (b n) -> p (a b) n", n=N)

            ch.link(nc.vector.tensor_tensor(L.rot2, ps, bias("l3_bqk"), ALU.add))
            ch.link(nc.vector.stream_shuffle(L.rot, L.rot2, [i ^ 8 for i in range(32)]))
            ch.link(nc.vector.tensor_tensor(eight(L.rot), eight(L.rot), angles(1), ALU.mult))
            ch.link(nc.vector.tensor_tensor(eight(L.rot2), eight(L.rot2), angles(0), ALU.mult))
            after(v, L.s["s1"], n)
            nc.vector.tensor_tensor(L.qk, L.rot, L.rot2, ALU.add).then_inc(L.s["qke"].sem, 1)

        def dve_narrow_o(v, ch, L, t):
            after(v, L.s["pv"], t + 1)
            o = psO[:, 0:272].rearrange("p (h d) -> p h d", d=17)
            ch.link(nc.vector.reciprocal(L.rs.unsqueeze(2), o[:, :, 16:17]))
            nc.vector.tensor_tensor(L.o16.rearrange("p (h d) -> p h d", d=16), o[:, :, 0:16],
                                    L.rs.unsqueeze(2).broadcast_to([P, H, 16]), ALU.mult).then_inc(L.s["on"].sem, 1)

        def dve_narrow_x(v, ch, L, t):
            after(v, L.s["xb"], t + 1)
            after(v, L.s["y"], t + 1)
            nc.vector.tensor_tensor(x[:, t, :], x[:, t, :], psO[:, 512:512 + D], ALU.add).then_inc(L.s["xupd"].sem, 1)
            after_all(v, su["table"], [(L.s["xupd"], t + 1)])
            dve_moments(ch, t)

        def dve_l1_qk(v, ch, L, n, norm_too, between=None):
            for i in range(4):
                after(v, L.s[f"sq{i}"], n + 1)
                ins = nc.vector.tensor_reduce(L.ss[:, i, :], L.sq[i % 2], AX.X, ALU.add)
                ins.then_inc(L.s[f"r{i}"].sem, 1)
                if i == 0 and between:
                    between()
                if i == 1 and norm_too:
                    dve_second_norm(v, ch, L, n + 2)
                    nc.vector.tensor_copy(L.ss33[:, 32:33], mv[:, 0, 1:2])
            after(v, L.s["r3"], n + 1)
            ch.link(nc.vector.tensor_scalar(L.ss, L.ss, 1.0 / 64, None, ALU.mult))
            dve_rsqrt(ch, L.ss33, L.ss33)
            if norm_too:
                nc.vector.tensor_copy(rstd[:, bass.ds(n + 2, 1)], L.ss33[:, 32:33])
            for i in range(4):
                nc.vector.tensor_tensor(L.qn[i], L.qn[i], L.ss[:, i, :].unsqueeze(2).broadcast_to([P, 8, 64]),
                                        ALU.mult).then_inc(L.s[f"n{i}"].sem, 1)

        def dve_second_norm(v, ch, L, n):
            after(v, L.s["rows_in"], (n + 1) * 32)
            tmp = L.tmpT.rearrange("p k n -> p (k n)")
            ch.link(nc.vector.tensor_scalar(tmp, x[:, n, :], moments[:, n, 0:1], L.rstd0[:, bass.ds(n, 1)],
                                            ALU.subtract, ALU.mult))
            ch.link(nc.vector.tensor_tensor(tmp, tmp, L.rows[:, 0:D], ALU.mult))
            ch.link(nc.vector.tensor_tensor(tmp, tmp, L.rows[:, D:2 * D], ALU.add))
            nc.vector.tensor_tensor(x[:, n, :], x[:, n, :], tmp, ALU.add).then_inc(L.s["sn"].sem, 1)
            after_all(v, su["table"], [(L.s["sn"], n + 1)])
            dve_moments(ch, n)

        def dve_l2_qk(v, ch, L, n, between=None):
            after(v, L.s["s1"], n)
            for i in (1, 3):
                if i == 3 and between:
                    between()
                after(v, L.s[f"i{i}"], n + 1)
                nc.vector.tensor_copy(L.qk[:, 4 * i:4 * i + 4, :], psW0[:, :].rearrange("p (a b) -> p a b", b=P)
                                      ).then_inc(L.s[f"e{i}"].sem, 1)

        def dve_l1_x1(v, ch, L, t):
            after(v, L.s["y"], t + 1)
            after(v, L.s["x1t"], t)
            if not isinstance(t, int) or t > 0:
                v.wait_ge(st["tab"], t * 32)
            nc.vector.tensor_tensor(L.x1, x[:, t, :], psP[:, 0:D], ALU.add).then_inc(L.s["xupd"].sem, 1)

        def dve_l1_gates(v, ch, L, t):
            after(v, L.s["lg"], t + 1)
            nc.vector.tensor_copy(gates[:, t, :], psP[:, 0:E8]).then_inc(L.s["gate"].sem, 1)

        def dve_l2_y(v, ch, L, t):
            after(v, L.s["y"], t + 1)
            yT = L.x1T
            ps = psP[:, 0:D].rearrange("p (k n) -> p k n", n=P)
            ch.link(nc.vector.tensor_tensor(yT, ps, c("l2_bout", 0, 2).unsqueeze(2).broadcast_to([P, KC, P]), ALU.add))
            nc.vector.tensor_tensor(four(yT), four(yT), batches(table("gate2"), t), ALU.mult).then_inc(L.s["yt"].sem, 1)

        def dve_l2_x(v, ch, L, t):
            after(v, L.s["bk"], t + 1)
            nc.vector.tensor_tensor(x[:, t, :], x[:, t, :], psP[:, 512:512 + D], ALU.add).then_inc(L.s["xupd"].sem, 1)
            after_all(v, su["table"], [(L.s["xupd"], t + 1)])
            dve_moments(ch, t)

        def dve_attention(v, ch, L):
            qk = dve_l2_qk if L.wide else dve_narrow_qk

            def first():
                ch.reset()
                if L.li == 1:
                    dve_rsqrt(ch, L.rstd0, moments[:, :, 1])
                    for n in range(2):
                        dve_second_norm(v, ch, L, n)
                    dve_rsqrt(ch, rstd[:, 0:2], moments[:, 0:2, 1])
                else:
                    dve_rstd(ch, rms=L.li == 3)
                dve_norm(v, ch, L, 0)
                dve_modulate(v, ch, L, 0)
                dve_norm(v, ch, L, 1)
                if L.li == 1:
                    dve_l1_qk(v, ch, L, 0, True)
                else:
                    qk(v, ch, L, 0)

            def step(t, ahead, behind):
                def gates_before():
                    if behind:
                        dve_l1_gates(v, ch, L, t - 1)

                def x_before():
                    if behind:
                        dve_l2_x(v, ch, L, t - 1)

                ch.reset()
                if ahead:
                    dve_modulate(v, ch, L, t + 1)
                if ahead >= 2:
                    dve_norm(v, ch, L, t + 2)
                dve_softmax(v, ch, L, t)
                if L.wide:
                    dve_prob_sums(v, ch, L, t)
                if L.li == 1:
                    if ahead:
                        dve_l1_qk(v, ch, L, t + 1, ahead == 3, gates_before)
                    else:
                        gates_before()
                    dve_l1_x1(v, ch, L, t)
                elif L.li == 2:
                    if ahead:
                        dve_l2_qk(v, ch, L, t + 1, x_before)
                    else:
                        x_before()
                    dve_l2_y(v, ch, L, t)
                else:
                    if ahead:
                        dve_narrow_qk(v, ch, L, t + 1)
                    if behind:
                        dve_narrow_x(v, ch, L, t - 1)
                    if L.li == 0 and isinstance(t, int) and t >= NT - KC - 1 and t < NT - 1:
                        dve_center(v, ch, t - (NT - KC - 1))
                    dve_narrow_o(v, ch, L, t)

            def last():
                {0: dve_narrow_x, 1: dve_l1_gates, 2: dve_l2_x, 3: dve_narrow_x}[L.li](v, ch, L, NT - 1)

            tiles(v, NT, first, step, last)

        def act_l1_square(a, L, n, i):
            after(a, L.s[f"cp{i}"], n + 1)
            after(a, L.s[f"r{(i + 2) % 4}"], n if i < 2 else n + 1)
            nc.scalar.activation(L.sq[i % 2], L.qn[i], ACT.Square).then_inc(L.s[f"sq{i}"].sem, 1)

        def act_qk(a, L, n):
            if L.li == 1:
                for i in range(4):
                    after(a, L.s[f"i{i}"], n + 1)
                    after(a, L.s[f"t{i}"], n)
                    ps = (psW0 if i % 2 else psW1)[:, :].rearrange("p (a b) -> p a b", b=64)
                    nc.scalar.activation(L.qn[i], ps, ACT.Copy).then_inc(L.s[f"cp{i}"].sem, 1)
                    if i < 3:
                        act_l1_square(a, L, n, i)
            if L.li == 2:
                for i in (0, 2):
                    after(a, L.s[f"i{i}"], n + 1)
                    if i == 0:
                        after(a, L.s["s1"], n)
                    nc.scalar.activation(L.qk[:, 4 * i:4 * i + 4, :], psW1[:, :].rearrange("p (a b) -> p a b", b=P),
                                         ACT.Copy).then_inc(L.s[f"e{i}"].sem, 1)

        def act_l1_turned(a, L, n, i):
            after(a, L.s[f"t{i}"], n + 1)
            if i == 0:
                after(a, L.s["s1"], n)
            ps = psO[:, i % 2 * 512:i % 2 * 512 + 512].rearrange("p (a b) -> p a b", b=P)
            g = 2 * (i // 2)
            nc.scalar.activation(L.qk[:, 4 * i:4 * i + 4, :], ps, ACT.Identity, bias=c("l1_qn", g + 1),
                                 scale=c("l1_qn", g)).then_inc(L.s[f"e{i}"].sem, 1)

        def act_v(a, L, n):
            if L.wide:
                after(a, L.s["v0"], n + 1)
                after(a, L.s["pv"], n)
                nc.scalar.activation(L.v[:, 0:512], psW1[:, :], ACT.Copy).then_inc(L.s["v0e"].sem, 1)
                after(a, L.s["v1"], n + 1)
                nc.scalar.activation(L.v[:, 512:1024], psW0[:, :], ACT.Copy).then_inc(L.s["v"].sem, 1)
            else:
                after(a, L.s["vp"], n + 1)
                after(a, L.s["pv"], n)
                nc.scalar.activation(L.v[:, :, 0:16], psW1[:, 0:D].rearrange("p (h d) -> p h d", d=16),
                                     ACT.Copy).then_inc(L.s["v"].sem, 1)

        def act_attention(a, L):
            scale = {0: 1.0, 1: 0.125, 2: 0.125, 3: 0.25}[L.li]

            def turned(n):
                if L.li == 1:
                    for i in range(4):
                        act_l1_turned(a, L, n, i)

            def narrow_o(t):
                after(a, L.s["ot"], t + 1)
                after(a, L.s["y"], t)
                for k in range(KC):
                    ins = nc.scalar.activation(L.oT[:, k, :], psO[:, 512 + k * P:512 + (k + 1) * P], ACT.Identity,
                                               bias=c(f"l{L.li}_bv", k), scale=0.0625 if L.li == 0 else 1.0)
                ins.then_inc(L.s["ote"].sem, 1)

            def finish(t):
                if L.li == 1:
                    after(a, L.s["x1t"], t + 1)
                    nc.scalar.activation(L.x1T, psP[:, 512:512 + D].rearrange("p (k n) -> p k n", n=P),
                                         ACT.Copy).then_inc(L.s["x1e"].sem, 1)
                elif not L.wide:
                    narrow_o(t)

            def first():
                act_qk(a, L, 0)
                if L.li == 1:
                    act_l1_square(a, L, 0, 3)
                act_v(a, L, 0)
                turned(0)

            def step(t, ahead, behind):
                for i in range(2):
                    E = L.E[:, 8 * i:8 * i + 8, :]
                    after(a, L.s[f"sub{i}"], t + 1)
                    nc.scalar.activation(E, E, ACT.Exp, scale=scale).then_inc(L.s[f"exp{i}"].sem, 1)
                    if i == 0 and behind:
                        finish(t - 1)
                if ahead:
                    act_qk(a, L, t + 1)
                after(a, L.s["ta"], t + 1)
                after(a, L.s["pv"], t)
                psp = psP[:, :].rearrange("p (a b) -> p a b", b=P)
                nc.scalar.activation(L.PT[:, 0:4, :], psp[:, 0:4, :], ACT.Copy).then_inc(L.s["pta"].sem, 1)
                after(a, L.s["tb"], t + 1)
                nc.scalar.activation(L.PT[:, 4:8, :], psp[:, 4:8, :], ACT.Copy).then_inc(L.s["ptb"].sem, 1)
                if ahead and L.li == 1:
                    act_l1_square(a, L, t + 1, 3)
                if L.wide:
                    after(a, L.s["pv"], t + 1)
                    after(a, L.s["y"], t)
                    for b in range(2):
                        ins = nc.scalar.activation(L.oT[:, :, b * N:(b + 1) * N],
                                                   psO[:, b * 512:(b + 1) * 512].rearrange("p (j n) -> p j n", n=N),
                                                   ACT.Copy)
                    ins.then_inc(L.s["ote"].sem, 1)
                if ahead:
                    act_v(a, L, t + 1)
                    turned(t + 1)

            tiles(a, NT, first, step, lambda: finish(NT - 1))

        def pool_attention(g, L):
            def masks(n):
                after(g, L.s["qke"], n + 1)
                for i, q in enumerate((L.qe, L.qo)):
                    ins = nc.gpsimd.tensor_tensor(q, L.qk[:, 0:KC, :], par[:, i:i + 1].unsqueeze(2)
                                                  .broadcast_to([P, KC, P]), ALU.mult)
                ins.then_inc(L.s["mask"].sem, 1)

            def first():
                if not L.wide:
                    nc.gpsimd.memset(L.v[:, :, 16:17], 1.0).then_inc(su["ones"], 1)
                    masks(0)

            def step(t, ahead, behind):
                if L.wide:
                    for i in range(2):
                        after(g, L.s[f"rsum{i}"], t + 1)
                        E = L.E[:, 8 * i:8 * i + 8, :]
                        nc.gpsimd.tensor_tensor(E, E, halves(L.rs)[i].unsqueeze(2).broadcast_to([P, 8, N]),
                                                ALU.mult).then_inc(L.s[f"prob{i}"].sem, 1)
                    return
                if ahead:
                    masks(t + 1)
                after(g, L.s["xn"], t + 1)
                nc.gpsimd.tensor_tensor(x[:, t, :], x[:, t, :], bias_row[:, 0 if L.li == 0 else 1, :],
                                        ALU.add).then_inc(L.s["xb"].sem, 1)

            tiles(g, NT, first, step)

        class FeedForward:

            def __init__(self, kind):
                self.kind = kind
                W = Region(work)
                self.xn = W.take(4, D)
                self.stat = W.take(4, 3)
                self.gT = W.take(KC, 512)
                self.tmp = W.take(512)
                self.hid = W.take(FJ, 512)
                if kind == "moe":
                    self.xg = [W.take(4, ROW) for _ in range(2)]
                    self.y = W.take(4, D)
                    self.wcol = [W.take(4) for _ in range(2)]
                    self.b1 = [W.take(FJ) for _ in range(2)]
                    self.b2 = [W.take(D) for _ in range(2)]
                    self.gidx, self.sidx = ([W.take(4).bitcast(I32) for _ in range(2)] for _ in range(2))
                    self.w1, self.w2 = fc1, fc2
                elif kind == "l2":
                    self.yT = W.take(KC, 512)
                    self.w1, self.w2 = [l2_w1] * 2, [l2_w2] * 2
                else:
                    self.act = [W.take(512) for _ in range(2)]
                    self.w1, self.w2 = [l3_gate] * 2, [l3_down] * 2
                self.s = signals("f_xn f_a f_h f_y f_done" + {"moe": "", "l2": " f_yt f_bk", "l3": ""}[kind], NG)
                self.s |= signals("f_hd f_he" + (" f_act" if kind == "l3" else ""), NG * FJ)
                if kind == "moe":
                    self.s |= signals("f_sc", NG * 64)
                    self.s |= signals("f_in0 f_in1 f_ga0 f_ga1", NG // 2 * 64)
                    self.s |= signals("f_gi0 f_gi1 f_si0 f_si1", NG // 2 * 16)

        HB = [psP[:, 0:512], psP[:, 512:1024], psO[:, 0:512], psO[:, 512:1024]]

        def pe_ff(pe, Q):
            def turn(n):
                after(pe, Q.s["f_xn"], n + 1)
                after(pe, Q.s["f_h"], n)
                for k, ps in enumerate((psW0, psW1)):
                    for r in range(4):
                        ins = nc.tensor.transpose(ps[:, r * P:(r + 1) * P], Q.xn[:, r, k * P:(k + 1) * P], ident)
                ins.then_inc(Q.s["f_a"].sem, 1)

            def hidden(t, u, half):
                after(pe, Q.s["f_h"], t + 1)
                if Q.kind == "moe":
                    after(pe, Q.s[f"f_in{u}"], (half + 1) * 64)
                for j in range(FJ):
                    if Q.kind == "l3":
                        after(pe, Q.s["f_he"], t * FJ + (j - 1))
                        for ps, w in ((HB[j % 2], l3_gate), (HB[2 + j % 2], l3_up)):
                            for k in range(KC):
                                ins = nc.tensor.matmul(ps, w[:, k, j * P:(j + 1) * P], Q.gT[:, k, :],
                                                       start=(k == 0), stop=(k == KC - 1))
                        ins.then_inc(Q.s["f_hd"].sem, 1)
                        continue
                    after(pe, Q.s["f_he"], t * FJ + (j - 3))
                    for k in range(KC):
                        ins = nc.tensor.matmul(HB[j % 4], Q.w1[u][:, k, j * P:(j + 1) * P], Q.gT[:, k, :],
                                               start=(k == 0), stop=(k == KC - 1))
                    ins.then_inc(Q.s["f_hd"].sem, 1)
                    if Q.kind == "l2" and j == FJ // 2 and not (isinstance(t, int) and t == 0):
                        back(t - 1)

            def back(t):
                after(pe, Q.s["f_yt"], t + 1)
                for r in range(4):
                    for k in range(KC):
                        ins = nc.tensor.transpose(psS[:, r * D + k * P:r * D + (k + 1) * P],
                                                  Q.yT[:, k, r * P:(r + 1) * P], ident)
                ins.then_inc(Q.s["f_bk"].sem, 1)

            def result(t, u):
                after(pe, Q.s["f_he"], t * FJ + FJ)
                after(pe, Q.s["f_done"], t)
                if Q.kind == "l2":
                    for q in range(KC):
                        for j in range(FJ):
                            ins = nc.tensor.matmul(psS[:, q * 512:(q + 1) * 512], Q.w2[u][:, j, q * P:(q + 1) * P],
                                                   Q.hid[:, j, :], start=(j == 0), stop=(j == FJ - 1))
                    ins.then_inc(Q.s["f_y"].sem, 1)
                    return
                for r in range(4):
                    for j in range(FJ):
                        ins = nc.tensor.matmul(psS[:, r * D:(r + 1) * D], Q.hid[:, j, r * P:(r + 1) * P],
                                               Q.w2[u][:, j, :], start=(j == 0), stop=(j == FJ - 1))
                ins.then_inc(Q.s["f_y"].sem, 1)

            def step(t, u, half, more):
                hidden(t, u, half)
                if more:
                    turn(t + 1)
                result(t, u)

            pairs(pe, NG, lambda: turn(0), step)
            if Q.kind == "l2":
                back(NG - 1)

        def dve_ff(v, ch, Q):
            def norm(n, u, half):
                if Q.kind == "moe":
                    after_all(v, su["table"], [(Q.s[f"f_ga{u}"], (half + 1) * 64)])
                    for r in range(4):
                        ins = nc.vector.bn_stats(stat6[:, r, :], Q.xg[u][:, r, 0:D])
                    ch.link(ins)
                    nc.vector.tensor_copy(Q.wcol[u].unsqueeze(2), Q.xg[u][:, :, bass.ds(n + D, 1)])
                    for r in range(4):
                        ins = nc.vector.bn_aggr(Q.stat[:, r, 0:2], stat6[:, r, :])
                    ch.link(ins)
                    dve_rsqrt(ch, Q.stat[:, :, 2], Q.stat[:, :, 1])
                after(v, Q.s["f_a"], n)
                for r in range(4):
                    if Q.kind == "moe":
                        ins = nc.vector.tensor_scalar(Q.xn[:, r, :], Q.xg[u][:, r, 0:D], Q.stat[:, r, 0:1],
                                                      Q.stat[:, r, 2:3], ALU.subtract, ALU.mult)
                    else:
                        ins = dve_normalise(Q.xn[:, r, :], x[:, n * 4 + r, :], n * 4 + r, rms=Q.kind == "l3")
                    if r < 3:
                        ch.link(ins)
                ins.then_inc(Q.s["f_xn"].sem, 1)

            def modulate(n):
                after(v, Q.s["f_a"], n + 1)
                after(v, Q.s["f_hd"], n * FJ)
                for k, ps in enumerate((psW0, psW1)):
                    if Q.kind == "moe":
                        ins = nc.vector.tensor_scalar(Q.gT[:, k, :], ps[:, :], c("l1_mlp", k), c("l1_mlp", 2 + k),
                                                      ALU.mult, ALU.add)
                        if k == 0:
                            ch.link(ins)
                        continue
                    g, b = table("g2f" if Q.kind == "l2" else "g3f"), table("b2f" if Q.kind == "l2" else "b3f")

                    def of(tb):
                        return tb[:, k, bass.ds(n * 8, 8)].unsqueeze(2).broadcast_to([P, 8, N])

                    def eight(ap):
                        return ap.rearrange("p (b n) -> p b n", n=N)

                    ch.link(nc.vector.tensor_tensor(eight(Q.gT[:, k, :]), eight(ps[:, :]), of(g), ALU.mult))
                    ins = nc.vector.tensor_tensor(eight(Q.gT[:, k, :]), eight(Q.gT[:, k, :]), of(b), ALU.add)
                    if k == 0:
                        ch.link(ins)
                ins.then_inc(Q.s["f_h"].sem, 1)

            def products(t):
                for j in range(FJ):
                    after(v, Q.s["f_act"], t * FJ + (j + 1))
                    if j == 0:
                        after(v, Q.s["f_y"], t)
                    nc.vector.tensor_tensor(Q.hid[:, j, :], Q.act[j % 2], HB[2 + j % 2], ALU.mult).then_inc(Q.s["f_he"].sem, 1)

            def add(t):
                after(v, Q.s["f_bk"], t + 1)
                xs = x[:, bass.ds(t * 4, 4), :]
                nc.vector.tensor_tensor(xs, xs, psS[:, :].rearrange("p (r d) -> p r d", d=D), ALU.add
                                        ).then_inc(Q.s["f_done"].sem, 1)
                after_all(v, su["table"], [(Q.s["f_done"], t + 1)])
                dve_group_moments(ch, t)

            def result(t, u):
                after(v, Q.s["f_y"], t + 1)
                if Q.kind == "l2":
                    for q in range(KC):
                        gate = table("gate2f")[:, q, bass.ds(t * 8, 8)].unsqueeze(2).broadcast_to([P, 8, N])
                        yT = Q.yT[:, q, :]
                        ch.link(nc.vector.tensor_scalar(yT, psS[:, q * 512:(q + 1) * 512], c("l2_b2", q), None, ALU.add))
                        y3 = yT.rearrange("p (b n) -> p b n", n=N)
                        ins = nc.vector.tensor_tensor(y3, y3, gate, ALU.mult)
                        if q == 0:
                            ch.link(ins)
                    ins.then_inc(Q.s["f_yt"].sem, 1)
                elif Q.kind == "l3":
                    xs = x[:, bass.ds(t * 4, 4), :]
                    nc.vector.tensor_tensor(xs, xs, psS[:, :].rearrange("p (r d) -> p r d", d=D), ALU.add
                                            ).then_inc(Q.s["f_done"].sem, 1)
                else:
                    after(v, Q.s["f_sc"], t * 64)
                    ch.link(nc.vector.tensor_tensor(Q.y, psS[:, :].rearrange("p (r d) -> p r d", d=D),
                                                    Q.b2[u].unsqueeze(1).broadcast_to([P, 4, D]), ALU.add))
                    nc.vector.tensor_tensor(Q.y, Q.y, Q.wcol[u].unsqueeze(2).broadcast_to([P, 4, D]), ALU.mult
                                            ).then_inc(Q.s["f_done"].sem, 1)

            def first():
                ch.reset()
                if Q.kind != "moe":
                    dve_rstd(ch, rms=Q.kind == "l3")
                norm(0, 0, 0)
                modulate(0)

            def step(t, u, half, more):
                ch.reset()
                if more:
                    norm(t + 1, 1 - u, half + u)
                if Q.kind == "l2" and not (isinstance(t, int) and t == 0):
                    add(t - 1)
                if Q.kind == "l3":
                    products(t)
                if more:
                    modulate(t + 1)
                result(t, u)

            pairs(v, NG, first, step)
            if Q.kind == "l2":
                add(NG - 1)

        def act_ff(a, Q):
            def step(t, u, half, more):
                if Q.kind == "moe":
                    after(a, Q.s[f"f_in{u}"], (half + 1) * 64)
                for j in range(FJ):
                    after(a, Q.s["f_hd"], t * FJ + (j + 1))
                    if Q.kind == "l3":
                        after(a, Q.s["f_he"], t * FJ + (j - 1))
                        nc.scalar.activation(Q.act[j % 2], HB[j % 2], ACT.Gelu).then_inc(Q.s["f_act"].sem, 1)
                        continue
                    if j == 0:
                        after(a, Q.s["f_y"], t)
                    bias = Q.b1[u][:, j:j + 1] if Q.kind == "moe" else c("l2_b1", j)
                    nc.scalar.activation(Q.hid[:, j, :], HB[j % 4], ACT.Gelu_apprx_tanh if Q.kind == "moe" else ACT.Gelu,
                                         bias=bias).then_inc(Q.s["f_he"].sem, 1)

            pairs(a, NG, lambda: None, step)
        def pool_moe(g, Q):
            def gather(n, u, half):
                after_all(g, su["table"], [(Q.s[f"f_gi{u}"], (half + 1) * 16), (Q.s["f_xn"], n - 1)])
                for r in range(4):
                    nc.gpsimd.indirect_dma_start(
                        out=Q.xg[u][:, r, :], out_offset=None, in_=gather_table,
                        in_offset=bass.IndirectOffsetOnAxis(ap=Q.gidx[u][:, r:r + 1], axis=0)
                    ).then_inc(Q.s[f"f_ga{u}"].sem, 16)

            def first():
                gather(0, 0, 0)
                gather(1, 1, 0)

            def step(t, u, half, ahead):
                if ahead == 2:
                    gather(t + 2, u, half + 1)
                after_all(g, su["table"], [(Q.s[f"f_si{u}"], (half + 1) * 16), (Q.s["f_done"], t + 1),
                                           (Q.s["f_sc"], t * 64)])
                for r in range(4):
                    nc.gpsimd.indirect_dma_start(
                        out=moe_sum, out_offset=bass.IndirectOffsetOnAxis(ap=Q.sidx[u][:, r:r + 1], axis=0),
                        in_=Q.y[:, r, :], in_offset=None, compute_op=ALU.add
                    ).then_inc(Q.s["f_sc"].sem, 16)

            g.wait_ge(st["gates"], 16)
            pairs(g, NG, first, step)

        def sp_moe(sp, Q):
            def weights(e, u):
                after(sp, Q.s["f_done"], e - 1)
                sp.dma_start(Q.w1[u], A["l1_fc1"][e].rearrange("(k p) n -> p k n", p=P)).then_inc(Q.s[f"f_in{u}"].sem, 16)
                sp.dma_start(Q.w2[u], A["l1_fc2"][e].rearrange("(k p) n -> p k n", p=P)).then_inc(Q.s[f"f_in{u}"].sem, 16)
                sp.dma_start(Q.b1[u], A["l1_b1"][e]).then_inc(Q.s[f"f_in{u}"].sem, 16)
                sp.dma_start(Q.b2[u], A["l1_b2"][e].broadcast_to([P, D])).then_inc(Q.s[f"f_in{u}"].sem, 16)

            def tokens(e, idx, signal):
                sp.dma_start(idx, slot_token.rearrange("(e p r) -> e p r", p=P, r=4)[e]).then_inc(signal.sem, 16)

            def step(t, u, half, ahead):
                if ahead == 2:
                    after(sp, Q.s[f"f_ga{u}"], (half + 1) * 64)
                    tokens(t + 2, Q.gidx[u], Q.s[f"f_gi{u}"])
                if ahead:
                    weights(t + 1, 1 - u)
                    after(sp, Q.s["f_sc"], t * 64)
                    tokens(t + 1, Q.sidx[1 - u], Q.s[f"f_si{1 - u}"])

            def first():
                weights(0, 0)
                sp.wait_ge(st["idx"], 16 * E8)
                tokens(0, Q.gidx[0], Q.s["f_gi0"])
                tokens(1, Q.gidx[1], Q.s["f_gi1"])
                tokens(0, Q.sidx[0], Q.s["f_si0"])

            pairs(sp, NG, first, step)

        consts = sb("consts", [P, NCONST])
        cc = {n: consts[:, a:a + w] for n, (a, w) in CONSTS.items()}
        ident, trig, lower, iota16, iota32 = cc["ident"], cc["trig"], cc["lower"], cc["iota16"], cc["iota32"]
        ones, par, pidx, tidx = cc["ones"], cc["par"], cc["pidx"], cc["tidx"]
        condT = work[:, 0:KC * B].rearrange("p (k b) -> p k b", b=B)
        silT = work[:, 128:256].rearrange("p (k b) -> p k b", b=B)
        hidT = work[:, 256:512].rearrange("p (k b) -> p k b", b=B)
        mod = work[:, 512:512 + 12 * B].rearrange("p (k b) -> p k b", b=B)

        rows0 = work[0:B, 10752:10752 + 2 * D]

        def pe_setup(pe):
            pe.wait_ge(ld["small"], 48)
            pe.wait_ge(ld["modw"], 80)

            def mm(ps, w, w0, src, n):
                for q in range(n):
                    for k in range(KC):
                        ins = nc.tensor.matmul(ps[:, q * B:(q + 1) * B], w[:, w0 + k, q * P:(q + 1) * P], src[:, k, :],
                                               start=(k == 0), stop=(k == KC - 1))
                return ins

            mm(psS[:, 0:256], m0, 0, condT, 4)
            mm(psW0[:, 0:128], m3a, 0, condT, 2)
            mm(psW0[:, 128:256], m3a, 2, condT, 2).then_inc(su["mm"], 1)
            pe.wait_ge(su["silu"], 1)
            mm(psS[:, 256:384], m1, 0, silT, 2)
            mm(psP[:, 0:512], m2[:, :, 0:1024], 0, silT, 8)
            mm(psP[:, 512:768], m2[:, :, 1024:1536], 0, silT, 4)
            pe.wait_ge(su["hidden"], 1)
            mm(psW1[:, 0:256], m3b, 0, hidT[:, 0:2, :], 4)
            mm(psW1[:, 256:512], m3b, 2, hidT[:, 2:4, :], 4).then_inc(su["mm2"], 1)
            pe.wait_ge(su["table"], 1)
            for i, name in enumerate(("g0", "b0")):
                for k in range(KC):
                    at = (i * KC + k) * P
                    ins = nc.tensor.transpose(psS[0:B, at:at + P], table(name)[:, k, :], ident)
            ins.then_inc(su["turned_rows"], 1)
            pe.wait_ge(su["rows"], 1)

        def act_setup(a):
            a.wait_ge(ld["small"], 48)
            nc.scalar.activation(silT, condT, ACT.Silu).then_inc(su["silu"], 1)
            a.wait_ge(su["mm"], 1)
            for i in range(4):
                ins = nc.scalar.activation(hidT[:, i, :], psW0[:, i * B:(i + 1) * B], ACT.Silu, bias=c("l3_tb1", i))
            ins.then_inc(su["hidden"], 1)
            a.wait_ge(su["turned_rows"], 1)
            nc.scalar.activation(rows0, psS[0:B, 0:2 * D], ACT.Copy).then_inc(su["rows"], 1)

        def dve_setup(v, ch):
            v.wait_ge(ld["small"], 48)
            ch.reset()

            def wide(ap):
                return ap.unsqueeze(2).broadcast_to([P, ap.shape[1], B])

            def tt(out, a, b, op=ALU.add):
                ch.link(nc.vector.tensor_tensor(out, a, b, op))

            def psv(ps, lo, n):
                return ps[:, lo * B:(lo + n) * B].rearrange("p (k b) -> p k b", b=B)

            ch.link(nc.vector.tensor_scalar(c("l0_bv", 0, 2), c("l0_bv", 0, 2), 1.0 / 16, None, ALU.mult))
            v.wait_ge(su["mm2"], 1)
            tt(mod[:, 0:4, :], psv(psS, 0, 4), wide(c("l0_bgb", 0, 4)))
            tt(table("g0"), mod[:, 0:2, :], wide(c("l0_g", 0, 2)), ALU.mult)
            tt(mod[:, 4:6, :], mod[:, 0:2, :], wide(c("l0_b", 0, 2)), ALU.mult)
            tt(table("b0"), mod[:, 4:6, :], mod[:, 2:4, :])
            ch.link(nc.vector.tensor_copy(table("g1"), wide(c("l1_g", 0, 2))))
            tt(mod[:, 0:2, :], psv(psS, 4, 2), wide(c("l1_bada", 0, 2)))
            tt(table("b1"), mod[:, 0:2, :], wide(c("l1_b", 0, 2)))
            tt(mod[:, 0:12, :], psv(psP, 0, 12), wide(c("l2_bmod", 0, 12)))
            for i, (b, g, gate) in enumerate((("b2", "g2", "gate2"), ("b2f", "g2f", "gate2f"))):
                ch.link(nc.vector.tensor_copy(table(b), mod[:, 6 * i:6 * i + 2, :]))
                ch.link(nc.vector.tensor_scalar(table(g), mod[:, 6 * i + 2:6 * i + 4, :], 1.0, None, ALU.add))
                ch.link(nc.vector.tensor_copy(table(gate), mod[:, 6 * i + 4:6 * i + 6, :]))
            tt(mod[:, 0:8, :], psv(psW1, 0, 8), wide(c("l3_tb2", 0, 8)))
            for i, (g, b, w) in enumerate((("g3", "b3", "l3_w1"), ("g3f", "b3f", "l3_w2"))):
                ch.link(nc.vector.tensor_scalar(mod[:, 4 * i:4 * i + 2, :], mod[:, 4 * i:4 * i + 2, :], 1.0, None, ALU.add))
                tt(table(g), mod[:, 4 * i:4 * i + 2, :], wide(c(w, 0, 2)), ALU.mult)
                ins = nc.vector.tensor_copy(table(b), mod[:, 4 * i + 2:4 * i + 4, :])
                if i == 0:
                    ch.link(ins)
            ins.then_inc(su["table"], 1)

        def dve_center(v, ch, k):
            v.wait_ge(ld["l1"], 48)
            W = Region(work)
            W.take(9000)
            mean = W.take(32)
            w = l1_w[:, k, 0:2 * F].rearrange("p (h d) -> p h d", d=64)
            ch.link(nc.vector.tensor_reduce(mean, w, AX.X, ALU.add))
            ch.link(nc.vector.tensor_scalar(mean, mean, 1.0 / 64, None, ALU.mult))
            nc.vector.tensor_tensor(w, w, mean.unsqueeze(2).broadcast_to([P, 32, 64]), ALU.subtract
                                    ).then_inc(su["center"], 1)

        W = Region(work)
        GE = NT * E8
        cmpT, rank, pre, pre2, sel = (W.take(NT, E8) for _ in range(5))
        cmp3 = W.take(3, GE).rearrange("p i (t e) -> p i t e", e=E8)
        cnt, need = W.take(3, E8), W.take(E8)
        gmx = W.take(NT)
        cur, keep = (W.take(E8).bitcast(I32) for _ in range(2))
        cand, steps = (W.take(3, E8).bitcast(I32) for _ in range(2))
        kept, level, unit = W.take(3, E8), W.take(E8), W.take(1)
        ri, ra, rb = (W.take(NT, E8).bitcast(I32) for _ in range(3))
        hotA = W.take(GE * 8).bitcast(BF16).rearrange("p (t e s) -> p t e s", e=E8, s=16)
        hotAp = W.take(GE * 8).bitcast(BF16).rearrange("p (t n) -> p t n", n=P)
        hotAt = W.take(GE * 8).bitcast(BF16).rearrange("p (t n) -> p t n", n=P)
        rt = sems("rt", "shift exp prob cnt tot keep cnt2 tot2 m w hot ix idx")

        def dve_route(v, ch, hotB):
            ch.reset()
            tt = lambda *a: ch.link(nc.vector.tensor_tensor(*a))
            ts = lambda *a: ch.link(nc.vector.tensor_scalar(*a))

            def over_tiles(ap):
                return ap.rearrange("p t e -> p e t")

            def every(ap):
                return ap.unsqueeze(1).broadcast_to([P, NT, E8])

            ch.link(nc.vector.tensor_reduce(gmx, gates[:, :, :], AX.X, ALU.max))
            nc.vector.tensor_tensor(gates[:, :, :], gates[:, :, :], gmx.unsqueeze(2).broadcast_to([P, NT, E8]),
                                    ALU.subtract).then_inc(rt["shift"], 1)
            v.wait_ge(rt["exp"], 1)
            ch.link(nc.vector.tensor_reduce(gmx, gates[:, :, :], AX.X, ALU.add))
            ch.link(nc.vector.reciprocal(gmx, gmx))
            nc.vector.tensor_tensor(gates[:, :, :], gates[:, :, :], gmx.unsqueeze(2).broadcast_to([P, NT, E8]),
                                    ALU.mult).then_inc(rt["prob"], 1)
            v.wait_ge(rt["prob"], 1)
            ch.link(nc.vector.memset(cur, 0))
            for i in range(3):
                ch.link(nc.vector.memset(steps[:, i, :], (i + 1) << 28))
            ch.link(nc.vector.memset(unit, float(1 << 28)))

            def two_bits(i):
                ch.reset()
                tt(cand, steps, cur.unsqueeze(1).broadcast_to([P, 3, E8]), ALU.bitwise_or)
                tt(cmp3, gates[:, :, :].unsqueeze(1).broadcast_to([P, 3, NT, E8]),
                   cand.bitcast(FP32).unsqueeze(2).broadcast_to([P, 3, NT, E8]), ALU.is_ge)
                nc.vector.tensor_reduce(cnt, cmp3.rearrange("p i t e -> p i e t"), AX.X, ALU.add).then_inc(rt["cnt"], 1)
                ch.link(nc.vector.tensor_scalar(steps, steps, 2, None, ALU.logical_shift_right))
                v.wait_ge(rt["tot"], i + 1)
                ts(kept, psW0[:, 0:3 * E8].rearrange("p (i e) -> p i e", e=E8), CAP - 0.5, None, ALU.is_ge)
                ch.link(nc.vector.tensor_reduce(level, kept.rearrange("p i e -> p e i"), AX.X, ALU.add))
                ts(keep, level, unit[:, 0:1], None, ALU.mult)
                tt(cur, cur, keep, ALU.bitwise_or)
                nc.vector.tensor_scalar(unit, unit, 0.25, None, ALU.mult).then_inc(rt["keep"], 1)
                v.wait_ge(rt["keep"], i + 1)

            with v.Fori(0, 15) as i:
                two_bits(i)
            ch.reset()
            thr = every(cur.bitcast(FP32))
            tt(sel, gates[:, :, :], thr, ALU.is_gt)
            tt(cmpT, gates[:, :, :], thr, ALU.is_equal)
            nc.vector.tensor_reduce(cnt[:, 0, :], over_tiles(sel), AX.X, ALU.add).then_inc(rt["cnt2"], 1)

            def ranks(mask, i):
                v.wait_ge(rt["w"], i + 1)
                within = psS[:, 0:GE].rearrange("p (t e) -> p t e", e=E8)
                total = psS[:, 512:512 + GE].rearrange("p (t e) -> p t e", e=E8)
                ch.link(nc.vector.memset(pre[:, 0:1, :], 0.0))
                ch.link(nc.vector.tensor_copy(pre[:, 1:NT, :], total[:, 0:NT - 1, :]))
                src, dst = pre, pre2
                k = 1
                while k < NT:
                    ch.link(nc.vector.tensor_copy(dst[:, 0:k, :], src[:, 0:k, :]))
                    tt(dst[:, k:NT, :], src[:, k:NT, :], src[:, 0:NT - k, :], ALU.add)
                    src, dst, k = dst, src, 2 * k
                tt(rank, within, src, ALU.add)

            v.wait_ge(rt["tot2"], 1)
            nc.vector.tensor_scalar(need, psW0[:, 0:E8], -1.0, float(CAP), ALU.mult, ALU.add).then_inc(rt["m"], 1)
            v.wait_ge(rt["m"], 1)
            ranks(cmpT, 0)
            tt(rank, rank, every(need), ALU.is_lt)
            tt(cmpT, cmpT, rank, ALU.mult)
            nc.vector.tensor_tensor(sel, sel, cmpT, ALU.add).then_inc(rt["m"], 1)
            v.wait_ge(rt["m"], 2)
            ranks(sel, 1)
            ts(rank, rank, 1.0, None, ALU.add)
            tt(rank, rank, sel, ALU.mult)
            ts(ri, rank, -1.0, None, ALU.add)
            ts(ra, ri, 5, None, ALU.arith_shift_right)
            ts(rb, ri, 31, None, ALU.bitwise_and)
            ch.link(nc.vector.tensor_copy(pre, ra))
            ch.link(nc.vector.tensor_copy(pre2, rb))
            flat = lambda ap: ap.rearrange("p t e -> p (t e)")
            for i in range(NT // 8):
                ti, ei = slice(8 * i, 8 * i + 8), slice(8 * i * E8, (8 * i + 8) * E8)
                tt(hotA[:, ti].rearrange("p t e s -> p (t e) s"), flat(pre)[:, ei].unsqueeze(2).broadcast_to([P, 64, 16]),
                   iota16.unsqueeze(1).broadcast_to([P, 64, 16]), ALU.is_equal)
                tt(hotB[:, ti].rearrange("p t (e s) -> p (t e) s", s=32),
                   flat(pre2)[:, ei].unsqueeze(2).broadcast_to([P, 64, 32]),
                   iota32.unsqueeze(1).broadcast_to([P, 64, 32]), ALU.is_equal)
                hotA3 = hotA[:, ti].rearrange("p t e s -> p t (e s)")
                ts(hotAp[:, ti], hotA3, pidx[:, 0:1], None, ALU.mult)
                nc.vector.tensor_tensor(hotAt[:, ti], hotA3, tidx[:, ti].unsqueeze(2).broadcast_to([P, 8, P]), ALU.mult
                                        ).then_inc(rt["hot"], 1)
            v.wait_ge(rt["ix"], 1)
            ts(flat(sel), psP[:, 512:512 + GE], 128.0, None, ALU.mult)
            nc.vector.tensor_tensor(flat(ri), flat(sel), psP[:, 0:GE], ALU.add).then_inc(rt["idx"], 1)

        def pe_route(pe, hotB):
            with pe.Fori(0, 15) as i:
                pe.wait_ge(rt["cnt"], i + 1)
                nc.tensor.matmul(psW0[:, 0:3 * E8], ones, cnt.rearrange("p i e -> p (i e)"), start=True, stop=True
                                 ).then_inc(rt["tot"], 1)
            pe.wait_ge(rt["cnt2"], 1)
            nc.tensor.matmul(psW0[:, 0:E8], ones, cnt[:, 0, :], start=True, stop=True).then_inc(rt["tot2"], 1)
            for i, mask in enumerate((cmpT, sel)):
                pe.wait_ge(rt["m"], i + 1)
                nc.tensor.matmul(psS[:, 0:GE], lower, mask.rearrange("p t e -> p (t e)"), start=True, stop=True)
                nc.tensor.matmul(psS[:, 512:512 + GE], ones, mask.rearrange("p t e -> p (t e)"),
                                 start=True, stop=True).then_inc(rt["w"], 1)
            for i in range(NT // 8):
                pe.wait_ge(rt["hot"], i + 1)
                for lo, hot in ((0, hotAp), (512, hotAt)):
                    for t in range(8 * i, 8 * i + 8):
                        ins = nc.tensor.matmul(psP[:, lo:lo + GE], hot[:, t, :], hotB[:, t, :],
                                               start=(t == 0), stop=(t == NT - 1))
            ins.then_inc(rt["ix"], 1)

        L = [Attention(i) for i in range(4)]
        Q = {k: FeedForward(k) for k in ("moe", "l2", "l3")}
        hotB = r2[:, 4096:4096 + GE * 16].bitcast(BF16).rearrange("p (t n) -> p t n", n=GE)
        assert 4096 + GE * 16 <= 8192

        ENDS = {"setup": (Signal(su["table"], 0), 1), "l0": (L[0].s["xupd"], NT), "l1": (L[1].s["gate"], NT),
                "route": (Signal(rt["idx"], 0), 1), "moe": (Q["moe"].s["f_done"], NG), "l2": (L[2].s["xupd"], NT),
                "l2ff": (Q["l2"].s["f_done"], NG), "l3": (L[3].s["xupd"], NT), "l3ff": (Q["l3"].s["f_done"], NG)}

        block = ctx.enter_context(nc.Block())

        def chunked(name):
            return A[name].rearrange("(k p) n -> p k n", p=P)

        def by_tile(ap):
            return ap.rearrange("(t p) d -> p t d", p=P)

        @block.sync
        def _(sp):
            sp.dma_start(consts[:, :], A["consts"]).then_inc(ld["small"], 16)
            sp.dma_start(col[:, :], A["cols"]).then_inc(ld["small"], 16)
            sp.dma_start(condT, chunked("condT")).then_inc(ld["small"], 16)
            sp.dma_start(m0, chunked("l0_mod")).then_inc(ld["modw"], 16)
            for i in range(4):
                sp.dma_start(x[:, 8 * i:8 * i + 8, :], by_tile(A["x"])[:, 8 * i:8 * i + 8, :]).then_inc(ld[f"x{i}"], 16)
            for dst, name in ((m1, "l1_mod"), (m2, "l2_mod"), (m3a, "l3_mod1"), (m3b, "l3_mod2")):
                sp.dma_start(dst, chunked(name)).then_inc(ld["modw"], 16)
            sp.dma_start(l0_w, chunked("l0_w")).then_inc(ld["l0"], 16)
            sp.dma_start(l0_wp, chunked("l0_wp")).then_inc(ld["l0"], 16)
            for i, name in enumerate(("l0_bp", "l3_bo")):
                sp.dma_start(bias_row[:, i, :], A[name].broadcast_to([P, D])).then_inc(ld["rows"], 16)
            sp.dma_start(l1_w, chunked("l1_w")).then_inc(ld["l1"], 16)
            sp.dma_start(l1_wout, chunked("l1_wout")).then_inc(ld["l1"], 16)
            sp.dma_start(l1_wgate, chunked("l1_wgate")).then_inc(ld["l1"], 16)
            if stage >= 2:
                sp.wait_ge(su["rows"], 1)
                sp.dma_start(mod_rows, rows0).then_inc(st["rows"], 16)
                sp.wait_ge(st["rows"], 16)
                by_pair = mod_rows.rearrange("(t b) d -> b t d", b=2)

                def rows(n):
                    for b in range(2):
                        sp.dma_start(L[1].rows[b * N:(b + 1) * N, :], by_pair[b:b + 1, n, :].broadcast_to([N, 2 * D])
                                     ).then_inc(L[1].s["rows_in"].sem, 16)

                def store(t):
                    after(sp, L[1].s["xupd"], t + 1)
                    sp.dma_start(by_tile(gather_table)[:, t, 0:D], L[1].x1).then_inc(st["tab"], 16)
                    sp.dma_start(by_tile(moe_sum)[:, t, :], L[1].x1).then_inc(st["tab"], 16)

                rows(0)
                for n in range(1, 4):
                    after(sp, L[1].s["sn"], n)
                    rows(n)
                with sp.Fori(0, NT - 4) as t:
                    store(t)
                    after(sp, L[1].s["sn"], t + 4)
                    rows(t + 4)
                with sp.Fori(NT - 4, NT) as t:
                    store(t)
                after(sp, L[1].s["gate"], NT)
                for dst, name in ((l2_w, "l2_w"), (l2_wout, "l2_wout"), (l2_w1, "l2_w1"), (l2_w2, "l2_w2")):
                    sp.dma_start(dst, chunked(name)).then_inc(ld["l2"], 16)
            if stage >= 3:
                sp.wait_ge(rt["prob"], 1)
                sp.dma_start(by_tile(gather_table)[:, :, D:ROW], gates[:, :, :]).then_inc(st["gates"], 16)
                sp.wait_ge(rt["idx"], 1)
                slots = slot_token.rearrange("(e a s) -> e a s", a=16, s=32)
                for e in range(E8):
                    sp.dma_start(slots[e], ri.rearrange("p t e -> p (t e)")[16 * e:16 * e + 16, 32 * e:32 * e + 32]
                                 ).then_inc(st["idx"], 16)
                sp.wait_ge(st["tab"], 32 * NT)
                sp_moe(sp, Q["moe"])
                after(sp, Q["moe"].s["f_sc"], 64 * E8)
            if stage >= 2:
                sp.wait_ge(st["tab"], 32 * NT)
                for i in range(4):
                    sp.dma_start(x[:, 8 * i:8 * i + 8, :], by_tile(moe_sum)[:, 8 * i:8 * i + 8, :]
                                 ).then_inc(ld[f"back{i}"], 16)
                for dst, name in ((l3_w, "l3_w"), (l3_wo, "l3_wo"), (l3_gate, "l3_gate"), (l3_up, "l3_up"),
                                  (l3_down, "l3_down")):
                    sp.dma_start(dst, chunked(name)).then_inc(ld["l3"], 16)
                for i in range(4):
                    sp.wait_ge(ld[f"back{i}"], 16)
            s, n = ENDS[{1: "l0", 2: "l1", 3: "moe", 5: "l2", 6: "l2ff", 7: "l3", 8: "l3ff"}[stage]]
            if stage >= 8:
                for i in range(NG):
                    after(sp, s, i + 1)
                    sp.dma_start(by_tile(out)[:, 4 * i:4 * i + 4, :], x[:, 4 * i:4 * i + 4, :]).then_inc(st["out"], 16)
                sp.wait_ge(st["out"], 16 * NG)
            else:
                after(sp, s, n)
                sp.dma_start(by_tile(out), x[:, :, :]).then_inc(st["out"], 16)
                sp.wait_ge(st["out"], 16)

        def following(eng, ended):
            after(eng, *ENDS[ended])

        @block.tensor
        def _(pe):
            pe_setup(pe)
            following(pe, "setup")
            pe_attention(pe, L[0])
            if stage >= 2:
                following(pe, "l0")
                pe_attention(pe, L[1])
            if stage >= 3:
                following(pe, "l1")
                pe_route(pe, hotB)
                following(pe, "route")
                pe_ff(pe, Q["moe"])
            if stage >= 5:
                following(pe, "moe")
                pe_attention(pe, L[2])
            if stage >= 6:
                following(pe, "l2")
                pe_ff(pe, Q["l2"])
            if stage >= 7:
                following(pe, "l2ff")
                pe_attention(pe, L[3])
            if stage >= 8:
                following(pe, "l3")
                pe_ff(pe, Q["l3"])

        @block.vector
        def _(v):
            ch = Chain(v, chain_dve)
            dve_all_moments(v, ch, [ld[f"x{i}"] for i in range(4)])
            dve_setup(v, ch)
            v.wait_ge(su["table"], 1)
            dve_attention(v, ch, L[0])
            if stage >= 2:
                following(v, "l0")
                v.wait_ge(st["rows"], 16)
                dve_attention(v, ch, L[1])
            if stage >= 3:
                following(v, "l1")
                v.wait_ge(st["tab"], 32 * NT)
                dve_route(v, ch, hotB)
                following(v, "route")
                v.wait_ge(st["idx"], 16 * E8)
                dve_ff(v, ch, Q["moe"])
            if stage >= 5:
                following(v, "moe")
                dve_all_moments(v, ch, [ld[f"back{i}"] for i in range(4)])
                dve_attention(v, ch, L[2])
            if stage >= 6:
                following(v, "l2")
                dve_ff(v, ch, Q["l2"])
            if stage >= 7:
                following(v, "l2ff")
                dve_attention(v, ch, L[3])
            if stage >= 8:
                following(v, "l3")
                dve_ff(v, ch, Q["l3"])

        @block.scalar
        def _(a):
            act_setup(a)
            following(a, "setup")
            act_attention(a, L[0])
            if stage >= 2:
                following(a, "l0")
                act_attention(a, L[1])
            if stage >= 3:
                a.wait_ge(rt["shift"], 1)
                nc.scalar.activation(gates[:, :, :], gates[:, :, :], ACT.Exp).then_inc(rt["exp"], 1)
                following(a, "route")
                act_ff(a, Q["moe"])
            if stage >= 5:
                following(a, "moe")
                act_attention(a, L[2])
            if stage >= 6:
                following(a, "l2")
                act_ff(a, Q["l2"])
            if stage >= 7:
                following(a, "l2ff")
                act_attention(a, L[3])
            if stage >= 8:
                following(a, "l3")
                act_ff(a, Q["l3"])

        @block.gpsimd
        def _(g):
            g.wait_ge(ld["small"], 48)
            g.wait_ge(ld["rows"], 32)
            following(g, "setup")
            pool_attention(g, L[0])
            if stage >= 2:
                following(g, "l0")
                pool_attention(g, L[1])
            if stage >= 3:
                following(g, "route")
                pool_moe(g, Q["moe"])
            if stage >= 5:
                following(g, "moe")
                pool_attention(g, L[2])
            if stage >= 7:
                following(g, "l2ff")
                pool_attention(g, L[3])


def host_arrays(I):
    a = {k: np.asarray(v) for k, v in I.items()}
    l0 = lambda n: a["L0_cond_" + n]
    l1 = lambda n: a["L1_cond_" + n]
    l2 = lambda n: a["L2_cond_" + n]
    l3 = lambda n: a["L3_cond_" + n]
    cat = np.concatenate
    wqkv = l0("Wqkv").reshape(H, 16, 3, D).transpose(2, 0, 1, 3).reshape(3 * D, D)
    bqkv = l0("bqkv").reshape(H, 16, 3).transpose(2, 0, 1).reshape(3, D)

    twice = lambda w: cat([w, w])
    vectors = {
        "l0_g": l0("ln_g"), "l0_b": l0("ln_b"), "l0_bgb": cat([l0("bg"), l0("bb")]),
        "l0_bqk": cat([bqkv[0], bqkv[1]]), "l0_bv": bqkv[2],
        "l1_bada": l1("b_ada"), "l1_g": l1("ln1_g"), "l1_b": l1("ln1_b"),
        "l1_qn": cat([twice(l1(n)) for n in ("qn_g", "qn_b", "kn_g", "kn_b")]),
        "l1_mlp": cat([l1("mlp_g"), l1("mlp_b")]),
        "l2_bmod": l2("b_mod"), "l2_bout": l2("b_out"), "l2_b1": l2("b1"), "l2_b2": l2("b2"),
        "l3_w1": l3("w_norm1"), "l3_w2": l3("w_norm2"), "l3_tb1": cat([l3("t1_b1"), l3("t2_b1")]),
        "l3_tb2": cat([l3("t1_b2"), l3("t2_b2")]), "l3_bqk": cat([l3("bq"), l3("bk")]), "l3_bv": l3("bv")}
    cols = cat([vectors[n].reshape(k, P).T for n, (_, k) in COLS.items()], axis=1)
    assert cols.shape == (P, NCOL)
    f32 = np.float32
    inv = (f32(1.0) / f32(10000.0) ** (np.arange(0, 16, 2, dtype=f32) / f32(16))).astype(f32)
    angle = (inv[:, None] * np.arange(N, dtype=f32)[None, :]).astype(f32)
    cos = np.tile(cat([np.cos(angle), np.cos(angle)]), (8, 1))
    sin = np.tile(cat([-np.sin(angle), np.sin(angle)]), (8, 1))
    parity = (np.arange(P) // 16) % 2
    blocks = {"ident": np.eye(P), "ones": np.ones((P, P)), "lower": np.triu(np.ones((P, P)), 1),
              "trig": cat([cos, sin], axis=1), "par": np.stack([1 - parity, parity], axis=1),
              "iota16": np.tile(np.arange(16), (P, 1)), "iota32": np.tile(np.arange(32), (P, 1)),
              "pidx": np.arange(P)[:, None], "tidx": np.tile(np.arange(NT), (P, 1))}
    consts = cat([blocks[n].astype(f32) for n in CONSTS], axis=1)
    arrays = {
        "x": a["x"].reshape(T, D), "condT": a["cond_1024"].T, "cols": cols, "consts": consts,
        "l0_mod": cat([l0("Wg").T, l0("Wb").T], axis=1), "l0_w": wqkv.T, "l0_wp": l0("Wp").T,
        "l0_bp": l0("bp")[None, :],
        "l1_mod": l1("W_ada").T, "l1_w": l1("Wqkv").T, "l1_wout": l1("Wout").T, "l1_wgate": l1("Wgate").T,
        "l1_fc1": l1("fc1s").transpose(0, 2, 1), "l1_fc2": l1("fc2s").transpose(0, 2, 1),
        "l1_b1": l1("b1s").reshape(E8, FJ, P).transpose(0, 2, 1), "l1_b2": l1("b2s")[:, None, :],
        "l2_mod": l2("W_mod"), "l2_w": l2("W_qkv"), "l2_wout": l2("W_out"), "l2_w1": l2("W1"), "l2_w2": l2("W2"),
        "l3_mod1": cat([l3("t1_w1"), l3("t2_w1")]), "l3_mod2": cat([l3("t1_w2"), l3("t2_w2")]),
        "l3_w": cat([l3("wq"), l3("wk"), l3("wv")], axis=1),
        "l3_wo": l3("wo"), "l3_bo": l3("bo")[None, :],
        "l3_gate": l3("w_gate"), "l3_up": l3("w_up"), "l3_down": l3("w_down")}
    return {k: np.ascontiguousarray(v) for k, v in arrays.items()}


def kernel(**inputs):
    import concourse.bacc as bacc
    from concourse.bass_utils import run_bass_kernel_spmd

    nc = bacc.Bacc("TRN2", target_bir_lowering=False, num_devices=1)
    arrays = host_arrays(inputs)
    A = {k: nc.dram_tensor("in_" + k, v.shape, FP32, kind="ExternalInput").ap() for k, v in arrays.items()}
    out = nc.dram_tensor("out", (T, D), FP32, kind="ExternalOutput").ap()
    build_program(nc, A, out)
    r = run_bass_kernel_spmd(nc, [{"in_" + k: v for k, v in arrays.items()}], core_ids=[0])
    return r.results[0]["out"].reshape(B, N, D)
```
